# Optimizing a Trainium2 kernel written in Bass

```python
import numpy as np
import jax
import jax.numpy as jnp

def _softmax(x, axis=-1):
    return jax.nn.softmax(x, axis=axis)

def _gelu(x):
    return jax.nn.gelu(x, approximate=True)

def _silu(x):
    return jax.nn.silu(x)

def _sigmoid(x):
    return jax.nn.sigmoid(x)

def _layernorm(x, axis=-1, eps=1e-05):
    m = jnp.mean(x, axis=axis, keepdims=True)
    v = jnp.var(x, axis=axis, keepdims=True)
    return (x - m) / jnp.sqrt(v + eps)

def _scatter_add(tgt, idx, src, axis=0):
    return tgt.at[idx].add(src)

def _segment_sum(src, seg, n):
    return jax.ops.segment_sum(src, seg, n)
kernel_name = 'mk_flamingo_gated_d4_seqx_r8_6b99dd'

def setup_inputs(seed: int=0):
    np.random.seed(seed)
    _w = jnp.asarray

    def _rec_inputs():
        import jax
        import jax.numpy as jnp
        _rk = jax.random.key(seed)
        x = -0.0002928 + 1 * jax.random.normal(jax.random.fold_in(_rk, 1), (8, 256, 128), jnp.float32)
        _lenS = 256 - jax.random.randint(jax.random.fold_in(_rk, 7), (8,), 0, max(1, 256 // 4) + 1, jnp.int32)
        _lenS2 = 512 - jax.random.randint(jax.random.fold_in(_rk, 8), (8,), 0, max(1, 512 // 4) + 1, jnp.int32)
        _ctx_1024P = jax.random.normal(jax.random.fold_in(_rk, 11), (8, 16, 128), jnp.float32)
        _ctx_1024c = jax.random.dirichlet(jax.random.fold_in(_rk, 511), 0.3 * jnp.ones((16,), jnp.float32), (8, 512))
        _ctx_1024t = jnp.einsum('bsk,bkd->bsd', _ctx_1024c, _ctx_1024P)
        _ctx_1024t = _ctx_1024t * jax.lax.rsqrt(jnp.mean(jnp.square(_ctx_1024t)) + 1e-12) * 0.953939
        ctx_1024 = -1.39393e-06 + 0.999914 * (_ctx_1024t + 0.3 * jax.random.normal(jax.random.fold_in(_rk, 611), (8, 512, 128), jnp.float32))
        itok_BxS_8_8191 = jax.random.randint(jax.random.fold_in(_rk, 12), (8, 256), 8, 1024, jnp.int32)
        itok_BxS2_1_8191 = jax.random.randint(jax.random.fold_in(_rk, 13), (8, 512), 1, 1024, jnp.int32)
        _validS = jnp.arange(256)[None, :] < _lenS[:, None]
        _validS2 = jnp.arange(512)[None, :] < _lenS2[:, None]
        _causal = jnp.tril(jnp.ones((256, 256), dtype=bool))
        mask_BxSxS2_if1 = jnp.where(jnp.ones((8, 256, 512), dtype=bool), 1, 0).astype(jnp.int32)
        mask_SxS2_bk0 = jnp.logical_not(jnp.broadcast_to(_validS2[0:1, :], (256, 512)))
        mask_BxS2_bk1 = jnp.broadcast_to(_validS2[:, :], (8, 512))
        _g = jax.random.normal(jax.random.fold_in(_rk, 9001), (2, 4), jnp.float32)
        _g = jnp.sign(_g) * jnp.maximum(jnp.abs(_g), 1.0) + (_g == 0) * 1.0
        g_xattn = _g[0]
        g_ffn = _g[1]
        return (x, ctx_1024, itok_BxS_8_8191, itok_BxS2_1_8191, mask_BxSxS2_if1, mask_SxS2_bk0, mask_BxS2_bk1, g_xattn, g_ffn)
    x, ctx_1024, itok_BxS_8_8191, itok_BxS2_1_8191, mask_BxSxS2_if1, mask_SxS2_bk0, mask_BxS2_bk1, g_xattn, g_ffn = _rec_inputs()

    def _L0_xattn_setup():
        import jax, jax.numpy as jnp
        import numpy as np
        D_MODEL = 64
        N_HEADS = 8
        D_KEYS = D_MODEL // N_HEADS
        DIN = D_MODEL * 2
        DPROJ = D_KEYS * N_HEADS * 2
        B, L = (2, 256)
        key = jax.random.key(seed)
        ks = jax.random.split(key, 11)
        s_in = 1.0 / np.sqrt(DIN)
        s_out = 1.0 / np.sqrt(DPROJ)
        return {'queries': jax.random.normal(ks[0], (B, L, DIN), jnp.float32), 'keys': jax.random.normal(ks[1], (B, L, DIN), jnp.float32), 'values': jax.random.normal(ks[2], (B, L, DIN), jnp.float32), 'Wq': jax.random.normal(ks[3], (DPROJ, DIN), jnp.float32) * s_in, 'bq': jax.random.normal(ks[4], (DPROJ,), jnp.float32) * s_in, 'Wk': jax.random.normal(ks[5], (DPROJ, DIN), jnp.float32) * s_in, 'bk': jax.random.normal(ks[6], (DPROJ,), jnp.float32) * s_in, 'Wv': jax.random.normal(ks[7], (DPROJ, DIN), jnp.float32) * s_in, 'bv': jax.random.normal(ks[8], (DPROJ,), jnp.float32) * s_in, 'Wo': jax.random.normal(ks[9], (DIN, DPROJ), jnp.float32) * s_out, 'bo': jax.random.normal(ks[10], (DIN,), jnp.float32) * s_out}
    _L0_xattn_all = _L0_xattn_setup()
    _L0_xattn_in = {k: v for k, v in _L0_xattn_all.items() if k in ('Wq', 'bq', 'Wk', 'bk', 'Wv', 'bv', 'Wo', 'bo')}
    del _L0_xattn_all

    def _L0_ffn_setup():
        import jax, jax.numpy as jnp
        import numpy as np
        E = 8
        TOP_K = 2
        B, S, D = (2, 512, 128)
        H = 512
        CAPACITY = 256

        def _moe(x, Wg, W1, b1, W2, b2):
            b, s, d = x.shape
            xf = x.reshape(b * s, d)
            logits = xf.astype(jnp.float32) @ Wg.astype(jnp.float32)
            probs = jax.nn.softmax(logits, axis=-1)
            vals, idx = jax.lax.top_k(probs, TOP_K)
            w = vals / (jnp.sum(vals, axis=-1, keepdims=True) + 1e-09)
            counts = jnp.zeros((E,), dtype=jnp.int32)
            combine = jnp.zeros((b * s, E), dtype=jnp.float32)
            for k in range(TOP_K):
                oh = jax.nn.one_hot(idx[:, k], E, dtype=jnp.int32)
                pos = jnp.cumsum(oh, axis=0) - 1 + counts[None, :]
                keep = (oh == 1) & (pos < CAPACITY)
                counts = counts + jnp.sum(keep.astype(jnp.int32), axis=0)
                combine = combine + w[:, k][:, None] * keep.astype(jnp.float32)
            out = jnp.zeros_like(xf)
            for e in range(E):
                h = jax.nn.gelu(xf @ W1[e] + b1[e])
                ye = h @ W2[e] + b2[e]
                out = out + combine[:, e][:, None].astype(xf.dtype) * ye
            return out.reshape(b, s, d)
        key = jax.random.key(seed)
        k0, k1, k2, k3 = jax.random.split(key, 4)
        return {'x': jax.random.normal(k0, (B, S, D), dtype=jnp.float32), 'Wg': jax.random.normal(k1, (D, E), dtype=jnp.float32) * 0.02, 'W1': jax.random.normal(k2, (E, D, H), dtype=jnp.float32) * 0.02, 'b1': jnp.zeros((E, H), dtype=jnp.float32), 'W2': jax.random.normal(k3, (E, H, D), dtype=jnp.float32) * 0.02, 'b2': jnp.zeros((E, D), dtype=jnp.float32)}
    _L0_ffn_all = _L0_ffn_setup()
    _L0_ffn_in = {k: v for k, v in _L0_ffn_all.items() if k in ('Wg', 'W1', 'b1', 'W2', 'b2')}
    del _L0_ffn_all

    def _L1_xattn_setup():
        import jax, jax.numpy as jnp
        import numpy as np
        B, T, D = (2, 256, 128)
        N, H = (16, 64)
        key = jax.random.key(seed)
        ks = jax.random.split(key, 8)
        glorot = lambda k, shape, fan_in, fan_out: jax.random.uniform(k, shape, jnp.float32, -1.0, 1.0) * np.sqrt(6.0 / (fan_in + fan_out))
        return {'q': jax.random.normal(ks[0], (B, T, D), jnp.float32), 'v': jax.random.normal(ks[1], (B, T, D), jnp.float32), 'k': jax.random.normal(ks[2], (B, T, D), jnp.float32), 'w_query': glorot(ks[3], (D, N, H), D, N * H), 'b_query': jnp.zeros((N, 1, H), jnp.float32), 'w_value': glorot(ks[4], (D, N, H), D, N * H), 'b_value': jnp.zeros((N, 1, H), jnp.float32), 'w_key': glorot(ks[5], (D, N, H), D, N * H), 'b_key': jnp.zeros((N, 1, H), jnp.float32), 'w_projection': glorot(ks[6], (N, D, H), N * H, D), 'b_projection': jnp.zeros((1, D), jnp.float32)}
    _L1_xattn_all = _L1_xattn_setup()
    _L1_xattn_in = {k: v for k, v in _L1_xattn_all.items() if k in ('w_query', 'b_query', 'w_value', 'b_value', 'w_key', 'b_key', 'w_projection', 'b_projection')}
    del _L1_xattn_all

    def _L1_ffn_setup():
        import jax, jax.numpy as jnp
        import numpy as np
        INT8_MAX = 127.0

        def _absmax_scale(x, axes):
            amax = jnp.max(jnp.abs(x), axis=axes, keepdims=True)
            return jnp.maximum(amax, 1e-12) / INT8_MAX
        key = jax.random.key(seed)
        k1, k2 = jax.random.split(key)
        lhs = jax.random.normal(k1, (4, 1024, 128), dtype=jnp.float32)
        rhs = jax.random.normal(k2, (128, 128), dtype=jnp.float32)
        return {'lhs': lhs, 'rhs': rhs}
    _L1_ffn_all = _L1_ffn_setup()
    _L1_ffn_in = {k: v for k, v in _L1_ffn_all.items() if k in ('rhs',)}
    del _L1_ffn_all

    def _L2_xattn_setup():
        import jax, jax.numpy as jnp
        import numpy as np
        DIM = 128
        NUM_HEADS = 16
        HEAD_DIM = DIM // NUM_HEADS

        def _slopes(num_heads):
            ratio = 2.0 ** (-8.0 / num_heads)
            return jnp.asarray([ratio ** i for i in range(1, num_heads + 1)], dtype=jnp.float32)
        key = jax.random.key(seed)
        ks = jax.random.split(key, 10)
        b, q_len, k_len = (2, 256, 512)
        query = jax.random.normal(ks[0], (b, q_len, DIM), dtype=jnp.float32)
        keys = jax.random.normal(ks[1], (b, k_len, DIM), dtype=jnp.float32)
        values = jax.random.normal(ks[2], (b, k_len, DIM), dtype=jnp.float32)
        query_pos = jnp.sort(jax.random.randint(ks[3], (b, q_len), 0, 1024), axis=-1)
        key_pos = jnp.sort(jax.random.randint(ks[4], (b, k_len), 0, 1024), axis=-1)
        mask = jnp.ones((b, q_len, k_len), dtype=jnp.int32)
        lim = float(np.sqrt(6.0 / (DIM + DIM)))
        W_q = jax.random.uniform(ks[5], (DIM, DIM), minval=-lim, maxval=lim, dtype=jnp.float32)
        W_k = jax.random.uniform(ks[6], (DIM, DIM), minval=-lim, maxval=lim, dtype=jnp.float32)
        W_v = jax.random.uniform(ks[7], (DIM, DIM), minval=-lim, maxval=lim, dtype=jnp.float32)
        W_o = jax.random.uniform(ks[8], (DIM, DIM), minval=-lim, maxval=lim, dtype=jnp.float32)
        return {'query': query, 'keys': keys, 'values': values, 'W_q': W_q, 'W_k': W_k, 'W_v': W_v, 'W_o': W_o, 'query_pos': query_pos, 'key_pos': key_pos, 'mask': mask}
    _L2_xattn_all = _L2_xattn_setup()
    _L2_xattn_in = {k: v for k, v in _L2_xattn_all.items() if k in ('W_q', 'W_k', 'W_v', 'W_o')}
    del _L2_xattn_all

    def _L2_ffn_setup():
        import jax, jax.numpy as jnp
        import numpy as np
        B, L, D = (2, 256, 128)
        E = 15
        H = D * 1
        K = 3
        T = 1.0
        key = jax.random.key(seed)
        ks = jax.random.split(key, 12)
        s = 0.02
        return {'x': jax.random.normal(ks[0], (B, L, D), dtype=jnp.float32), 'router_W': jax.random.normal(ks[1], (D, E), dtype=jnp.float32) * s, 'router_b': jnp.zeros((E,), dtype=jnp.float32), 'sW1': jax.random.normal(ks[2], (D, H), dtype=jnp.float32) * s, 'sb1': jnp.zeros((H,), dtype=jnp.float32), 'sW2': jax.random.normal(ks[3], (H, D), dtype=jnp.float32) * s, 'sb2': jnp.zeros((D,), dtype=jnp.float32), 'eW1': jax.random.normal(ks[4], (E, D, H), dtype=jnp.float32) * s, 'eb1': jnp.zeros((E, H), dtype=jnp.float32), 'eW2': jax.random.normal(ks[5], (E, H, D), dtype=jnp.float32) * s, 'eb2': jnp.zeros((E, D), dtype=jnp.float32)}
    _L2_ffn_all = _L2_ffn_setup()
    _L2_ffn_in = {k: v for k, v in _L2_ffn_all.items() if k in ('router_W', 'router_b', 'sW1', 'sb1', 'sW2', 'sb2', 'eW1', 'eb1', 'eW2', 'eb2')}
    del _L2_ffn_all

    def _L3_xattn_setup():
        import jax, jax.numpy as jnp
        import numpy as np
        B, S, DIM, EMBED, HEAD = (2, 256, 128, 128, 16)
        HEAD_DIM = EMBED // HEAD
        key = jax.random.key(seed)
        ks = jax.random.split(key, 11)
        std = 1.0 / np.sqrt(DIM)
        inp = {'q': jax.random.normal(ks[0], (B, S, DIM), jnp.float32), 'k': jax.random.normal(ks[1], (B, S, DIM), jnp.float32), 'v': jax.random.normal(ks[2], (B, S, DIM), jnp.float32), 'tri_mask': jnp.tril(jnp.ones((S, S), dtype=bool)), 'padding_mask': jnp.arange(S)[None, :] < jnp.array([S, S - 32])[:, None], 'Wq': jax.random.normal(ks[3], (EMBED, DIM), jnp.float32) * std, 'bq': jnp.zeros((EMBED,), jnp.float32), 'Wk': jax.random.normal(ks[4], (EMBED, DIM), jnp.float32) * std, 'bk': jnp.zeros((EMBED,), jnp.float32), 'Wv': jax.random.normal(ks[5], (EMBED, DIM), jnp.float32) * std, 'bv': jnp.zeros((EMBED,), jnp.float32), 'Wo': jax.random.normal(ks[6], (EMBED, EMBED), jnp.float32) * std, 'bo': jnp.zeros((EMBED,), jnp.float32)}
        return inp
    _L3_xattn_all = _L3_xattn_setup()
    _L3_xattn_in = {k: v for k, v in _L3_xattn_all.items() if k in ('Wq', 'bq', 'Wk', 'bk', 'Wv', 'bv', 'Wo', 'bo')}
    del _L3_xattn_all

    def _L3_ffn_setup():
        import jax, jax.numpy as jnp
        import numpy as np
        IN_FEATURES = 128
        OUT_FEATURES = 128
        B, S = (8, 512)
        key = jax.random.key(seed)
        kx, kw = jax.random.split(key)
        x = jax.random.normal(kx, (B, S, IN_FEATURES), dtype=jnp.float32)
        weight = jax.random.normal(kw, (OUT_FEATURES, IN_FEATURES), dtype=jnp.float32) * 0.1
        bias = jnp.zeros((OUT_FEATURES,), dtype=jnp.float32)
        return {'x': x, 'weight': weight, 'bias': bias}
    _L3_ffn_all = _L3_ffn_setup()
    _L3_ffn_in = {k: v for k, v in _L3_ffn_all.items() if k in ('weight', 'bias')}
    del _L3_ffn_all
    return {'x': x, 'ctx_1024': ctx_1024, 'itok_BxS_8_8191': itok_BxS_8_8191, 'itok_BxS2_1_8191': itok_BxS2_1_8191, 'mask_BxSxS2_if1': mask_BxSxS2_if1, 'mask_SxS2_bk0': mask_SxS2_bk0, 'mask_BxS2_bk1': mask_BxS2_bk1, 'g_xattn': g_xattn, 'g_ffn': g_ffn, 'L0_xattn_Wq': _L0_xattn_in['Wq'], 'L0_xattn_bq': _L0_xattn_in['bq'], 'L0_xattn_Wk': _L0_xattn_in['Wk'], 'L0_xattn_bk': _L0_xattn_in['bk'], 'L0_xattn_Wv': _L0_xattn_in['Wv'], 'L0_xattn_bv': _L0_xattn_in['bv'], 'L0_xattn_Wo': _L0_xattn_in['Wo'], 'L0_xattn_bo': _L0_xattn_in['bo'], 'L0_ffn_Wg': _L0_ffn_in['Wg'], 'L0_ffn_W1': _L0_ffn_in['W1'], 'L0_ffn_b1': _L0_ffn_in['b1'], 'L0_ffn_W2': _L0_ffn_in['W2'], 'L0_ffn_b2': _L0_ffn_in['b2'], 'L1_xattn_w_query': _L1_xattn_in['w_query'], 'L1_xattn_b_query': _L1_xattn_in['b_query'], 'L1_xattn_w_value': _L1_xattn_in['w_value'], 'L1_xattn_b_value': _L1_xattn_in['b_value'], 'L1_xattn_w_key': _L1_xattn_in['w_key'], 'L1_xattn_b_key': _L1_xattn_in['b_key'], 'L1_xattn_w_projection': _L1_xattn_in['w_projection'], 'L1_xattn_b_projection': _L1_xattn_in['b_projection'], 'L1_ffn_rhs': _L1_ffn_in['rhs'], 'L2_xattn_W_q': _L2_xattn_in['W_q'], 'L2_xattn_W_k': _L2_xattn_in['W_k'], 'L2_xattn_W_v': _L2_xattn_in['W_v'], 'L2_xattn_W_o': _L2_xattn_in['W_o'], 'L2_ffn_router_W': _L2_ffn_in['router_W'], 'L2_ffn_router_b': _L2_ffn_in['router_b'], 'L2_ffn_sW1': _L2_ffn_in['sW1'], 'L2_ffn_sb1': _L2_ffn_in['sb1'], 'L2_ffn_sW2': _L2_ffn_in['sW2'], 'L2_ffn_sb2': _L2_ffn_in['sb2'], 'L2_ffn_eW1': _L2_ffn_in['eW1'], 'L2_ffn_eb1': _L2_ffn_in['eb1'], 'L2_ffn_eW2': _L2_ffn_in['eW2'], 'L2_ffn_eb2': _L2_ffn_in['eb2'], 'L3_xattn_Wq': _L3_xattn_in['Wq'], 'L3_xattn_bq': _L3_xattn_in['bq'], 'L3_xattn_Wk': _L3_xattn_in['Wk'], 'L3_xattn_bk': _L3_xattn_in['bk'], 'L3_xattn_Wv': _L3_xattn_in['Wv'], 'L3_xattn_bv': _L3_xattn_in['bv'], 'L3_xattn_Wo': _L3_xattn_in['Wo'], 'L3_xattn_bo': _L3_xattn_in['bo'], 'L3_ffn_weight': _L3_ffn_in['weight'], 'L3_ffn_bias': _L3_ffn_in['bias']}

def reference(x, ctx_1024, itok_BxS_8_8191, itok_BxS2_1_8191, mask_BxSxS2_if1, mask_SxS2_bk0, mask_BxS2_bk1, g_xattn, g_ffn, L0_xattn_Wq, L0_xattn_bq, L0_xattn_Wk, L0_xattn_bk, L0_xattn_Wv, L0_xattn_bv, L0_xattn_Wo, L0_xattn_bo, L0_ffn_Wg, L0_ffn_W1, L0_ffn_b1, L0_ffn_W2, L0_ffn_b2, L1_xattn_w_query, L1_xattn_b_query, L1_xattn_w_value, L1_xattn_b_value, L1_xattn_w_key, L1_xattn_b_key, L1_xattn_w_projection, L1_xattn_b_projection, L1_ffn_rhs, L2_xattn_W_q, L2_xattn_W_k, L2_xattn_W_v, L2_xattn_W_o, L2_ffn_router_W, L2_ffn_router_b, L2_ffn_sW1, L2_ffn_sb1, L2_ffn_sW2, L2_ffn_sb2, L2_ffn_eW1, L2_ffn_eb1, L2_ffn_eW2, L2_ffn_eb2, L3_xattn_Wq, L3_xattn_bq, L3_xattn_Wk, L3_xattn_bk, L3_xattn_Wv, L3_xattn_bv, L3_xattn_Wo, L3_xattn_bo, L3_ffn_weight, L3_ffn_bias):
    import jax
    import jax.numpy as jnp

    def _L0_xattn_ref(queries, keys, values, Wq, bq, Wk, bk, Wv, bv, Wo, bo):
        import jax, jax.numpy as jnp
        import numpy as np
        D_MODEL = 64
        N_HEADS = 8
        D_KEYS = D_MODEL // N_HEADS
        DIN = D_MODEL * 2
        DPROJ = D_KEYS * N_HEADS * 2
        B, L = (2, 256)
        b, l, _ = queries.shape
        H, E = (N_HEADS, 2)
        q = (queries @ Wq.T + bq).reshape(b, l, -1, H, E)
        k = (keys @ Wk.T + bk).reshape(b, l, -1, H, E)
        v = (values @ Wv.T + bv).reshape(b, l, -1, H, E)
        scale = 1.0 / np.sqrt(E)
        scores = jnp.einsum('bnlhe,bnshe->bnhls', q, k)
        A = jax.nn.softmax(scale * scores, axis=-1)
        out = jnp.einsum('bnhls,bnshd->bnlhd', A, v)
        out = out.reshape(b, l, -1)
        return out @ Wo.T + bo

    def _L0_ffn_ref(x, Wg, W1, b1, W2, b2):
        import jax, jax.numpy as jnp
        import numpy as np
        E = 8
        TOP_K = 2
        B, S, D = (2, 512, 128)
        H = 512
        CAPACITY = 256

        def _moe(x, Wg, W1, b1, W2, b2):
            b, s, d = x.shape
            xf = x.reshape(b * s, d)
            logits = xf.astype(jnp.float32) @ Wg.astype(jnp.float32)
            probs = jax.nn.softmax(logits, axis=-1)
            vals, idx = jax.lax.top_k(probs, TOP_K)
            w = vals / (jnp.sum(vals, axis=-1, keepdims=True) + 1e-09)
            counts = jnp.zeros((E,), dtype=jnp.int32)
            combine = jnp.zeros((b * s, E), dtype=jnp.float32)
            for k in range(TOP_K):
                oh = jax.nn.one_hot(idx[:, k], E, dtype=jnp.int32)
                pos = jnp.cumsum(oh, axis=0) - 1 + counts[None, :]
                keep = (oh == 1) & (pos < CAPACITY)
                counts = counts + jnp.sum(keep.astype(jnp.int32), axis=0)
                combine = combine + w[:, k][:, None] * keep.astype(jnp.float32)
            out = jnp.zeros_like(xf)
            for e in range(E):
                h = jax.nn.gelu(xf @ W1[e] + b1[e])
                ye = h @ W2[e] + b2[e]
                out = out + combine[:, e][:, None].astype(xf.dtype) * ye
            return out.reshape(b, s, d)
        return _moe(x, Wg, W1, b1, W2, b2)

    def _L1_xattn_ref(q, v, k, w_query, b_query, w_value, b_value, w_key, b_key, w_projection, b_projection):
        import jax, jax.numpy as jnp
        import numpy as np
        B, T, D = (2, 256, 128)
        N, H = (16, 64)
        query = jnp.einsum('btd,dnh->bnth', q, w_query) + b_query
        value = jnp.einsum('btd,dnh->bnth', v, w_value) + b_value
        key_p = jnp.einsum('btd,dnh->bnth', k, w_key) + b_key
        scale = 1.0 / jnp.sqrt(jnp.asarray(H, query.dtype))
        scores = jnp.einsum('bnth,bnsh->bnts', query, key_p) * scale
        weights = jax.nn.softmax(scores, axis=-1)
        attn = jnp.einsum('bnts,bnsh->bnth', weights, value)
        out = jnp.einsum('bnth,ndh->btd', attn, w_projection) + b_projection
        return out

    def _L1_ffn_ref(lhs, rhs):
        import jax, jax.numpy as jnp
        import numpy as np
        INT8_MAX = 127.0

        def _absmax_scale(x, axes):
            amax = jnp.max(jnp.abs(x), axis=axes, keepdims=True)
            return jnp.maximum(amax, 1e-12) / INT8_MAX
        lhs_scale = _absmax_scale(lhs, (2,))
        rhs_scale = _absmax_scale(rhs, (0,))
        q_lhs = jnp.clip(jnp.round(lhs / lhs_scale), -INT8_MAX, INT8_MAX).astype(jnp.int8)
        q_rhs = jnp.clip(jnp.round(rhs / rhs_scale), -INT8_MAX, INT8_MAX).astype(jnp.int8)
        acc = jax.lax.dot_general(q_lhs, q_rhs, (((2,), (0,)), ((), ())), preferred_element_type=jnp.int32)
        return acc.astype(jnp.float32) * lhs_scale * rhs_scale

    def _L2_xattn_ref(query, keys, values, W_q, W_k, W_v, W_o, query_pos, key_pos, mask):
        import jax, jax.numpy as jnp
        import numpy as np
        DIM = 128
        NUM_HEADS = 16
        HEAD_DIM = DIM // NUM_HEADS

        def _slopes(num_heads):
            ratio = 2.0 ** (-8.0 / num_heads)
            return jnp.asarray([ratio ** i for i in range(1, num_heads + 1)], dtype=jnp.float32)
        b, q_len, _ = query.shape
        k_len = keys.shape[1]
        scale = 1.0 / np.sqrt(HEAD_DIM)
        Q = (query @ W_q.T).reshape(b, q_len, NUM_HEADS, HEAD_DIM).transpose(0, 2, 1, 3)
        K = (keys @ W_k.T).reshape(b, k_len, NUM_HEADS, HEAD_DIM).transpose(0, 2, 1, 3)
        V = (values @ W_v.T).reshape(b, k_len, NUM_HEADS, HEAD_DIM).transpose(0, 2, 1, 3)
        scores = jnp.einsum('bhqd,bhkd->bhqk', Q, K) * scale
        dist = (query_pos[:, :, None] - key_pos[:, None, :]).astype(scores.dtype)
        bias = -_slopes(NUM_HEADS)[None, :, None, None] * dist[:, None, :, :]
        scores = scores + bias
        scores = jnp.where(mask[:, None, :, :] == 0, -jnp.inf, scores)
        m = jnp.max(scores, axis=-1, keepdims=True)
        e = jnp.exp(scores - m)
        attn = e / (1.0 + jnp.sum(e, axis=-1, keepdims=True))
        out = jnp.einsum('bhqk,bhkd->bhqd', attn, V)
        out = out.transpose(0, 2, 1, 3).reshape(b, q_len, DIM)
        return out @ W_o.T

    def _L2_ffn_ref(x, router_W, router_b, sW1, sb1, sW2, sb2, eW1, eb1, eW2, eb2):
        import jax, jax.numpy as jnp
        import numpy as np
        B, L, D = (2, 256, 128)
        E = 15
        H = D * 1
        K = 3
        T = 1.0
        b, l, d = x.shape
        n = b * l
        xt = x.reshape(n, d)
        shared = jax.nn.relu(xt @ sW1 + sb1) @ sW2 + sb2
        logits = xt @ router_W + router_b
        probs = jax.nn.softmax(logits / T, axis=-1)
        top_p, top_i = jax.lax.top_k(probs, K)
        cw = jnp.zeros((n, E), dtype=probs.dtype)
        cw = cw.at[jnp.arange(n)[:, None], top_i].set(top_p)
        h = jax.nn.relu(jnp.einsum('nd,edh->neh', xt, eW1) + eb1)
        ye = jnp.einsum('neh,ehd->ned', h, eW2) + eb2
        routed = jnp.einsum('ned,ne->nd', ye, cw)
        return (shared + routed).reshape(b, l, d)

    def _L3_xattn_ref(q, k, v, tri_mask, padding_mask, Wq, bq, Wk, bk, Wv, bv, Wo, bo):
        import jax, jax.numpy as jnp
        import numpy as np
        B, S, DIM, EMBED, HEAD = (2, 256, 128, 128, 16)
        HEAD_DIM = EMBED // HEAD
        scale = EMBED ** (-0.5)
        neg = jnp.finfo(q.dtype).min

        def split_heads(x):
            b, s, _ = x.shape
            return x.reshape(b, s, HEAD, HEAD_DIM).transpose(0, 2, 1, 3)
        qh = split_heads(q @ Wq.T + bq)
        kh = split_heads(k @ Wk.T + bk)
        vh = split_heads(v @ Wv.T + bv)
        energy = jnp.einsum('bhse,bhke->bhsk', qh, kh) * scale
        keep = padding_mask[:, None, None, :] & tri_mask[None, None, :, :]
        energy = jnp.where(keep, energy, neg)
        attn = jax.nn.softmax(energy, axis=-1)
        out = jnp.einsum('bhsk,bhke->bhse', attn, vh)
        out = out.transpose(0, 2, 1, 3).reshape(q.shape[0], q.shape[1], EMBED)
        return out @ Wo.T + bo

    def _L3_ffn_ref(x, weight, bias):
        import jax, jax.numpy as jnp
        import numpy as np
        IN_FEATURES = 128
        OUT_FEATURES = 128
        B, S = (8, 512)
        w_scale = jnp.mean(jnp.abs(weight))
        q_weight = jnp.sign(weight) * (jnp.abs(weight) > 0.5 * w_scale).astype(weight.dtype)
        i_scale = jnp.max(jnp.abs(x)) / 127.0
        q_input = jnp.clip(jnp.round(x / i_scale), -128.0, 127.0)
        out = jnp.einsum('bsk,ok->bso', q_input, q_weight) * w_scale * i_scale
        out = out + bias
        return out
    x = x + jnp.tanh(g_xattn[0]) * _L0_xattn_ref(_layernorm(x, axis=-1), ctx_1024, ctx_1024, L0_xattn_Wq, L0_xattn_bq, L0_xattn_Wk, L0_xattn_bk, L0_xattn_Wv, L0_xattn_bv, L0_xattn_Wo, L0_xattn_bo)
    x = x + jnp.tanh(g_ffn[0]) * _L0_ffn_ref(_layernorm(x, axis=-1), L0_ffn_Wg, L0_ffn_W1, L0_ffn_b1, L0_ffn_W2, L0_ffn_b2)
    x = x + jnp.tanh(g_xattn[1]) * _L1_xattn_ref(_layernorm(x, axis=-1), ctx_1024, ctx_1024, L1_xattn_w_query, L1_xattn_b_query, L1_xattn_w_value, L1_xattn_b_value, L1_xattn_w_key, L1_xattn_b_key, L1_xattn_w_projection, L1_xattn_b_projection)
    x = x + jnp.tanh(g_ffn[1]) * _L1_ffn_ref(_layernorm(x, axis=-1), L1_ffn_rhs)
    x = x + jnp.tanh(g_xattn[2]) * _L2_xattn_ref(_layernorm(x, axis=-1), ctx_1024, ctx_1024, L2_xattn_W_q, L2_xattn_W_k, L2_xattn_W_v, L2_xattn_W_o, itok_BxS_8_8191, itok_BxS2_1_8191, mask_BxSxS2_if1)
    x = x + jnp.tanh(g_ffn[2]) * _L2_ffn_ref(_layernorm(x, axis=-1), L2_ffn_router_W, L2_ffn_router_b, L2_ffn_sW1, L2_ffn_sb1, L2_ffn_sW2, L2_ffn_sb2, L2_ffn_eW1, L2_ffn_eb1, L2_ffn_eW2, L2_ffn_eb2)
    x = x + jnp.tanh(g_xattn[3]) * _L3_xattn_ref(_layernorm(x, axis=-1), ctx_1024, ctx_1024, mask_SxS2_bk0, mask_BxS2_bk1, L3_xattn_Wq, L3_xattn_bq, L3_xattn_Wk, L3_xattn_bk, L3_xattn_Wv, L3_xattn_bv, L3_xattn_Wo, L3_xattn_bo)
    x = x + jnp.tanh(g_ffn[3]) * _L3_ffn_ref(_layernorm(x, axis=-1), L3_ffn_weight, L3_ffn_bias)
    return x

_drawn_inputs = setup_inputs


def setup_inputs(seed=0):
    import zlib

    import numpy as np

    out = dict(_drawn_inputs(seed))
    spreads = {'L0_ffn_b1': (0.0, 0.678),
     'L0_ffn_b2': (0.0, 0.1),
     'L1_xattn_b_query': (0.0, 0.8),
     'L1_xattn_b_value': (0.0, 0.1),
     'L1_xattn_b_key': (0.0, 0.8),
     'L1_xattn_b_projection': (0.0, 0.1),
     'L2_ffn_router_b': (0.0, 0.8),
     'L2_ffn_sb1': (0.0, 0.8),
     'L2_ffn_sb2': (0.0, 0.8),
     'L2_ffn_eb1': (0.0, 0.8),
     'L2_ffn_eb2': (0.0, 0.8),
     'L3_xattn_bq': (0.0, 0.8),
     'L3_xattn_bk': (0.0, 0.8),
     'L3_xattn_bv': (0.0, 0.8),
     'L3_xattn_bo': (0.0, 0.8),
     'L3_ffn_bias': (0.0, 0.8)}
    factors = {'L0_xattn_bq': 2.692,
     'L0_ffn_W1': 2.795,
     'L2_xattn_W_q': 4.139,
     'L2_xattn_W_k': 4.151,
     'L2_ffn_router_W': 8.0,
     'L2_ffn_sW1': 8.0,
     'L2_ffn_sW2': 8.0,
     'L2_ffn_eW1': 8.0,
     'L2_ffn_eW2': 8.0,
     'L3_xattn_Wq': 8.0,
     'L3_xattn_Wk': 8.0}
    for name, (base, spread) in spreads.items():
        noise = np.random.default_rng([zlib.crc32(name.encode()), seed]).standard_normal(out[name].shape)
        drawn = base * np.exp(spread * noise) if base else spread * noise
        out[name] = jnp.asarray(drawn.astype(out[name].dtype))
    for name, factor in factors.items():
        out[name] = (out[name] * factor).astype(out[name].dtype)
    return out
```

```python
from contextlib import ExitStack

import numpy as np

import concourse.bass as bass
from concourse import mybir

P = 128
B, S, S2, D = 8, 256, 512, 128
NTILE = B * S // P
QT = S // P
KT = S2 // P
CHUNK = 512
NCHUNK = B * S // CHUNK
HEADS = 16
BIG = 2.0 ** 100
LN_EPS = 1e-5

F32 = mybir.dt.float32
BF16 = mybir.dt.bfloat16
I32 = mybir.dt.int32
U8 = mybir.dt.uint8
U32 = mybir.dt.uint32
ALU = mybir.AluOpType
ACT = mybir.ActivationFunctionType
AX = mybir.AxisListType


class Phase:

    used = []

    def __init__(self, nc, name):
        self.nc, self.name, self.stack = nc, name, ExitStack()

    def __enter__(self):
        self.stack.__enter__()
        return self

    def __exit__(self, *exc):
        return self.stack.__exit__(*exc)

    def sb(self, name, shape, dt=F32):
        return self.stack.enter_context(self.nc.sbuf_tensor(f"{self.name}_{name}", shape, dt))

    def ps(self, name, shape, dt=F32):
        return self.stack.enter_context(self.nc.psum_tensor(f"{self.name}_{name}", shape, dt))

    def sem(self, name):
        handle = self.nc.alloc_semaphore(f"{self.name}_{name}")
        Phase.used.append(handle)
        return handle

    @staticmethod
    def clear_used(nc):
        nc.clear_and_free_semaphores(Phase.used)
        nc.all_engine_barrier()
        Phase.used.clear()

    def block(self):
        return self.nc.Block(no_gpsimd_drain=True)


class Resident:
    pass


def load_phase(nc, io, res):
    with Phase(nc, "load") as ph:
        loaded, gates_in, gates_done = ph.sem("loaded"), ph.sem("gates_in"), ph.sem("gates_done")
        ones_done, cast_done = ph.sem("ones_done"), ph.sem("cast_done")
        raw_gates = ph.sb("raw_gates", [P, 8])
        with ph.block() as block:
            @block.sync
            def _(sp):
                sp.dma_start(raw_gates[:, 0:4], io["g_xattn"].partition_broadcast(P)).then_inc(gates_in, 16)
                sp.dma_start(raw_gates[:, 4:8], io["g_ffn"].partition_broadcast(P)).then_inc(gates_in, 16)
                sp.dma_start(res.ident[:], io["c_ident"]).then_inc(loaded, 16)
                sp.dma_start(res.X[:], io["x"].rearrange("(t p) d -> p t d", p=P)).then_inc(loaded, 16)
                sp.wait_ge(loaded, 32)

            @block.scalar
            def _(act):
                act.wait_ge(gates_in, 32)
                act.activation(res.gates[:], raw_gates[:], ACT.Tanh).then_inc(gates_done, 1)
                act.wait_ge(gates_done, 1)

            @block.vector
            def _(dve):
                dve.memset(res.ones[:], 1.0).then_inc(ones_done, 1)
                dve.memset(res.onesb[:], 1.0).then_inc(ones_done, 1)
                dve.wait_ge(loaded, 32)
                dve.tensor_copy(res.identb[:], res.ident[:]).then_inc(cast_done, 1)
                dve.wait_ge(cast_done, 1)
                dve.wait_ge(ones_done, 2)


def norm_phase(nc, io, res, name, transposed=True):
    with Phase(nc, name) as ph:
        stats = ph.sb("stats", [P, NTILE, 6])
        mv = ph.sb("mv", [P, NTILE, 2])
        std = ph.sb("std", [P, NTILE])
        r0 = ph.sb("r0", [P, NTILE])
        rr = ph.sb("rr", [P, NTILE])
        rstd = ph.sb("rstd", [P, NTILE])
        var_eps = ph.sb("var_eps", [P, NTILE])
        psT = [ph.ps(f"psT{i}", [P, CHUNK]) for i in range(2)]
        stats_done, aggr_done = ph.sem("stats_done"), ph.sem("aggr_done")
        var_done, std_done, newton = ph.sem("var_done"), ph.sem("std_done"), ph.sem("newton")
        xn_done, turned, copied = ph.sem("xn_done"), ph.sem("turned"), ph.sem("copied")
        with ph.block() as block:
            @block.vector
            def _(dve):
                for t in range(NTILE):
                    dve.bn_stats(stats[:, t, :], res.X[:, t, :]).then_inc(stats_done, 1)
                for t in range(NTILE):
                    dve.wait_ge(stats_done, t + 1)
                    dve.bn_aggr(mv[:, t, :], stats[:, t, :]).then_inc(aggr_done, 1)
                dve.wait_ge(aggr_done, NTILE)
                dve.tensor_scalar(var_eps[:], mv[:, :, 1], LN_EPS, None, ALU.add).then_inc(var_done, 1)
                dve.wait_ge(std_done, 1)
                dve.reciprocal(r0[:], std[:]).then_inc(newton, 1)
                dve.wait_ge(newton, 1)
                dve.tensor_tensor(rr[:], r0[:], r0[:], ALU.mult).then_inc(newton, 1)
                dve.wait_ge(newton, 2)
                dve.tensor_tensor(std[:], rr[:], var_eps[:], ALU.mult).then_inc(newton, 1)
                dve.wait_ge(newton, 3)
                dve.tensor_scalar(rr[:], std[:], -0.5, 1.5, ALU.mult, ALU.add).then_inc(newton, 1)
                dve.wait_ge(newton, 4)
                dve.tensor_tensor(rstd[:], r0[:], rr[:], ALU.mult).then_inc(newton, 1)
                dve.wait_ge(newton, 5)
                for t in range(NTILE):
                    dve.tensor_scalar(res.xn[:, t, :], res.X[:, t, :], mv[:, t, 0:1], rstd[:, t:t + 1],
                                      ALU.subtract, ALU.mult).then_inc(xn_done, 1)
                dve.wait_ge(xn_done, NTILE)

            @block.scalar
            def _(act):
                act.wait_ge(var_done, 1)
                act.activation(std[:], var_eps[:], ACT.Sqrt).then_inc(std_done, 1)
                if transposed:
                    for c in range(NCHUNK):
                        act.wait_ge(turned, c + 1)
                        act.copy(res.xnT[:, c * CHUNK:(c + 1) * CHUNK], psT[c % 2][:]).then_inc(copied, 1)
                    act.wait_ge(copied, NCHUNK)

            @block.tensor
            def _(pe):
                if transposed:
                    for c in range(NCHUNK):
                        if c >= 2:
                            pe.wait_ge(copied, c - 1)
                        for k in range(4):
                            t = 4 * c + k
                            pe.wait_ge(xn_done, t + 1)
                            last = pe.transpose(psT[c % 2][:, k * P:(k + 1) * P], res.xn[:, t, :], res.ident[:])
                        last.then_inc(turned, 1)


def store_phase(nc, io, res):
    with Phase(nc, "store") as ph:
        stored = ph.sem("stored")
        with ph.block() as block:
            @block.sync
            def _(sp):
                sp.dma_start(io["out"].rearrange("(t p) d -> p t d", p=P), res.X[:]).then_inc(stored, 16)
                sp.wait_ge(stored, 16)



L0_GROUPS, L0_HEADS, L0_E = 8, 8, 2
L0_KEYS = 2 * L0_GROUPS
L0_SCORES = L0_GROUPS * L0_HEADS * L0_KEYS


def layer0_attention(nc, io, res):
    scale = 1.0 / float(np.sqrt(L0_E))
    with Phase(nc, "a0") as ph:
        Q = ph.sb("Q", [P, NTILE, D])
        K = ph.sb("K", [P, NTILE, 2, D])
        V = ph.sb("V", [P, NTILE, 2, D])
        O = ph.sb("O", [P, NTILE, D])
        project_qkv_layer0(nc, io, res, Q, K, V)
        attend_layer0(nc, Q, K, V, O, scale)
        with Phase(nc, "a0o") as po:
            project_out(nc, io, res, po, O, "L0_WoT", "L0_bo", res.gates[:, 0:1])


def project_qkv_layer0(nc, io, res, Q, K, V):
    with Phase(nc, "a0p") as ph:
        ctxT = ph.sb("ctxT", [P, NTILE, P, 2])
        wq = ph.sb("wq", [P, D])
        wkv = ph.sb("wkv", [P, 2 * D])
        bq = ph.sb("bq", [P, D])
        bkv = ph.sb("bkv", [P, 2, 2 * D])
        psQ = [ph.ps(f"psQ{i}", [P, CHUNK]) for i in range(2)]
        psKV = [ph.ps(f"psKV{i}", [P, 2, 2 * D]) for i in range(2)]
        w_in, ctx_in = ph.sem("w_in"), [ph.sem(f"ctx_in{i}") for i in range(4)]
        q_ready, kv_ready, q_out, kv_out = ph.sem("q_ready"), ph.sem("kv_ready"), ph.sem("q_out"), ph.sem("kv_out")
        n_w = 7
        with ph.block() as block:
            @block.sync
            def _(sp):
                sp.dma_start(wq[:], io["L0_WqT"]).then_inc(w_in, 16)
                sp.dma_start(wkv[:, 0:D], io["L0_WkT"]).then_inc(w_in, 16)
                sp.dma_start(wkv[:, D:2 * D], io["L0_WvT"]).then_inc(w_in, 16)
                sp.dma_start(bq[:], io["L0_bq"].partition_broadcast(P)).then_inc(w_in, 16)
                for j, name in enumerate(("L0_bk", "L0_bv")):
                    for two in range(2):
                        if j == 1 and two == 1:
                            continue
                        sp.dma_start(bkv[:, two, j * D:(j + 1) * D], io[name].partition_broadcast(P)).then_inc(w_in, 16)
                sp.dma_start(bkv[:, 1, D:2 * D], io["L0_bv"].partition_broadcast(P)).then_inc(ctx_in[0], 16)
                for i in range(4):
                    sp.dma_start(ctxT[:, 4 * i:4 * i + 4], io["ctxT"].rearrange("d (t n c) -> d t n c", n=P, c=2)[:, 4 * i:4 * i + 4]).then_inc(ctx_in[i], 16)

            @block.tensor
            def _(pe):
                pe.wait_ge(w_in, 16 * n_w)
                for t in range(NTILE):
                    if t % 4 == 0:
                        pe.wait_ge(ctx_in[t // 4], 32 if t == 0 else 16)
                    if t >= 2:
                        pe.wait_ge(q_out, t - 1)
                        pe.wait_ge(kv_out, 2 * (t - 1))
                    pe.matmul(psQ[t % 2][:, 0:D], res.xnT[:, t * P:(t + 1) * P], wq[:], start=True, stop=True).then_inc(q_ready, 1)
                    for two in range(2):
                        last = pe.matmul(psKV[t % 2][:, two, :], ctxT[:, t, :, two], wkv[:], start=True, stop=True)
                    last.then_inc(kv_ready, 1)

            @block.vector
            def _(dve):
                dve.wait_ge(w_in, 16 * n_w)
                dve.wait_ge(ctx_in[0], 32)
                for t in range(NTILE):
                    dve.wait_ge(q_ready, t + 1)
                    dve.tensor_tensor(Q[:, t, :], psQ[t % 2][:, 0:D], bq[:], ALU.add).then_inc(q_out, 1)
                    dve.wait_ge(kv_ready, t + 1)
                    dve.tensor_tensor(K[:, t], psKV[t % 2][:, :, 0:D], bkv[:, :, 0:D], ALU.add).then_inc(kv_out, 1)
                    dve.tensor_tensor(V[:, t], psKV[t % 2][:, :, D:2 * D], bkv[:, :, D:2 * D], ALU.add).then_inc(kv_out, 1)


def attend_layer0(nc, Q, K, V, O, scale):
    full = [P, L0_GROUPS, L0_HEADS, L0_KEYS]
    rows = L0_GROUPS * L0_HEADS
    with Phase(nc, "a0a") as ph:
        m0 = [ph.sb(f"m0_{i}", full) for i in range(2)]
        sc = [ph.sb(f"sc_{i}", full) for i in range(2)]
        ex = [ph.sb(f"ex_{i}", full) for i in range(2)]
        pv0 = [ph.sb(f"pv0_{i}", full) for i in range(2)]
        pv1 = ph.sb("pv1", full)
        m1 = ph.sb("m1", full)
        mx = [ph.sb(f"mx_{i}", [P, rows]) for i in range(2)]
        den = ph.sb("den", [P, rows])
        rec = ph.sb("rec", [P, rows])
        osum = ph.sb("osum", [P, 2, rows])
        m0_done, m1_done, add_done, max_done = (ph.sem(n) for n in ("m0_done", "m1_done", "add_done", "max_done"))
        sub_done, exp_done, pv0_done, pv1_done = (ph.sem(n) for n in ("sub_done", "exp_done", "pv0_done", "pv1_done"))
        den_done, rec_done, osum_done, norm_done = (ph.sem(n) for n in ("den_done", "rec_done", "osum_done", "norm_done"))

        def q_of(t, e):
            v = Q[:, bass.ds(t, 1), :].rearrange("p o (l h e) -> p (o l) h e", h=L0_HEADS, e=L0_E)
            return v[:, :, :, e:e + 1].to_broadcast(full)

        def kv_of(M, t, e):
            v = M[:, bass.ds(t, 1), :, :].rearrange("p o c (s h e) -> p e o h (c s)", h=L0_HEADS, e=L0_E)
            return v[:, e, :, :, :].to_broadcast(full)

        def flat(a):
            return a[:].rearrange("p l h s -> p (l h) s")

        with ph.block() as block:
            @block.gpsimd
            def _(pool):
                def products(t, b):
                    pool.tensor_tensor(m0[b][:], q_of(t, 0), kv_of(K, t, 0), ALU.mult).then_inc(m0_done, 1)

                def subtract(t, b):
                    pool.wait_ge(max_done, t + 1)
                    pool.tensor_tensor(flat(sc[b]), flat(sc[b]), mx[b][:].unsqueeze(2).to_broadcast([P, rows, L0_KEYS]),
                                       ALU.subtract).then_inc(sub_done, 1)

                def weighted(t, b):
                    pool.wait_ge(exp_done, t + 1)
                    pool.tensor_tensor(pv0[b][:], ex[b][:], kv_of(V, t, 0), ALU.mult).then_inc(pv0_done, 1)

                def step(v, b, first=False, last=False):
                    weighted(v - 1, 1 - b)
                    if not last:
                        pool.wait_ge(add_done, v)
                        products(v + 1, 1 - b)
                    subtract(v, b)

                products(0, 0)
                products(1, 1)
                subtract(0, 0)
                with pool.Fori(0, (NTILE - 2) // 2) as i:
                    for k in range(2):
                        step(2 * i + 1 + k, (1 + k) % 2)
                step(NTILE - 1, 1, last=True)
                weighted(NTILE - 1, 1)

            @block.scalar
            def _(act):
                with act.Fori(0, NTILE // 2) as i:
                    for b in range(2):
                        act.wait_ge(sub_done, 2 * i + b + 1)
                        act.activation(ex[b][:], sc[b][:], ACT.Exp, scale=scale).then_inc(exp_done, 1)

            @block.vector
            def _(dve):
                def front(t, b, first=False):
                    dve.tensor_tensor(m1[:], q_of(t, 1), kv_of(K, t, 1), ALU.mult).then_inc(m1_done, 1)
                    dve.wait_ge(m0_done, t + 1)
                    dve.wait_ge(m1_done, t + 1)
                    if not first:
                        dve.wait_ge(exp_done, t - 1)
                    dve.tensor_tensor(sc[b][:], m0[b][:], m1[:], ALU.add).then_inc(add_done, 1)
                    dve.wait_ge(add_done, t + 1)
                    dve.tensor_reduce(mx[b][:], flat(sc[b]), AX.X, ALU.max).then_inc(max_done, 1)

                def back(t, b):
                    dve.wait_ge(exp_done, t + 1)
                    dve.tensor_reduce(den[:], flat(ex[b]), AX.X, ALU.add).then_inc(den_done, 1)
                    dve.tensor_tensor(pv1[:], ex[b][:], kv_of(V, t, 1), ALU.mult).then_inc(pv1_done, 1)
                    dve.wait_ge(den_done, t + 1)
                    dve.reciprocal(rec[:], den[:]).then_inc(rec_done, 1)
                    dve.wait_ge(pv1_done, t + 1)
                    dve.tensor_reduce(osum[:, 1, :], flat(pv1), AX.X, ALU.add).then_inc(osum_done, 1)
                    dve.wait_ge(pv0_done, t + 1)
                    dve.tensor_reduce(osum[:, 0, :], flat(pv0[b]), AX.X, ALU.add).then_inc(osum_done, 1)
                    dve.wait_ge(rec_done, t + 1)
                    dve.wait_ge(osum_done, 2 * (t + 1))
                    dve.tensor_tensor(O[:, bass.ds(t, 1), :].rearrange("p o (r e) -> p (o r) e", e=L0_E),
                                      osum[:].rearrange("p e r -> p r e"),
                                      rec[:].unsqueeze(2).to_broadcast([P, rows, L0_E]), ALU.mult).then_inc(norm_done, 1)

                front(0, 0, first=True)
                front(1, 1, first=True)
                back(0, 0)
                with dve.Fori(0, (NTILE - 2) // 2) as i:
                    for k in range(2):
                        front(2 * i + 2 + k, k)
                        back(2 * i + 1 + k, (1 + k) % 2)
                back(NTILE - 1, 1)
                dve.wait_ge(norm_done, NTILE)


def project_out(nc, io, res, ph, O, wo_name, bo_name, gate):
    wo = ph.sb("wo", [P, D])
    bo = ph.sb("bo", [1, D])
    OT = [ph.sb(f"OT{i}", [P, CHUNK]) for i in range(2)]
    psT = [ph.ps(f"psT{i}", [P, CHUNK]) for i in range(2)]
    psY = [ph.ps(f"psY{i}", [P, CHUNK]) for i in range(2)]
    w_in, turned, copied, projected, added = (ph.sem(n) for n in ("w_in", "turned", "copied", "projected", "added"))
    with ph.block() as block:
        @block.sync
        def _(sp):
            sp.dma_start(wo[:], io[wo_name]).then_inc(w_in, 16)
            sp.dma_start(bo[:], io[bo_name].unsqueeze(0)).then_inc(w_in, 16)

        @block.tensor
        def _(pe):
            def turn(c):
                if c >= 2:
                    pe.wait_ge(copied, c - 1)
                for k in range(4):
                    last = pe.transpose(psT[c % 2][:, k * P:(k + 1) * P], O[:, 4 * c + k, :], res.ident[:])
                last.then_inc(turned, 1)

            turn(0)
            pe.wait_ge(w_in, 32)
            for c in range(NCHUNK):
                if c + 1 < NCHUNK:
                    turn(c + 1)
                pe.wait_ge(copied, c + 1)
                if c >= 2:
                    pe.wait_ge(added, c - 1)
                for k in range(4):
                    y = psY[c % 2][:, k * P:(k + 1) * P]
                    pe.matmul(y, res.ones[0:1, :], bo[:], start=True, stop=False)
                    last = pe.matmul(y, OT[c % 2][:, k * P:(k + 1) * P], wo[:], start=False, stop=True)
                last.then_inc(projected, 1)

        @block.scalar
        def _(act):
            for c in range(NCHUNK):
                act.wait_ge(turned, c + 1)
                if c >= 2:
                    act.wait_ge(projected, c - 1)
                act.copy(OT[c % 2][:], psT[c % 2][:]).then_inc(copied, 1)

        @block.vector
        def _(dve):
            for c in range(NCHUNK):
                dve.wait_ge(projected, c + 1)
                x = res.X[:, 4 * c:4 * c + 4, :].rearrange("p t d -> p (t d)")
                dve.scalar_tensor_tensor(x, psY[c % 2][:], gate, x, ALU.mult, ALU.add).then_inc(added, 1)
            dve.wait_ge(added, NCHUNK)



def experts(nc, io, res, name, E, H, act_fn, weights, biases, out_bias, combine, gate_done=None):
    HC = H // P
    w1_dram, w2_dram = weights
    HB = max(2, HC)
    with Phase(nc, name) as ph:
        w1 = [ph.sb(f"w1_{i}", [P, H]) for i in range(2)]
        w2 = [ph.sb(f"w2_{i}", [P, HC, D]) for i in range(2)]
        b1 = [ph.sb(f"b1_{i}", [P, HC]) for i in range(2)]
        b2 = ph.sb("b2", [E, D])
        hT = [ph.sb(f"hT{i}", [P, HC, CHUNK]) for i in range(2)]
        cT = ph.sb("cT", [E, NTILE, P])
        psH = [ph.ps(f"psH{i}", [P, CHUNK]) for i in range(HB)]
        psY = [ph.ps(f"psY{i}", [P, 4, D]) for i in range(2)]
        w_in = [ph.sem(f"w_in{i}") for i in range(2)]
        b2_in, hidden, acted, made, added = (ph.sem(n) for n in ("b2_in", "hidden", "acted", "made", "added"))
        c_turned, c_copied, b2_made, b2_added = (ph.sem(n) for n in ("c_turned", "c_copied", "b2_made", "b2_added"))
        n_hidden = NCHUNK * HC

        with ph.block() as block:
            @block.sync
            def _(sp):
                def load(e, b):
                    ds = bass.ds(e, 1)
                    sp.dma_start(w1[b][:], w1_dram[ds].rearrange("o p h -> p (o h)")).then_inc(w_in[b], 16)
                    sp.dma_start(w2[b][:], w2_dram[ds].rearrange("o (c p) d -> p (o c) d", p=P)).then_inc(w_in[b], 16)
                    sp.dma_start(b1[b][:], biases[ds].rearrange("o p c -> p (o c)")).then_inc(w_in[b], 16)

                sp.dma_start(b2[:], out_bias).then_inc(b2_in, 16)
                for b in range(2):
                    load(b, b)
                with sp.Fori(1, E // 2) as i:
                    for b in range(2):
                        sp.wait_ge(made, (2 * i + b - 1) * NCHUNK)
                        load(2 * i + b, b)

            @block.tensor
            def _(pe):
                def expert(e, b, first):
                    pe.wait_ge(w_in[b], 48 * (e // 2 + 1) if first else 48 * (first_i[0] + 1))
                    for c in range(NCHUNK + 1):
                        if c < NCHUNK:
                            for k in range(HC):
                                n = c * HC + k
                                bank = n % HB
                                if not first or n >= HB:
                                    pe.wait_ge(acted, e * n_hidden + n - HB + 1)
                                pe.matmul(psH[bank][:], w1[b][:, k * P:(k + 1) * P], res.xnT[:, c * CHUNK:(c + 1) * CHUNK],
                                          start=True, stop=True).then_inc(hidden, 1)
                        if c >= 1:
                            m = c - 1
                            pe.wait_ge(acted, e * n_hidden + c * HC)
                            if not first or m >= 2:
                                pe.wait_ge(added, e * NCHUNK + m - 1)
                            for t in range(4):
                                for k in range(HC):
                                    last = pe.matmul(psY[m % 2][:, t, :], hT[m % 2][:, k, t * P:(t + 1) * P], w2[b][:, k, :],
                                                     start=(k == 0), stop=(k == HC - 1))
                            last.then_inc(made, 1)

                first_i = [0]
                expert(0, 0, True)
                first_i[0] = 0
                expert(1, 1, False)
                with pe.Fori(1, E // 2) as i:
                    first_i[0] = i
                    for b in range(2):
                        expert(2 * i + b, b, False)
                pe.wait_ge(b2_in, 16)
                for c in range(NCHUNK):
                    pe.wait_ge(acted, E * n_hidden)
                    if c >= 2:
                        pe.wait_ge(c_copied, c - 1)
                    for t in range(4):
                        last = pe.transpose(psH[c % 2][0:E, t * P:(t + 1) * P], combine[:, :, 4 * c + t], res.ident[:])
                    last.then_inc(c_turned, 1)
                for c in range(NCHUNK):
                    pe.wait_ge(c_copied, c + 1)
                    pe.wait_ge(added, E * NCHUNK)
                    if c >= 2:
                        pe.wait_ge(b2_added, c - 1)
                    for t in range(4):
                        last = pe.matmul(psY[c % 2][:, t, :], cT[:, 4 * c + t, :], b2[:], start=True, stop=True)
                    last.then_inc(b2_made, 1)

            @block.scalar
            def _(act):
                def expert(e, b, first, i):
                    act.wait_ge(w_in[b], 48 * (i + 1))
                    for c in range(NCHUNK):
                        if not first or c >= 2:
                            act.wait_ge(made, e * NCHUNK + c - 1)
                        for k in range(HC):
                            n = c * HC + k
                            act.wait_ge(hidden, e * n_hidden + n + 1)
                            act.activation(hT[c % 2][:, k, :], psH[n % HB][:], act_fn, bias=b1[b][:, k:k + 1]).then_inc(acted, 1)

                expert(0, 0, True, 0)
                expert(1, 1, False, 0)
                with act.Fori(1, E // 2) as i:
                    for b in range(2):
                        expert(2 * i + b, b, False, i)
                for c in range(NCHUNK):
                    act.wait_ge(c_turned, c + 1)
                    act.copy(cT[:, 4 * c:4 * c + 4, :].rearrange("e t p -> e (t p)"), psH[c % 2][0:E, :]).then_inc(c_copied, 1)

            @block.vector
            def _(dve):
                with dve.Fori(0, E) as e:
                    for c in range(NCHUNK):
                        dve.wait_ge(made, e * NCHUNK + c + 1)
                        for k in range(4):
                            t = 4 * c + k
                            last = dve.scalar_tensor_tensor(res.X[:, t, :], psY[c % 2][:, k, :], combine[:, bass.ds(e, 1), t],
                                                            res.X[:, t, :], ALU.mult, ALU.add)
                        last.then_inc(added, 1)
                for c in range(NCHUNK):
                    dve.wait_ge(b2_made, c + 1)
                    x = res.X[:, 4 * c:4 * c + 4, :]
                    dve.tensor_tensor(x, psY[c % 2][:], x, ALU.add).then_inc(b2_added, 1)
                dve.wait_ge(b2_added, NCHUNK)


def route(nc, io, res, name, E, top_k, w_name, b_name, finish):
    EP = max(E, 8)
    with Phase(nc, name) as ph:
        wg = ph.sb("wg", [P, E])
        bg = ph.sb("bg", [P, E])
        iota = ph.sb("iota", [P, E])
        prob = ph.sb("prob", [P, NTILE, E])
        top = ph.sb("top", [P, NTILE])
        den = ph.sb("den", [P, NTILE])
        rec = ph.sb("rec", [P, NTILE])
        val = ph.sb("val", [P, NTILE, 8])
        idx = ph.sb("idx", [P, NTILE, 8], U32)
        idxf = ph.sb("idxf", [P, NTILE, 8])
        onehot = ph.sb("onehot", [P, top_k, NTILE, E])
        psL = ph.ps("psL", [P, NTILE, E])
        w_in, logits, biased, topped, shifted, exped, summed, inverted, normed = (
            ph.sem(n) for n in ("w_in", "logits", "biased", "topped", "shifted", "exped", "summed", "inverted", "normed"))
        sorted_, indexed, floated, hot = (ph.sem(n) for n in ("sorted", "indexed", "floated", "hot"))
        wide = [P, NTILE, E]
        with ph.block() as block:
            @block.sync
            def _(sp):
                sp.dma_start(wg[:], io[w_name]).then_inc(w_in, 16)
                sp.dma_start(iota[:], io["c_iota"][0:E].partition_broadcast(P)).then_inc(w_in, 16)
                if b_name:
                    sp.dma_start(bg[:], io[b_name].partition_broadcast(P)).then_inc(w_in, 16)

            @block.tensor
            def _(pe):
                pe.wait_ge(w_in, 48 if b_name else 32)
                for t in range(NTILE):
                    last = pe.matmul(psL[:, t, :], res.xnT[:, t * P:(t + 1) * P], wg[:], start=True, stop=True)
                last.then_inc(logits, 1)

            @block.scalar
            def _(act):
                act.wait_ge(shifted, 1)
                act.activation(prob[:], prob[:], ACT.Exp).then_inc(exped, 1)

            @block.vector
            def _(dve):
                dve.wait_ge(w_in, 48 if b_name else 32)
                dve.wait_ge(logits, 1)
                if b_name:
                    dve.tensor_tensor(prob[:], psL[:], bg[:].unsqueeze(1).to_broadcast(wide), ALU.add).then_inc(biased, 1)
                else:
                    dve.tensor_copy(prob[:], psL[:]).then_inc(biased, 1)
                dve.wait_ge(biased, 1)
                dve.tensor_reduce(top[:], prob[:], AX.X, ALU.max).then_inc(topped, 1)
                dve.wait_ge(topped, 1)
                dve.tensor_tensor(prob[:], prob[:], top[:].unsqueeze(2).to_broadcast(wide), ALU.subtract).then_inc(shifted, 1)
                dve.wait_ge(exped, 1)
                dve.tensor_reduce(den[:], prob[:], AX.X, ALU.add).then_inc(summed, 1)
                dve.wait_ge(summed, 1)
                dve.reciprocal(rec[:], den[:]).then_inc(inverted, 1)
                dve.wait_ge(inverted, 1)
                dve.tensor_tensor(prob[:], prob[:], rec[:].unsqueeze(2).to_broadcast(wide), ALU.mult).then_inc(normed, 1)
                dve.wait_ge(normed, 1)
                for t in range(NTILE):
                    dve.max(val[:, t, :], prob[:, t, :]).then_inc(sorted_, 1)
                for t in range(NTILE):
                    dve.wait_ge(sorted_, t + 1)
                    dve.max_index(idx[:, t, :], val[:, t, :], prob[:, t, :]).then_inc(indexed, 1)
                dve.wait_ge(indexed, NTILE)
                dve.tensor_copy(idxf[:], idx[:]).then_inc(floated, 1)
                dve.wait_ge(floated, 1)
                for k in range(top_k):
                    dve.tensor_tensor(onehot[:, k], iota[:].unsqueeze(1).to_broadcast(wide),
                                      idxf[:, :, k:k + 1].to_broadcast(wide), ALU.is_equal).then_inc(hot, 1)
                dve.wait_ge(hot, top_k)
        finish(ph, prob, val, onehot)


def layer0_experts(nc, io, res):
    E, H, capacity = 8, 512, 256
    wide = [P, NTILE, E]
    with Phase(nc, "f0") as outer:
        combine = outer.sb("combine", [P, E, NTILE])

        def keep_by_capacity(ph, prob, val, onehot):
            tri = ph.sb("tri", [P, P])
            psC = [ph.ps(f"psC{k}", wide) for k in range(2)]
            psT = ph.ps("psT", [P, E])
            kept = ph.sb("kept", [P, 2, NTILE, E])
            weighted = ph.sb("weighted", [P, 2, NTILE, E])
            first = ph.sb("first", [P, E])
            pair = ph.sb("pair", [P, NTILE])
            inv = ph.sb("inv", [P, NTILE])
            weight = ph.sb("weight", [P, 2, NTILE])
            tri_in, counted, step = ph.sem("tri_in"), ph.sem("counted"), ph.sem("step")
            with ph.block() as block:
                @block.sync
                def _(sp):
                    sp.dma_start(tri[:], io["c_tri"]).then_inc(tri_in, 16)

                @block.tensor
                def _(pe):
                    pe.wait_ge(tri_in, 16)
                    for k in range(2):
                        pe.matmul(psC[k][:], tri[:], onehot[:, k], start=True, stop=False, skip_group_check=True)
                        for t in range(NTILE - 1):
                            last = pe.matmul(psC[k][:, t + 1:, :], res.ones[:], onehot[:, k, t:t + 1, :].to_broadcast([P, NTILE - 1 - t, E]),
                                             start=False, stop=(t == NTILE - 2), skip_group_check=True)
                        last.then_inc(counted, 1)
                    for t in range(NTILE):
                        last = pe.matmul(psT[:], res.ones[:], onehot[:, 0, t, :], start=(t == 0), stop=(t == NTILE - 1))
                    last.then_inc(counted, 1)

                @block.vector
                def _(dve):
                    dve.tensor_tensor(pair[:], val[:, :, 0], val[:, :, 1], ALU.add).then_inc(step, 1)
                    dve.wait_ge(step, 1)
                    dve.tensor_scalar(pair[:], pair[:], 1e-9, None, ALU.add).then_inc(step, 1)
                    dve.wait_ge(step, 2)
                    dve.reciprocal(inv[:], pair[:]).then_inc(step, 1)
                    dve.wait_ge(step, 3)
                    for k in range(2):
                        dve.scalar_tensor_tensor(weight[:, k], val[:, :, k], res.gates[:, 4:5], inv[:], ALU.mult, ALU.mult).then_inc(step, 1)
                    dve.wait_ge(counted, 3)
                    dve.tensor_scalar(first[:], psT[:], float(capacity), None, ALU.min).then_inc(step, 1)
                    dve.tensor_scalar(kept[:, 0], psC[0][:], float(capacity), None, ALU.is_le).then_inc(step, 1)
                    dve.wait_ge(step, 7)
                    dve.tensor_tensor(kept[:, 1], psC[1][:], first[:].unsqueeze(1).to_broadcast(wide), ALU.add).then_inc(step, 1)
                    dve.wait_ge(step, 8)
                    dve.tensor_scalar(kept[:, 1], kept[:, 1], float(capacity), None, ALU.is_le).then_inc(step, 1)
                    dve.wait_ge(step, 9)
                    for k in range(2):
                        dve.tensor_tensor(weighted[:, k], kept[:, k], onehot[:, k], ALU.mult).then_inc(step, 1)
                    dve.wait_ge(step, 11)
                    for k in range(2):
                        dve.tensor_tensor(kept[:, k], weighted[:, k], weight[:, k].unsqueeze(2).to_broadcast(wide), ALU.mult).then_inc(step, 1)
                    dve.wait_ge(step, 13)
                    dve.tensor_tensor(combine[:].rearrange("p e t -> p t e"), kept[:, 0], kept[:, 1], ALU.add).then_inc(step, 1)
                    dve.wait_ge(step, 14)

        route(nc, io, res, "f0r", E, 2, "L0_Wg", None, keep_by_capacity)
        experts(nc, io, res, "f0e", E, H, ACT.Gelu_apprx_tanh, (io["L0_W1"], io["L0_W2"]), io["L0_b1"], io["L0_b2"], combine)


def layer2_experts(nc, io, res):
    E, top_k = 15, 3
    with Phase(nc, "f2") as outer:
        combine = outer.sb("combine", [P, E + 1, NTILE])

        def chosen(ph, prob, val, onehot):
            mask = ph.sb("mask", [P, NTILE, E])
            step = ph.sem("step")
            with ph.block() as block:
                @block.vector
                def _(dve):
                    dve.tensor_copy(combine[:, 0, :], res.gates[:, 6:7].to_broadcast([P, NTILE])).then_inc(step, 1)
                    dve.tensor_tensor(mask[:], onehot[:, 0], onehot[:, 1], ALU.add).then_inc(step, 1)
                    dve.wait_ge(step, 2)
                    dve.tensor_tensor(mask[:], mask[:], onehot[:, 2], ALU.add).then_inc(step, 1)
                    dve.wait_ge(step, 3)
                    dve.scalar_tensor_tensor(combine[:, 1:, :].rearrange("p e t -> p t e"), mask[:], res.gates[:, 6:7], prob[:],
                                             ALU.mult, ALU.mult).then_inc(step, 1)
                    dve.wait_ge(step, 4)

        route(nc, io, res, "f2r", E, top_k, "L2_router_W", "L2_router_b", chosen)
        experts(nc, io, res, "f2e", E + 1, D, ACT.Relu, (io["L2_W1"], io["L2_W2"]), io["L2_b1"], io["L2_b2"], combine)



HEAD_E = D // HEADS
PAIRS = HEADS // 2
PAIR_ROWS = 2 * HEAD_E
COMBOS = ((0, 0), (0, 1), (0, 2), (1, 0), (1, 1), (2, 0))
COMBO_ROWS = len(COMBOS) * PAIR_ROWS
RING = 3
V_COLS = 32
SLOT = HEAD_E + 1


class LayerTwo:
    name, weights, q_bias = "a2", "L2", False
    scale = 1.0 / float(np.sqrt(HEAD_E))
    gate, sink, slopes = 2, 1.0, True


class LayerThree:
    name, weights, q_bias = "a3", "L3", True
    scale = float(D) ** -0.5
    gate, sink, slopes = 3, 0.0, False


def split_and_store(nc, io, res, cfg, qs, ks, ps_scr, bias_row, wo):
    n_q, n_k = NCHUNK, B * S2 // CHUNK
    with Phase(nc, cfg.name + "p") as ph:
        wq, wk = ph.sb("wq", [P, D]), ph.sb("wk", [P, D])
        bq, bk, bv = ph.sb("bq", [P, 1]), ph.sb("bk", [P, 1]), ph.sb("bv", [P, 1])
        bqs = ph.sb("bqs", [P, 1])
        bo = ph.sb("bo", [1, D])
        ctx = [ph.sb(f"ctx{i}", [P, CHUNK]) for i in range(2)]
        y = [ph.sb(f"y{i}", [P, CHUNK]) for i in range(2)]
        rest = ph.sb("rest", [P, CHUNK])
        parts = [ph.sb(f"parts{i}", [P, 3, CHUNK], BF16) for i in range(2)]
        pos = ph.sb("pos", [B, S2], I32)
        posf, posr = ph.sb("posf", [B, S2]), ph.sb("posr", [B, S2])
        pos_parts = ph.sb("pos_parts", [B, 3, S2], BF16)
        psY = [ph.ps(f"psY{i}", [P, CHUNK]) for i in range(2)]
        psB = ph.ps("psB", [1, D])
        w_in, ctx_in, projected, biased = ph.sem("w_in"), [ph.sem(f"ctx_in{i}") for i in range(2)], ph.sem("projected"), ph.sem("biased")
        split, pos_split, bias_made, bias_scaled = ph.sem("split"), ph.sem("pos_split"), ph.sem("bias_made"), ph.sem("bias_scaled")
        stored, row_done = [ph.sem(f"stored{i}") for i in range(2)], ph.sem("row_done")
        n_w = 3 + 4 * cfg.q_bias + cfg.slopes
        w = cfg.weights
        with ph.block() as block:
            @block.sync
            def _(sp):
                sp.dma_start(wq[:], io[w + "_WqT"]).then_inc(w_in, 16)
                sp.dma_start(wk[:], io[w + "_WkT"]).then_inc(w_in, 16)
                sp.dma_start(wo[:], io[w + "_WoT"]).then_inc(w_in, 16)
                if cfg.q_bias:
                    for t, b in ((bq, "_bq"), (bk, "_bk"), (bv, "_bv")):
                        sp.dma_start(t[:], io[w + b].unsqueeze(1)).then_inc(w_in, 16)
                    sp.dma_start(bo[:], io[w + "_bo"].unsqueeze(0)).then_inc(w_in, 16)
                if cfg.slopes:
                    sp.dma_start(pos[:], io["key_pos"]).then_inc(w_in, 16)
                for n in range(n_k):
                    if n >= 2:
                        sp.wait_ge(projected, n_q + n - 1)
                    sp.dma_start(ctx[n % 2][:], io["ctxT"][:, n * CHUNK:(n + 1) * CHUNK]).then_inc(ctx_in[n % 2], 16)

            @block.tensor
            def _(pe):
                pe.wait_ge(w_in, 16 * n_w)
                for n in range(n_q + n_k):
                    if n >= 2:
                        pe.wait_ge(biased, n - 1)
                    if n < n_q:
                        pe.matmul(psY[n % 2][:], wq[:], res.xnT[:, n * CHUNK:(n + 1) * CHUNK], start=True, stop=True).then_inc(projected, 1)
                    else:
                        m = n - n_q
                        pe.wait_ge(ctx_in[m % 2], 16 * (m // 2 + 1))
                        pe.matmul(psY[n % 2][:], wk[:], ctx[m % 2][:], start=True, stop=True).then_inc(projected, 1)
                if cfg.q_bias:
                    pe.matmul(psB[:], bv[:], wo[:], start=True, stop=True).then_inc(bias_made, 1)

            @block.scalar
            def _(act):
                if cfg.q_bias:
                    act.wait_ge(bias_scaled, 1)
                for n in range(n_q + n_k):
                    act.wait_ge(projected, n + 1)
                    if n >= 2:
                        act.wait_ge(split, 4 * (n - 1))
                    is_q = n < n_q
                    bias = (bqs if is_q else bk)[:] if cfg.q_bias else 0.0
                    act.activation(y[n % 2][:], psY[n % 2][:], ACT.Identity, bias=bias, scale=cfg.scale if is_q else 1.0).then_inc(biased, 1)

            @block.vector
            def _(dve):
                dve.wait_ge(w_in, 16 * n_w)
                if cfg.q_bias:
                    dve.tensor_scalar(bqs[:], bq[:], cfg.scale, None, ALU.mult).then_inc(bias_scaled, 1)
                for n in range(n_q + n_k):
                    dve.wait_ge(biased, n + 1)
                    if n >= 2:
                        dve.wait_ge(stored[n % 2], 32 * (n // 2) if n - 2 < n_q else 32 * (n_q // 2) + 16 * ((n - n_q) // 2))
                    p0, p1, p2 = (parts[n % 2][:, k, :] for k in range(3))
                    dve.tensor_copy(p0, y[n % 2][:]).then_inc(split, 1)
                    dve.wait_ge(split, 4 * n + 1)
                    dve.tensor_tensor(rest[:], y[n % 2][:], p0, ALU.subtract).then_inc(split, 1)
                    dve.wait_ge(split, 4 * n + 2)
                    dve.tensor_copy(p1, rest[:]).then_inc(split, 1)
                    dve.wait_ge(split, 4 * n + 3)
                    dve.tensor_tensor(p2, rest[:], p1, ALU.subtract).then_inc(split, 1)
                if cfg.slopes:
                    p0, p1, p2 = (pos_parts[:, k, :] for k in range(3))
                    dve.tensor_copy(posf[:], pos[:]).then_inc(pos_split, 1)
                    dve.wait_ge(pos_split, 1)
                    dve.tensor_copy(p0, posf[:]).then_inc(pos_split, 1)
                    dve.wait_ge(pos_split, 2)
                    dve.tensor_tensor(posr[:], posf[:], p0, ALU.subtract).then_inc(pos_split, 1)
                    dve.wait_ge(pos_split, 3)
                    dve.tensor_copy(p1, posr[:]).then_inc(pos_split, 1)
                    dve.wait_ge(pos_split, 4)
                    dve.tensor_tensor(p2, posr[:], p1, ALU.subtract).then_inc(pos_split, 1)
                if cfg.q_bias:
                    dve.wait_ge(bias_made, 1)
                    dve.tensor_tensor(bias_row[:], psB[:], bo[:], ALU.add).then_inc(row_done, 1)
                    dve.wait_ge(row_done, 1)

            @block.gpsimd
            def _(pool):
                for n in range(n_q + n_k):
                    pool.wait_ge(split, 4 * n + 4)
                    if n < n_q:
                        for b in range(2):
                            pool.dma_start(qs[2 * n + b].rearrange("c f q -> f c q"), parts[n % 2][:, :, b * S:(b + 1) * S]).then_inc(stored[n % 2], 16)
                    else:
                        pool.dma_start(ks[n - n_q].rearrange("c f k -> f c k"), parts[n % 2][:]).then_inc(stored[n % 2], 16)
                n_stored = 32 * (n_q // 2) + 16 * (n_k // 2)
                if cfg.slopes:
                    pool.wait_ge(pos_split, 5)
                    pool.dma_start(ps_scr, pos_parts[:]).then_inc(stored[0], 16)
                pool.wait_ge(stored[0], n_stored + 16 * cfg.slopes)
                pool.wait_ge(stored[1], n_stored)


def narrow_attention(nc, io, res, cfg):
    rows = COMBO_ROWS + (9 if cfg.slopes else 0)
    with Phase(nc, cfg.name) as ph:
        qs = nc.dram_tensor(cfg.name + "_qs", [B, 3, D, S], BF16).ap()
        ks = nc.dram_tensor(cfg.name + "_ks", [B, 3, D, S2], BF16).ap()
        pos_scr = nc.dram_tensor(cfg.name + "_pos", [B, 3, S2], BF16).ap()
        max_scr = nc.dram_tensor(cfg.name + "_max", [RING, 3, HEADS * QT, P], BF16).ap()
        wo = ph.sb("wo", [P, D])
        wv = ph.sb("wv", [P, D])
        bias_row = ph.sb("bias_row", [1, D])
        split_and_store(nc, io, res, cfg, qs, ks, pos_scr, bias_row, wo)

        k_op = [ph.sb(f"k_op{i}", [P, PAIRS, S2], BF16) for i in range(RING)]
        q_op = [ph.sb(f"q_op{i}", [P, HEADS, S], BF16) for i in range(RING)]
        cT = [ph.sb(f"cT{i}", [P, S2]) for i in range(RING)]
        values = [ph.sb(f"values{i}", [P, KT, HEADS, V_COLS]) for i in range(RING)]
        madd = [ph.sb(f"madd{i}", [P, QT, S2], BF16) for i in range(RING)]
        maddT = [ph.sb(f"maddT{i}", [P, KT, S], BF16) for i in range(RING)]
        mx = [ph.sb(f"mx{i}", [P, HEADS * QT]) for i in range(RING)]
        max_rest = ph.sb("max_rest", [HEADS * QT, P])
        max_parts = ph.sb("max_parts", [HEADS * QT, 3, P], BF16)
        probs = [ph.sb(f"probs{i}", [P, KT, S]) for i in range(4)]
        OT = ph.sb("OT", [P, 2, S])
        den, rec = ph.sb("den", [P, 4, 4, 2]), ph.sb("rec", [P, 4, 4, 2])
        A = ph.sb("A", [P, QT, D])
        AT = ph.sb("AT", [P, S])
        junk = [ph.sb(f"junk{i}", [P, S2], BF16) for i in range(2)]
        carrier = [ph.sb(f"carrier{i}", [P, 1]) for i in range(2)]
        if cfg.slopes:
            mask_i = [ph.sb(f"mask{i}", [P, QT, S2], I32) for i in range(RING)]
            maskT_i = [ph.sb(f"maskT{i}", [P, KT, S], I32) for i in range(RING)]
        else:
            tri, triT = ph.sb("tri", [P, QT, S2], BF16), ph.sb("triT", [P, KT, S], BF16)
            padT = ph.sb("padT", [P, B, KT])
            padT_now = [ph.sb(f"padT_now{i}", [P, KT]) for i in range(RING)]
            pad = ph.sb("pad", [P, B, S2], BF16)

        psM = [ph.ps(f"psM{i}", [P, S2]) for i in range(2)]
        psE = [ph.ps(f"psE{i}", [P, KT, S]) for i in range(2)]
        psO = ph.ps("psO", [P, 2, S])
        psX = ph.ps("psX", [P, CHUNK])

        with Phase(nc, cfg.name + "c") as pc:
            const_in, const_done, static_done = pc.sem("const_in"), pc.sem("const_done"), pc.sem("static_done")
            if cfg.slopes:
                slopes = pc.sb("slopes", [P, HEADS, S])
            else:
                tri_i, triT_i, padT_i = pc.sb("tri_i", [P, QT, S2], U8), pc.sb("triT_i", [P, KT, S], U8), pc.sb("padT_i", [P, B, KT], U8)
                pad_i = pc.sb("pad_i", [P, B, S2], U8)
            with pc.block() as block:
                @block.sync
                def _(sp):
                    sp.dma_start(wv[:], io[cfg.weights + "_WvT"]).then_inc(const_in, 16)
                    if cfg.slopes:
                        sp.dma_start(slopes[COMBO_ROWS:COMBO_ROWS + 9], io["c_slopes"]).then_inc(const_in, 16)
                    else:
                        sp.dma_start(tri_i[:], io["tri"].rearrange("(t p) k -> p t k", p=P)).then_inc(const_in, 16)
                        sp.dma_start(triT_i[:], io["triT"].rearrange("(t p) q -> p t q", p=P)).then_inc(const_in, 16)
                        sp.dma_start(padT_i[:], io["padT"]).then_inc(const_in, 16)
                        sp.dma_start(pad_i[:].rearrange("p b k -> p (b k)"), io["pad"].partition_broadcast(P)).then_inc(const_in, 16)
                    sp.wait_ge(const_in, 32 if cfg.slopes else 80)

                @block.gpsimd
                def _(pool):
                    for r in range(RING):
                        pool.memset(k_op[r][:], 1.0).then_inc(static_done, 1)
                        pool.memset(values[r][:], 0.0).then_inc(static_done, 1)

                @block.vector
                def _(dve):
                    for r in range(RING):
                        dve.memset(q_op[r][:], 0.0).then_inc(const_done, 1)
                    dve.wait_ge(const_in, 32 if cfg.slopes else 80)
                    dve.wait_ge(const_done, RING)
                    dve.wait_ge(static_done, 2 * RING)
                    for r in range(RING):
                        if cfg.slopes:
                            dve.tensor_copy(q_op[r][COMBO_ROWS:COMBO_ROWS + 9], slopes[COMBO_ROWS:COMBO_ROWS + 9]).then_inc(const_done, 1)
                        for s in range(2):
                            heads = values[r][:].rearrange("p k (g s j) m -> p (k g) s j m", g=2, s=2)[:, :, s, :, s * SLOT + HEAD_E]
                            dve.memset(heads, 1.0).then_inc(const_done, 1)
                    if not cfg.slopes:
                        dve.tensor_scalar(tri[:], tri_i[:], BIG, None, ALU.mult).then_inc(const_done, 1)
                        dve.tensor_scalar(triT[:], triT_i[:], BIG, None, ALU.mult).then_inc(const_done, 1)
                        dve.tensor_copy(padT[:], padT_i[:]).then_inc(const_done, 1)
                        dve.tensor_copy(pad[:], pad_i[:]).then_inc(const_done, 1)
                    dve.wait_ge(const_done, 4 * RING if cfg.slopes else 3 * RING + 4)

        n_loads = 2 * len(COMBOS) + len(COMBOS) + 1 + (3 + 2 if cfg.slopes else 0)
        loaded = [ph.sem(f"loaded{i}") for i in range(RING)]
        masked = ph.sem("masked")
        max_scored, max_read = ph.sem("max_scored"), ph.sem("max_read")
        max_turned, max_split = ph.sem("max_turned"), ph.sem("max_split")
        max_stored, max_in = ph.sem("max_stored"), [ph.sem(f"max_in{i}") for i in range(RING)]
        v_made, v_out = ph.sem("v_made"), ph.sem("v_out")
        scored, exped, weighted = ph.sem("scored"), ph.sem("exped"), ph.sem("weighted")
        out_read, out_turned, den_done, rec_done, normed = (ph.sem(n) for n in ("out_read", "out_turned", "den_done", "rec_done", "normed"))
        back_turned, back_copied, projected, added = (ph.sem(n) for n in ("back_turned", "back_copied", "projected", "added"))
        pad_taken, pad_mixed = ph.sem("pad_taken"), ph.sem("pad_mixed")

        max_slots = [[h for h in range(4 * s // 3, 4 * (s + 1) // 3) if h < HEADS] for s in range(HEADS)]
        OUT_SLOT, BACK_SLOT, PROJECT_SLOT, MAX_SLOT, V_SLOT = 1, 4, 7, 12, 13

        def steps(eng, step):
            step(0, 0, 0)
            step(1, 1, 0)
            with eng.Fori(0, (B - 2) // RING) as i:
                for k in range(RING):
                    step(RING * i + 2 + k, (2 + k) % RING, i + (2 + k) // RING, inner=True)
            step(B, B % RING, 0)

        with ph.block() as block:
            @block.sync
            def _(sp):
                def load(u, r):
                    one = bass.ds(u, 1)
                    for c, (cq, ck) in enumerate(COMBOS):
                        rows_c = slice(c * PAIR_ROWS, (c + 1) * PAIR_ROWS)
                        sp.dma_start(k_op[r][rows_c], ks[one, ck].rearrange("o (t r) k -> (o r) t k", r=PAIR_ROWS)).then_inc(loaded[r], 16)
                        for j in range(2):
                            rows_j = slice(c * PAIR_ROWS + j * HEAD_E, c * PAIR_ROWS + (j + 1) * HEAD_E)
                            sp.dma_start(q_op[r][rows_j, j::2, :],
                                         qs[one, cq].rearrange("o (t j e) q -> j (o e) t q", j=2, e=HEAD_E)[j]).then_inc(loaded[r], 16)
                    sp.dma_start(cT[r][:], io["ctxT"][:, bass.ds(u * S2, S2)]).then_inc(loaded[r], 16)
                    if cfg.slopes:
                        for a in range(3):
                            at = COMBO_ROWS + 3 * a
                            sp.dma_start(k_op[r][at:at + 3], pos_scr[one].rearrange("o c k -> (o c) k").unsqueeze(1).to_broadcast([3, PAIRS, S2])).then_inc(loaded[r], 16)
                        sp.dma_start(mask_i[r][:], io["mask"][one].rearrange("o (t p) k -> p (o t) k", p=P)).then_inc(loaded[r], 16)
                        sp.dma_start(maskT_i[r][:], io["maskT"][one].rearrange("o (t p) q -> p (o t) q", p=P)).then_inc(loaded[r], 16)

                def maxima(v, r):
                    sp.wait_ge(max_split, v * 4 + 4)
                    sp.dma_start(max_scr[r].rearrange("c n q -> n c q"), max_parts[:]).then_inc(max_stored, 16)
                    sp.wait_ge(max_stored, v * 16 + 16)
                    sp.dma_start(q_op[r][rows:rows + 3].rearrange("c h q -> c (h q)"),
                                 max_scr[r].rearrange("c n q -> c (n q)")).then_inc(max_in[r], 16)

                load(0, 0)
                load(1, 1)
                maxima(0, 0)
                with sp.Fori(0, (B - 2) // RING) as i:
                    for k in range(RING):
                        v, r = RING * i + 2 + k, (2 + k) % RING
                        sp.wait_ge(weighted, (v - 2) * HEADS + 1)
                        load(v, r)
                        maxima(v - 1, (r - 1) % RING)
                maxima(B - 1, (B - 1) % RING)

            @block.gpsimd
            def _(pool):
                def masks(u, r, turn, first):
                    pool.wait_ge(loaded[r], 16 * n_loads * (turn + 1))
                    if not first:
                        pool.wait_ge(weighted, (u - RING + 1) * HEADS)
                    if cfg.slopes:
                        pool.tensor_scalar(madd[r][:], mask_i[r][:], 0.0, -BIG, ALU.is_equal, ALU.mult).then_inc(masked, 1)
                        pool.tensor_scalar(maddT[r][:], maskT_i[r][:], 0.0, -BIG, ALU.is_equal, ALU.mult).then_inc(masked, 1)
                    else:
                        pool.tensor_copy(padT_now[r][:], padT[:, bass.ds(u, 1), :].rearrange("p o k -> p (o k)")).then_inc(pad_taken, 1)
                        pool.tensor_tensor(madd[r][:], tri[:], pad[:, bass.ds(u, 1), :].to_broadcast([P, QT, S2]), ALU.mult).then_inc(pad_mixed, 1)
                        pool.wait_ge(pad_mixed, u + 1)
                        pool.tensor_scalar(madd[r][:], madd[r][:], BIG, None, ALU.subtract).then_inc(masked, 1)
                        pool.wait_ge(pad_taken, u + 1)
                        for t in range(KT):
                            last = pool.tensor_scalar(maddT[r][:, t, :], triT[:, t, :], padT_now[r][:, t:t + 1], BIG, ALU.mult, ALU.subtract)
                        last.then_inc(masked, 1)

                for u in range(RING):
                    masks(u, u, 0, True)
                with pool.Fori(1, 2) as i:
                    for r in range(RING):
                        masks(RING * i + r, r, i, False)
                for u in range(2 * RING, B):
                    masks(u, u % RING, u // RING, False)

            @block.tensor
            def _(pe):
                def turn_out(u):
                    pe.wait_ge(out_read, u + 1)
                    for t in range(QT):
                        for g in range(2):
                            n = t * 2 + g
                            last = pe.transpose(psX[:, n * P:(n + 1) * P], OT[:, g, t * P:(t + 1) * P], res.ident[:])
                    last.then_inc(out_turned, 1)

                def turn_back(u):
                    pe.wait_ge(normed, 2 * u + 2)
                    for t in range(QT):
                        last = pe.transpose(psX[:, t * P:(t + 1) * P], A[:, t, :], res.ident[:])
                    last.then_inc(back_turned, 1)

                def project(u):
                    pe.wait_ge(back_copied, u + 1)
                    for t in range(QT):
                        y = psX[:, t * P:(t + 1) * P]
                        if cfg.q_bias:
                            pe.matmul(y, res.ones[0:1, :], bias_row[:], start=True, stop=False)
                        last = pe.matmul(y, AT[:, t * P:(t + 1) * P], wo[:], start=not cfg.q_bias, stop=True)
                    last.then_inc(projected, 1)

                def maximum(v, r, h, first):
                    for t in range(QT):
                        n = QT * h + t
                        if not (first and n < 2):
                            pe.wait_ge(max_read, v * HEADS * QT + n - 1)
                        pe.matmul(psM[t][:], q_op[r][0:rows, h, t * P:(t + 1) * P], k_op[r][0:rows, h // 2, :],
                                  start=True, stop=True).then_inc(max_scored, 1)

                def score(w, r, h, first):
                    if not (first and h < 2):
                        pe.wait_ge(exped, w * HEADS + h - 1)
                    for t in range(KT):
                        out = psE[h % 2][:, t, :]
                        pe.matmul(out, k_op[r][0:rows + 3, h // 2, t * P:(t + 1) * P], q_op[r][0:rows + 3, h, :], start=True, stop=False)
                        last = pe.matmul(out, res.identb[:], maddT[r][:, t, :], start=False, stop=True)
                    last.then_inc(scored, 1)

                def weigh(w, r, h, first):
                    pe.wait_ge(exped, w * HEADS + h + 1)
                    if h == 0 and not first:
                        pe.wait_ge(out_read, w)
                    g, s, j = h // 8, h % 8 // 4, h % 4
                    for t in range(KT):
                        last = pe.matmul(psO[32 * j:32 * j + 32, g, :], values[r][:, t, h, :], probs[h % 4][:, t, :],
                                         start=(s == 0 and t == 0), stop=(s == 1 and t == KT - 1),
                                         tile_position=(0, 32 * j), skip_group_check=True)
                    last.then_inc(weighted, 1)

                def step(v, r, turn, inner=False):
                    take_max, take_exp, finish = inner or v < B, inner or v >= 1, inner or v >= 2
                    before = (r - 1) % RING
                    if take_max:
                        pe.wait_ge(loaded[r], 16 * n_loads * (turn + 1))
                    if take_exp:
                        turn_before = turn - (r == 0) if inner else (v - 1) // RING
                        pe.wait_ge(max_in[before], 16 * (turn_before + 1))
                        pe.wait_ge(masked, v * 2)
                        pe.wait_ge(v_out, 2 * v)
                    for s in range(HEADS):
                        if take_max:
                            for h in max_slots[s]:
                                maximum(v, r, h, not inner and v == 0)
                        if take_exp:
                            score(v - 1, before, s, not inner and v == 1)
                            if s:
                                weigh(v - 1, before, s - 1, not inner and v == 1)
                        if finish:
                            if s == OUT_SLOT:
                                pe.wait_ge(v_out, 2 * v)
                                turn_out(v - 2)
                            if s == BACK_SLOT:
                                turn_back(v - 2)
                            if s == PROJECT_SLOT:
                                project(v - 2)
                        if take_max:
                            if s == MAX_SLOT:
                                pe.wait_ge(max_read, (v + 1) * HEADS * QT)
                                if finish:
                                    pe.wait_ge(added, v - 1)
                                elif inner or v >= 1:
                                    pe.wait_ge(v_out, 2 * v)
                                pe.transpose(psX[0:HEADS * QT, 0:P], mx[r][:], res.ident[:]).then_inc(max_turned, 1)
                            if s == V_SLOT:
                                pe.wait_ge(max_split, 4 * v + 4)
                                for t in range(KT):
                                    last = pe.matmul(psX[:, t * P:(t + 1) * P], cT[r][:, t * P:(t + 1) * P], wv[:], start=True, stop=True)
                                last.then_inc(v_made, 1)
                    if take_exp:
                        weigh(v - 1, before, HEADS - 1, not inner and v == 1)

                steps(pe, step)
                pe.wait_ge(added, B - 1)
                turn_out(B - 1)
                turn_back(B - 1)
                project(B - 1)

            @block.scalar
            def _(act):
                def heads(w, first):
                    for h in range(HEADS):
                        act.wait_ge(scored, w * HEADS + h + 1)
                        if not (first and h < 4):
                            act.wait_ge(weighted, w * HEADS + h - 3)
                        act.activation(probs[h % 4][:], psE[h % 2][:], ACT.Exp).then_inc(exped, 1)

                heads(0, True)
                with act.Fori(1, B) as w:
                    heads(w, False)

            @block.vector
            def _(dve):
                def normalise(u):
                    dve.wait_ge(out_turned, u + 1)
                    turned = psX[:].rearrange("p (n j m) -> p n j m", n=4, j=4)
                    dve.tensor_scalar(den[:], turned[:, :, :, HEAD_E:2 * SLOT:SLOT], cfg.sink, None, ALU.add).then_inc(den_done, 1)
                    dve.wait_ge(den_done, u + 1)
                    dve.reciprocal(rec[:], den[:]).then_inc(rec_done, 1)
                    dve.wait_ge(rec_done, u + 1)
                    for s in range(2):
                        dve.tensor_tensor(A[:].rearrange("p t (g s j c) -> p (t g) s j c", g=2, s=2, j=4)[:, :, s],
                                          turned[:, :, :, s * SLOT:s * SLOT + HEAD_E],
                                          rec[:, :, :, s:s + 1].to_broadcast([P, 4, 4, HEAD_E]), ALU.mult).then_inc(normed, 1)

                def copy_back(u):
                    dve.wait_ge(back_turned, u + 1)
                    dve.tensor_copy(AT[:], psX[:, 0:S]).then_inc(back_copied, 1)

                def add(u):
                    dve.wait_ge(projected, u + 1)
                    x = res.X[:, bass.ds(u * QT, QT), :].rearrange("p t d -> p (t d)")
                    dve.scalar_tensor_tensor(x, psX[:, 0:S], res.gates[:, cfg.gate:cfg.gate + 1], x, ALU.mult, ALU.add).then_inc(added, 1)

                def maximum(v, r, h):
                    for t in range(QT):
                        n = QT * h + t
                        dve.wait_ge(max_scored, v * HEADS * QT + n + 1)
                        dve.memset(carrier[t][:], 0.0)
                        dve.tensor_tensor_reduce(junk[t][:], psM[t][:], madd[r][:, t, :], 1.0, -3.0e38, ALU.add, ALU.max,
                                                 mx[r][:, n:n + 1]).then_inc(max_read, 1)

                def split_max(v):
                    dve.wait_ge(max_turned, v + 1)
                    m = psX[0:HEADS * QT, 0:P]
                    dve.tensor_scalar(max_parts[:, 0, :], m, -1.0, None, ALU.mult).then_inc(max_split, 1)
                    dve.wait_ge(max_split, 4 * v + 1)
                    dve.scalar_tensor_tensor(max_rest[:], m, -1.0, max_parts[:, 0, :], ALU.mult, ALU.subtract).then_inc(max_split, 1)
                    dve.wait_ge(max_split, 4 * v + 2)
                    dve.tensor_copy(max_parts[:, 1, :], max_rest[:]).then_inc(max_split, 1)
                    dve.wait_ge(max_split, 4 * v + 3)
                    dve.tensor_tensor(max_parts[:, 2, :], max_rest[:], max_parts[:, 1, :], ALU.subtract).then_inc(max_split, 1)

                def copy_values(v, r):
                    dve.wait_ge(v_made, v + 1)
                    for s in range(2):
                        dve.tensor_copy(values[r][:].rearrange("p k (g s j) m -> p (k g) s j m", g=2, s=2)[:, :, s, :, s * SLOT:s * SLOT + HEAD_E],
                                        psX[:].rearrange("p (n s j c) -> p n s j c", s=2, j=4, c=HEAD_E)[:, :, s]).then_inc(v_out, 1)

                def step(v, r, turn, inner=False):
                    take_max, take_exp, finish = inner or v < B, inner or v >= 1, inner or v >= 2
                    if take_max:
                        dve.wait_ge(masked, 2 * v + 2)
                        if inner or v >= 1:
                            dve.wait_ge(max_stored, 16 * v)
                    for s in range(HEADS):
                        if take_max:
                            for h in max_slots[s]:
                                maximum(v, r, h)
                        if finish:
                            if s == OUT_SLOT:
                                normalise(v - 2)
                            if s == BACK_SLOT:
                                copy_back(v - 2)
                            if s == PROJECT_SLOT:
                                add(v - 2)
                        if take_max:
                            if s == MAX_SLOT:
                                split_max(v)
                            if s == V_SLOT:
                                copy_values(v, r)
                    if take_exp:
                        dve.wait_ge(weighted, v * HEADS)
                        dve.tensor_copy(OT[:], psO[:]).then_inc(out_read, 1)

                steps(dve, step)
                normalise(B - 1)
                copy_back(B - 1)
                add(B - 1)
                dve.wait_ge(added, B)



WIDE_E = 64
WIDE_V = HEADS * WIDE_E
W_PAIRS = HEADS // 2
VC = WIDE_V // CHUNK


def fold_weights(nc, io, res, G, q_bias, wv, wo, bias_row):
    scale = 1.0 / 8.0
    with Phase(nc, "a1p") as ph:
        wq, wk = ph.sb("wq", [WIDE_E, HEADS, D]), ph.sb("wk", [WIDE_E, HEADS, D])
        bq = ph.sb("bq", [WIDE_E, HEADS])
        bv = ph.sb("bv", [P, W_PAIRS])
        bp = ph.sb("bp", [1, D])
        psG = [ph.ps(f"psG{i}", [P, 4, D]) for i in range(2)]
        psB = ph.ps("psB", [P, HEADS])
        psR = ph.ps("psR", [1, D])
        w_in, folded, copied, bias_made, bias_done = (ph.sem(n) for n in ("w_in", "folded", "copied", "bias_made", "bias_done"))
        with ph.block() as block:
            @block.sync
            def _(sp):
                sp.dma_start(wq[:], io["L1_wq"].rearrange("n e d -> e n d")).then_inc(w_in, 16)
                sp.dma_start(wk[:], io["L1_wk"].rearrange("n e d -> e n d")).then_inc(w_in, 16)
                sp.dma_start(bq[:], io["L1_bq"]).then_inc(w_in, 16)
                sp.dma_start(bv[:], io["L1_bv"]).then_inc(w_in, 16)
                sp.dma_start(bp[:], io["L1_bp"]).then_inc(w_in, 16)
                sp.dma_start(wv[:], io["L1_wv"]).then_inc(w_in, 16)
                sp.dma_start(wo[:], io["L1_wo"].rearrange("(c p) d -> p c d", p=P)).then_inc(w_in, 16)

            @block.tensor
            def _(pe):
                pe.wait_ge(w_in, 16 * 7)
                for n in range(HEADS):
                    if n % 4 == 0 and n >= 8:
                        pe.wait_ge(copied, n // 4 - 1)
                    last = pe.matmul(psG[n // 4 % 2][:, n % 4, :], wq[:, n, :], wk[:, n, :], start=True, stop=True)
                    if n % 4 == 3:
                        last.then_inc(folded, 1)
                for n in range(HEADS):
                    pe.matmul(psB[:, n:n + 1], wk[:, n, :], bq[:, n:n + 1], start=True, stop=True)
                for p in range(W_PAIRS):
                    last = pe.matmul(psR[:], bv[:, p:p + 1], wo[:, p, :], start=(p == 0), stop=(p == W_PAIRS - 1))
                last.then_inc(bias_made, 1)

            @block.vector
            def _(dve):
                for c in range(HEADS // 4):
                    dve.wait_ge(folded, c + 1)
                    dve.tensor_scalar(G[:, 4 * c:4 * c + 4, :], psG[c % 2][:], scale, None, ALU.mult).then_inc(copied, 1)
                dve.wait_ge(bias_made, 1)
                dve.tensor_scalar(q_bias[:], psB[:], scale, None, ALU.mult).then_inc(bias_done, 1)
                dve.tensor_tensor(bias_row[:], psR[:], bp[:], ALU.add).then_inc(bias_done, 1)
                dve.wait_ge(bias_done, 2)


def layer1_attention(nc, io, res):
    halves = 2
    with Phase(nc, "a1") as ph:
        max_scr = nc.dram_tensor("a1_max", [RING, HEADS * QT, P], BF16).ap()
        G = ph.sb("G", [P, HEADS, D])
        q_bias = ph.sb("q_bias", [P, HEADS])
        wv = ph.sb("wv", [P, WIDE_V])
        wo = ph.sb("wo", [P, W_PAIRS, D])
        bias_row = ph.sb("bias_row", [1, D])
        fold_weights(nc, io, res, G, q_bias, wv, wo, bias_row)

        cT = [ph.sb(f"cT{i}", [P, S2]) for i in range(RING)]
        cTb = [ph.sb(f"cTb{i}", [P, S2], BF16) for i in range(RING)]
        q_op = [ph.sb(f"q_op{i}", [P, HEADS, S]) for i in range(RING)]
        q_b = [ph.sb(f"q_b{i}", [P, S], BF16) for i in range(4)]
        values = [ph.sb(f"values{i}", [P, KT, WIDE_V]) for i in range(RING)]
        max_row = [ph.sb(f"max_row{i}", [P, HEADS * S], BF16) for i in range(RING)]
        mx = [ph.sb(f"mx{i}", [P, HEADS * QT]) for i in range(RING)]
        max_b = ph.sb("max_b", [HEADS * QT, P], BF16)
        probs = [ph.sb(f"probs{i}", [P, KT, S]) for i in range(4)]
        rec = ph.sb("rec", [P, S])
        OT = ph.sb("OT", [P, W_PAIRS, S])

        psM = [ph.ps(f"psM{i}", [P, S2]) for i in range(2)]
        psE = [ph.ps(f"psE{i}", [P, 2, S]) for i in range(halves)]
        psO = ph.ps("psO", [P, 2, S])
        psQ = [ph.ps(f"psQ{i}", [P, CHUNK]) for i in range(2)]
        psY = ph.ps("psY", [P, CHUNK])

        loaded = [ph.sem(f"loaded{i}") for i in range(RING)]
        cast, zeroed, q_cast = ph.sem("cast"), ph.sem("zeroed"), ph.sem("q_cast")
        q_made, q_out = ph.sem("q_made"), ph.sem("q_out")
        max_scored, max_read = ph.sem("max_scored"), ph.sem("max_read")
        max_turned, max_cast, max_stored = ph.sem("max_turned"), ph.sem("max_cast"), ph.sem("max_stored")
        max_in = [ph.sem(f"max_in{i}") for i in range(RING)]
        v_made, v_out = ph.sem("v_made"), ph.sem("v_out")
        scored, exped, weighted = ph.sem("scored"), ph.sem("exped"), ph.sem("weighted")
        inverted, normed = ph.sem("inverted"), ph.sem("normed")
        projected, added = ph.sem("projected"), ph.sem("added")
        n_v = KT * VC

        max_slots = [[h for h in range(4 * s // 3, 4 * (s + 1) // 3) if h < HEADS] for s in range(HEADS)]
        OUT_SLOT, V_SLOT, MAX_SLOT = 0, 1, 12

        def steps(eng, step):
            step(0, 0, 0)
            step(1, 1, 0)
            with eng.Fori(0, (B - 2) // RING) as i:
                for k in range(RING):
                    step(RING * i + 2 + k, (2 + k) % RING, i + (2 + k) // RING, inner=True)
            step(B, B % RING, B // RING)

        with ph.block() as block:
            @block.sync
            def _(sp):
                def load(u, r):
                    sp.dma_start(cT[r][:], io["ctxT"][:, bass.ds(u * S2, S2)]).then_inc(loaded[r], 16)

                def maxima(v, r):
                    sp.wait_ge(max_cast, v + 1)
                    sp.dma_start(max_scr[r], max_b[:]).then_inc(max_stored, 16)
                    sp.wait_ge(max_stored, v * 16 + 16)
                    sp.dma_start(max_row[r][0:1, :], max_scr[r].rearrange("n q -> (n q)").unsqueeze(0)).then_inc(max_in[r], 16)

                load(0, 0)
                load(1, 1)
                sp.wait_ge(zeroed, RING)
                maxima(0, 0)
                with sp.Fori(0, (B - 2) // RING) as i:
                    for k in range(RING):
                        v, r = RING * i + 2 + k, (2 + k) % RING
                        sp.wait_ge(weighted, (v - 2) * HEADS + 1)
                        load(v, r)
                        maxima(v - 1, (r - 1) % RING)
                maxima(B - 1, (B - 1) % RING)

            @block.gpsimd
            def _(pool):
                for r in range(RING):
                    pool.memset(max_row[r][:], 0.0).then_inc(zeroed, 1)

            @block.tensor
            def _(pe):
                def query(v, r, h, first):
                    if not (first and h < 2):
                        pe.wait_ge(q_cast, v * HEADS + h - 1)
                    pe.matmul(psQ[h % 2][:, 0:S], G[:, h, :], res.xnT[:, bass.ds(v * S, S)], start=True, stop=True).then_inc(q_made, 1)

                def maximum(v, r, h, first):
                    pe.wait_ge(q_cast, v * HEADS + h + 1)
                    for t in range(QT):
                        n = QT * h + t
                        if not (first and n < 2):
                            pe.wait_ge(max_read, v * HEADS * QT + n - 1)
                        pe.matmul(psM[t][:], q_b[h % 4][:, t * P:(t + 1) * P], cTb[r][:], start=True, stop=True).then_inc(max_scored, 1)

                def score(w, r, h, first):
                    for half in range(halves):
                        if not (first and h == 0):
                            pe.wait_ge(exped, (w * HEADS + h - 1) * halves + half + 1)
                        for t in range(2):
                            out, k = psE[half][:, t, :], (2 * half + t) * P
                            pe.matmul(out, cT[r][:, k:k + P], q_op[r][:, h, :], start=True, stop=False)
                            last = pe.matmul(out, res.onesb[:], max_row[r][:, h * S:(h + 1) * S], start=False, stop=True)
                        last.then_inc(scored, 1)

                def weigh(w, r, h, first):
                    pe.wait_ge(exped, (w * HEADS + h + 1) * halves)
                    pair, i = h // 2, h % 2
                    if i == 0 and not (first and h == 0):
                        pe.wait_ge(normed, w * W_PAIRS + pair)
                    rows = slice(i * WIDE_E, (i + 1) * WIDE_E)
                    for t in range(KT):
                        pe.matmul(psO[rows, 0, :], values[r][:, t, h * WIDE_E:(h + 1) * WIDE_E], probs[h % 4][:, t, :],
                                  start=(t == 0), stop=False, tile_position=(0, i * WIDE_E), skip_group_check=True)
                    for t in range(KT):
                        last = pe.matmul(psO[rows, 1, :], res.ones[:, 0:WIDE_E], probs[h % 4][:, t, :],
                                         start=False, stop=(t == KT - 1), tile_position=(0, i * WIDE_E), skip_group_check=True)
                    last.then_inc(weighted, 1)

                def project(u):
                    pe.wait_ge(normed, (u + 1) * W_PAIRS)
                    for t in range(QT):
                        y = psY[:, t * P:(t + 1) * P]
                        pe.matmul(y, res.ones[0:1, :], bias_row[:], start=True, stop=False)
                        for p in range(W_PAIRS):
                            last = pe.matmul(y, OT[:, p, t * P:(t + 1) * P], wo[:, p, :], start=False, stop=(p == W_PAIRS - 1))
                    last.then_inc(projected, 1)

                def value(v, r, n, wait):
                    if n > 0:
                        pe.wait_ge(v_out, v * n_v + n)
                    t, c = n // VC, n % VC
                    pe.matmul(psY[:], cT[r][:, t * P:(t + 1) * P], wv[:, c * CHUNK:(c + 1) * CHUNK], start=True, stop=True).then_inc(v_made, 1)

                def step(v, r, turn, inner=False):
                    take_max, take_exp, finish = inner or v < B, inner or v >= 1, inner or v >= 2
                    first, before = not inner and v == 0, (r - 1) % RING
                    if take_max:
                        pe.wait_ge(loaded[r], 16 * (turn + 1))
                        query(v, r, 0, first)
                        query(v, r, 1, first)
                    if take_exp:
                        turn_before = turn - (r == 0) if inner else (v - 1) // RING
                        pe.wait_ge(q_out, v * HEADS)
                        pe.wait_ge(max_in[before], 16 * (turn_before + 1))
                        pe.wait_ge(v_out, v * n_v)
                    for s in range(HEADS):
                        if finish and s == OUT_SLOT:
                            pe.wait_ge(max_cast, v)
                            project(v - 2)
                        if take_max:
                            if V_SLOT <= s < V_SLOT + n_v:
                                if s == V_SLOT:
                                    if finish:
                                        pe.wait_ge(added, v - 1)
                                    elif not first:
                                        pe.wait_ge(max_cast, v)
                                value(v, r, s - V_SLOT, first)
                            for h in max_slots[s]:
                                if h + 2 < HEADS:
                                    query(v, r, h + 2, first)
                                if h == 0:
                                    pe.wait_ge(cast, v + 1)
                                maximum(v, r, h, first)
                        if take_exp:
                            score(v - 1, before, s, not inner and v == 1)
                            if s:
                                weigh(v - 1, before, s - 1, not inner and v == 1)
                        if take_max and s == MAX_SLOT:
                            pe.wait_ge(max_read, (v + 1) * HEADS * QT)
                            pe.wait_ge(v_out, (v + 1) * n_v)
                            pe.transpose(psY[0:HEADS * QT, 0:P], mx[r][:], res.ident[:]).then_inc(max_turned, 1)
                    if take_exp:
                        weigh(v - 1, before, HEADS - 1, not inner and v == 1)

                steps(pe, step)
                project(B - 1)

            @block.scalar
            def _(act):
                def query(v, r, h, first):
                    act.wait_ge(q_made, v * HEADS + h + 1)
                    act.activation(q_op[r][:, h, :], psQ[h % 2][:, 0:S], ACT.Identity, bias=q_bias[:, h:h + 1]).then_inc(q_out, 1)
                    if not (first and h < 4):
                        act.wait_ge(max_scored, (v * HEADS + h - 3) * QT)
                    act.activation(q_b[h % 4][:], psQ[h % 2][:, 0:S], ACT.Identity, bias=q_bias[:, h:h + 1]).then_inc(q_cast, 1)

                def step(v, r, turn, inner=False):
                    take_max, take_exp = inner or v < B, inner or v >= 1
                    first = not inner and v == 0
                    if take_max:
                        query(v, r, 0, first)
                        query(v, r, 1, first)
                    for s in range(HEADS):
                        if take_max:
                            if V_SLOT <= s < V_SLOT + n_v:
                                n = s - V_SLOT
                                act.wait_ge(v_made, v * n_v + n + 1)
                                act.copy(values[r][:, n // VC, n % VC * CHUNK:(n % VC + 1) * CHUNK], psY[:]).then_inc(v_out, 1)
                            for h in max_slots[s]:
                                if h + 2 < HEADS:
                                    query(v, r, h + 2, first)
                        if take_exp:
                            w = v - 1
                            if not (not inner and v == 1 and s < 4):
                                act.wait_ge(weighted, w * HEADS + s - 3)
                            for half in range(halves):
                                act.wait_ge(scored, (w * HEADS + s) * halves + half + 1)
                                act.activation(probs[s % 4][:, 2 * half:2 * half + 2, :], psE[half][:], ACT.Exp).then_inc(exped, 1)

                steps(act, step)

            @block.vector
            def _(dve):
                def normalise(w, pair):
                    dve.wait_ge(weighted, w * HEADS + 2 * pair + 2)
                    dve.reciprocal(rec[:], psO[:, 1, :]).then_inc(inverted, 1)
                    dve.wait_ge(inverted, w * W_PAIRS + pair + 1)
                    dve.tensor_tensor(OT[:, pair, :], psO[:, 0, :], rec[:], ALU.mult).then_inc(normed, 1)

                def add(u):
                    dve.wait_ge(projected, u + 1)
                    x = res.X[:, bass.ds(u * QT, QT), :].rearrange("p t d -> p (t d)")
                    dve.scalar_tensor_tensor(x, psY[:, 0:S], res.gates[:, 1:2], x, ALU.mult, ALU.add).then_inc(added, 1)

                def step(v, r, turn, inner=False):
                    take_max, take_exp, finish = inner or v < B, inner or v >= 1, inner or v >= 2
                    if take_max:
                        dve.wait_ge(loaded[r], 16 * (turn + 1))
                        dve.tensor_copy(cTb[r][:], cT[r][:]).then_inc(cast, 1)
                    for s in range(HEADS):
                        if finish and s == OUT_SLOT:
                            add(v - 2)
                        if take_max:
                            for h in max_slots[s]:
                                for t in range(QT):
                                    n = QT * h + t
                                    dve.wait_ge(max_scored, v * HEADS * QT + n + 1)
                                    dve.tensor_reduce(mx[r][:, n:n + 1], psM[t][:], AX.X, ALU.max).then_inc(max_read, 1)
                        if take_exp and s >= 2 and s % 2 == 0:
                            normalise(v - 1, s // 2 - 1)
                        if take_max and s == MAX_SLOT:
                            dve.wait_ge(max_turned, v + 1)
                            if inner or v >= 1:
                                dve.wait_ge(max_stored, 16 * v)
                            dve.tensor_scalar(max_b[:], psY[0:HEADS * QT, 0:P], -1.0, None, ALU.mult).then_inc(max_cast, 1)
                    if take_exp:
                        normalise(v - 1, W_PAIRS - 1)

                steps(dve, step)
                add(B - 1)
                dve.wait_ge(added, B)



ROUND = 1.5 * 2.0 ** 23
INT8_MAX = 127.0


def layer1_int8(nc, io, res):
    with Phase(nc, "q1") as ph:
        wT = ph.sb("wT", [P, D])
        w_max, w_scale, w_inv = (ph.sb(n, [P, 1]) for n in ("w_max", "w_scale", "w_inv"))
        wr = ph.sb("wr", [P, D])
        wq = ph.sb("wq", [P, D], BF16)
        diag = ph.sb("diag", [P, P])
        col_scale = ph.sb("col_scale", [P, D])
        x_max, x_scale, x_inv, x_gate = (ph.sb(n, [P, NTILE]) for n in ("x_max", "x_scale", "x_inv", "x_gate"))
        xr = ph.sb("xr", [P, NTILE, D])
        tmp = [ph.sb(f"tmp{i}", [P, D]) for i in range(2)]
        xq = ph.sb("xq", [P, NTILE * P], BF16)
        psW = ph.ps("psW", [P, CHUNK])
        psT = [ph.ps(f"psT{i}", [P, CHUNK]) for i in range(2)]
        psY = [ph.ps(f"psY{i}", [P, 4, D]) for i in range(2)]
        w_in, step, w_turned, w_copied = (ph.sem(n) for n in ("w_in", "step", "w_turned", "w_copied"))
        rounded, turned, copied, made, scaled, added = (ph.sem(n) for n in ("rounded", "turned", "copied", "made", "scaled", "added"))
        with ph.block() as block:
            @block.sync
            def _(sp):
                sp.dma_start(wT[:], io["L1_rhsT"]).then_inc(w_in, 16)

            @block.vector
            def _(dve):
                dve.tensor_reduce(x_max[:], res.xn[:], AX.X, ALU.max, apply_absolute_value=True).then_inc(step, 1)
                dve.wait_ge(step, 1)
                dve.tensor_scalar(x_scale[:], x_max[:], 1e-12, 1.0 / INT8_MAX, ALU.max, ALU.mult).then_inc(step, 1)
                dve.wait_ge(step, 2)
                dve.reciprocal(x_inv[:], x_scale[:]).then_inc(step, 1)
                dve.tensor_scalar(x_gate[:], x_scale[:], res.gates[:, 5:6], None, ALU.mult).then_inc(step, 1)
                dve.wait_ge(step, 4)
                for t in range(NTILE):
                    dve.tensor_scalar(xr[:, t, :], res.xn[:, t, :], x_inv[:, t:t + 1], ROUND, ALU.mult, ALU.add).then_inc(step, 1)
                dve.wait_ge(step, 4 + NTILE)
                dve.tensor_scalar(xr[:], xr[:], ROUND, INT8_MAX, ALU.subtract, ALU.min).then_inc(step, 1)
                dve.wait_ge(step, 5 + NTILE)
                dve.tensor_scalar(xr[:], xr[:], -INT8_MAX, None, ALU.max).then_inc(rounded, 1)
                dve.wait_ge(w_in, 16)
                dve.tensor_reduce(w_max[:], wT[:], AX.X, ALU.max, apply_absolute_value=True).then_inc(step, 1)
                dve.wait_ge(step, 6 + NTILE)
                dve.tensor_scalar(w_scale[:], w_max[:], 1e-12, 1.0 / INT8_MAX, ALU.max, ALU.mult).then_inc(step, 1)
                dve.wait_ge(step, 7 + NTILE)
                dve.reciprocal(w_inv[:], w_scale[:]).then_inc(step, 1)
                dve.tensor_scalar(diag[:], res.ident[:], w_scale[:], None, ALU.mult).then_inc(step, 1)
                dve.wait_ge(step, 9 + NTILE)
                dve.tensor_scalar(wr[:], wT[:], w_inv[:], ROUND, ALU.mult, ALU.add).then_inc(step, 1)
                dve.wait_ge(step, 10 + NTILE)
                dve.tensor_scalar(wr[:], wr[:], ROUND, INT8_MAX, ALU.subtract, ALU.min).then_inc(step, 1)
                dve.wait_ge(step, 11 + NTILE)
                dve.tensor_scalar(wr[:], wr[:], -INT8_MAX, None, ALU.max).then_inc(rounded, 1)
                dve.wait_ge(w_turned, 1)
                dve.tensor_copy(wq[:], psW[:, 0:D]).then_inc(w_copied, 1)
                dve.tensor_copy(col_scale[:], psW[:, D:2 * D]).then_inc(w_copied, 1)
                dve.wait_ge(w_copied, 2)
                for c in range(NCHUNK):
                    dve.wait_ge(made, c + 1)
                    for k in range(4):
                        t = 4 * c + k
                        dve.scalar_tensor_tensor(tmp[k % 2][:], psY[c % 2][:, k, :], x_gate[:, t:t + 1], col_scale[:],
                                                 ALU.mult, ALU.mult).then_inc(scaled, 1)
                        dve.wait_ge(scaled, t + 1)
                        dve.tensor_tensor(res.X[:, t, :], res.X[:, t, :], tmp[k % 2][:], ALU.add).then_inc(added, 1)
                dve.wait_ge(added, NTILE)

            @block.tensor
            def _(pe):
                pe.wait_ge(rounded, 1)
                for c in range(NCHUNK):
                    if c >= 2:
                        pe.wait_ge(copied, c - 1)
                    for k in range(4):
                        last = pe.transpose(psT[c % 2][:, k * P:(k + 1) * P], xr[:, 4 * c + k, :], res.ident[:])
                    last.then_inc(turned, 1)
                pe.wait_ge(rounded, 2)
                pe.transpose(psW[:, 0:D], wr[:], res.ident[:])
                pe.matmul(psW[:, D:2 * D], res.ones[:], diag[:], start=True, stop=True).then_inc(w_turned, 1)
                pe.wait_ge(w_copied, 2)
                for c in range(NCHUNK):
                    pe.wait_ge(copied, c + 1)
                    if c >= 2:
                        pe.wait_ge(scaled, 4 * (c - 1))
                    for k in range(4):
                        t = 4 * c + k
                        last = pe.matmul(psY[c % 2][:, k, :], xq[:, t * P:(t + 1) * P], wq[:], start=True, stop=True)
                    last.then_inc(made, 1)

            @block.scalar
            def _(act):
                for c in range(NCHUNK):
                    act.wait_ge(turned, c + 1)
                    act.copy(xq[:, c * CHUNK:(c + 1) * CHUNK], psT[c % 2][:]).then_inc(copied, 1)


def layer3_ternary(nc, io, res):
    with Phase(nc, "q3") as ph:
        w = ph.sb("w", [P, D])
        w_abs, w_mean, w_low, x_abs, x_scale, x_inv, out_scale = (
            ph.sb(n, [P, 1]) for n in ("w_abs", "w_mean", "w_low", "x_abs", "x_scale", "x_inv", "out_scale"))
        w_half = ph.sb("w_half", [P, 1])
        over, under = ph.sb("over", [P, D]), ph.sb("under", [P, D])
        wq = ph.sb("wq", [P, D], BF16)
        bias = ph.sb("bias", [P, D])
        x_top = ph.sb("x_top", [1, 1])
        xr = ph.sb("xr", [P, NTILE, D])
        tmp = [ph.sb(f"tmp{i}", [P, D]) for i in range(2)]
        xq = ph.sb("xq", [P, NTILE * P], BF16)
        psS = ph.ps("psS", [P, CHUNK])
        psT = [ph.ps(f"psT{i}", [P, CHUNK]) for i in range(2)]
        psY = [ph.ps(f"psY{i}", [P, 4, D]) for i in range(2)]
        w_in, step, x_reduced, x_turned, x_topped, w_reduced, w_summed = (
            ph.sem(n) for n in ("w_in", "step", "x_reduced", "x_turned", "x_topped", "w_reduced", "w_summed"))
        rounded, ternary, turned, copied, made, scaled, added = (
            ph.sem(n) for n in ("rounded", "ternary", "turned", "copied", "made", "scaled", "added"))
        with ph.block() as block:
            @block.sync
            def _(sp):
                sp.dma_start(w[:], io["L3_wT"]).then_inc(w_in, 16)
                sp.dma_start(bias[:], io["L3_bias"].partition_broadcast(P)).then_inc(w_in, 16)

            @block.vector
            def _(dve):
                dve.tensor_reduce(x_abs[:], res.xn[:], AX.XY, ALU.max, apply_absolute_value=True).then_inc(x_reduced, 1)
                dve.wait_ge(w_in, 32)
                dve.tensor_reduce(w_abs[:], w[:], AX.X, ALU.add, apply_absolute_value=True).then_inc(w_reduced, 1)
                dve.wait_ge(x_turned, 1)
                dve.tensor_reduce(x_top[:], psS[0:1, 0:P], AX.X, ALU.max).then_inc(x_topped, 1)
                dve.wait_ge(w_summed, 1)
                dve.tensor_scalar(w_mean[:], psS[:, P:P + 1], 1.0 / (D * D), None, ALU.mult).then_inc(step, 1)
                dve.tensor_scalar(w_half[:], psS[:, P:P + 1], 0.5 / (D * D), None, ALU.mult).then_inc(step, 1)
                dve.tensor_scalar(w_low[:], psS[:, P:P + 1], -0.5 / (D * D), None, ALU.mult).then_inc(step, 1)
                dve.tensor_scalar(x_scale[:], psS[:, P + 1:P + 2], 1.0 / INT8_MAX, None, ALU.mult).then_inc(step, 1)
                dve.wait_ge(step, 4)
                dve.reciprocal(x_inv[:], x_scale[:]).then_inc(step, 1)
                dve.tensor_scalar(over[:], w[:], w_half[:], None, ALU.is_gt).then_inc(step, 1)
                dve.tensor_scalar(under[:], w[:], w_low[:], None, ALU.is_lt).then_inc(step, 1)
                dve.scalar_tensor_tensor(out_scale[:], w_mean[:], res.gates[:, 7:8], x_scale[:], ALU.mult, ALU.mult).then_inc(step, 1)
                dve.wait_ge(step, 8)
                dve.tensor_tensor(wq[:], over[:], under[:], ALU.subtract).then_inc(ternary, 1)
                dve.tensor_scalar(bias[:], bias[:], res.gates[:, 7:8], None, ALU.mult).then_inc(step, 1)
                dve.tensor_scalar(xr[:], res.xn[:], x_inv[:], ROUND, ALU.mult, ALU.add).then_inc(step, 1)
                dve.wait_ge(step, 10)
                dve.tensor_scalar(xr[:], xr[:], ROUND, INT8_MAX, ALU.subtract, ALU.min).then_inc(step, 1)
                dve.wait_ge(step, 11)
                dve.tensor_scalar(xr[:], xr[:], -INT8_MAX - 1.0, None, ALU.max).then_inc(rounded, 1)
                for c in range(NCHUNK):
                    dve.wait_ge(made, c + 1)
                    for k in range(4):
                        t = 4 * c + k
                        dve.scalar_tensor_tensor(tmp[k % 2][:], psY[c % 2][:, k, :], out_scale[:], bias[:],
                                                 ALU.mult, ALU.add).then_inc(scaled, 1)
                        dve.wait_ge(scaled, t + 1)
                        dve.tensor_tensor(res.X[:, t, :], res.X[:, t, :], tmp[k % 2][:], ALU.add).then_inc(added, 1)
                dve.wait_ge(added, NTILE)

            @block.tensor
            def _(pe):
                pe.wait_ge(x_reduced, 1)
                pe.transpose(psS[0:1, 0:P], x_abs[:], res.ident[:]).then_inc(x_turned, 1)
                pe.wait_ge(w_reduced, 1)
                pe.wait_ge(x_topped, 1)
                pe.matmul(psS[:, P:P + 1], res.ones[:], w_abs[:], start=True, stop=True)
                pe.matmul(psS[:, P + 1:P + 2], res.ones[0:1, :], x_top[:], start=True, stop=True).then_inc(w_summed, 1)
                pe.wait_ge(rounded, 1)
                for c in range(NCHUNK):
                    if c >= 2:
                        pe.wait_ge(copied, c - 1)
                    for k in range(4):
                        last = pe.transpose(psT[c % 2][:, k * P:(k + 1) * P], xr[:, 4 * c + k, :], res.ident[:])
                    last.then_inc(turned, 1)
                pe.wait_ge(ternary, 1)
                for c in range(NCHUNK):
                    pe.wait_ge(copied, c + 1)
                    if c >= 2:
                        pe.wait_ge(scaled, 4 * (c - 1))
                    for k in range(4):
                        t = 4 * c + k
                        last = pe.matmul(psY[c % 2][:, k, :], xq[:, t * P:(t + 1) * P], wq[:], start=True, stop=True)
                    last.then_inc(made, 1)

            @block.scalar
            def _(act):
                for c in range(NCHUNK):
                    act.wait_ge(turned, c + 1)
                    act.copy(xq[:, c * CHUNK:(c + 1) * CHUNK], psT[c % 2][:]).then_inc(copied, 1)


def more_layouts(a, io):
    io["c_iota"] = np.arange(16, dtype=np.float32)
    io["c_tri"] = np.triu(np.ones((P, P), np.float32))
    io["L0_Wg"] = a["L0_ffn_Wg"]
    io["L0_W1"], io["L0_W2"], io["L0_b2"] = a["L0_ffn_W1"], a["L0_ffn_W2"], a["L0_ffn_b2"]
    io["L0_b1"] = a["L0_ffn_b1"].reshape(8, 4, P).transpose(0, 2, 1)
    shared = lambda s, e: np.concatenate([a["L2_ffn_" + s][None], a["L2_ffn_" + e]])
    io["L2_router_W"], io["L2_router_b"] = a["L2_ffn_router_W"], a["L2_ffn_router_b"]
    io["L2_W1"], io["L2_W2"], io["L2_b2"] = shared("sW1", "eW1"), shared("sW2", "eW2"), shared("sb2", "eb2")
    io["L2_b1"] = shared("sb1", "eb1").reshape(16, 1, P).transpose(0, 2, 1)
    io["L1_rhsT"] = a["L1_ffn_rhs"].T
    io["L3_wT"], io["L3_bias"] = a["L3_ffn_weight"].T, a["L3_ffn_bias"]

    io["key_pos"] = a["itok_BxS2_1_8191"]
    io["mask"] = a["mask_BxSxS2_if1"]
    io["maskT"] = a["mask_BxSxS2_if1"].transpose(0, 2, 1)
    io["tri"] = a["mask_SxS2_bk0"]
    io["triT"] = np.ascontiguousarray(a["mask_SxS2_bk0"].T)
    io["pad"] = a["mask_BxS2_bk1"].reshape(B * S2)
    io["padT"] = np.ascontiguousarray(a["mask_BxS2_bk1"].reshape(B, KT, P).transpose(2, 0, 1))
    ratio = 2.0 ** (-8.0 / HEADS)
    rest = np.array([ratio ** i for i in range(1, HEADS + 1)], np.float32)
    io["c_slopes"] = np.zeros((9, HEADS, S), np.float32)
    for part in range(3):
        top = (rest.view(np.uint32) & np.uint32(0xFFFF0000)).view(np.float32)
        io["c_slopes"][3 * part:3 * part + 3] = top[None, :, None]
        rest = rest - top

    io["L1_wq"] = a["L1_xattn_w_query"].transpose(1, 2, 0)
    io["L1_wk"] = a["L1_xattn_w_key"].transpose(1, 2, 0)
    io["L1_wv"] = a["L1_xattn_w_value"].reshape(D, WIDE_V)
    io["L1_wo"] = a["L1_xattn_w_projection"].transpose(0, 2, 1).reshape(WIDE_V, D)
    io["L1_bq"] = a["L1_xattn_b_query"].reshape(HEADS, WIDE_E).T
    io["L1_bv"] = a["L1_xattn_b_value"].reshape(W_PAIRS, P).T
    io["L1_bp"] = a["L1_xattn_b_projection"]



def build(nc, io, stop=99, start=0):
    res = Resident()
    with Phase(nc, "res") as ph:
        res.X = ph.sb("X", [P, NTILE, D])
        res.xn = ph.sb("xn", [P, NTILE, D])
        res.xnT = ph.sb("xnT", [P, NTILE * P])
        res.gates = ph.sb("gates", [P, 8])
        res.ident = ph.sb("ident", [P, P])
        res.identb = ph.sb("identb", [P, P], BF16)
        res.ones = ph.sb("ones", [P, P])
        res.onesb = ph.sb("onesb", [P, P], BF16)
        load_phase(nc, io, res)
        steps = [
            lambda: (norm_phase(nc, io, res, "n0"), layer0_attention(nc, io, res)),
            lambda: (norm_phase(nc, io, res, "n1"), layer0_experts(nc, io, res)),
            lambda: (norm_phase(nc, io, res, "n2"), layer1_attention(nc, io, res)),
            lambda: (norm_phase(nc, io, res, "n3", transposed=False), layer1_int8(nc, io, res)),
            lambda: (norm_phase(nc, io, res, "n4"), narrow_attention(nc, io, res, LayerTwo)),
            lambda: (norm_phase(nc, io, res, "n5"), layer2_experts(nc, io, res)),
            lambda: (norm_phase(nc, io, res, "n6"), narrow_attention(nc, io, res, LayerThree)),
            lambda: (norm_phase(nc, io, res, "n7", transposed=False), layer3_ternary(nc, io, res)),
        ]
        for n, step in enumerate(steps[start:stop]):
            if n in (3, 5, 7):
                Phase.clear_used(nc)
            step()
        store_phase(nc, io, res)



def layouts(inputs):
    a = {k: np.asarray(v) for k, v in inputs.items()}
    tr = lambda w: np.ascontiguousarray(w.T)
    io = {
        "x": a["x"].reshape(B * S, D),
        "ctxT": np.ascontiguousarray(a["ctx_1024"].reshape(B * S2, D).T),
        "g_xattn": a["g_xattn"], "g_ffn": a["g_ffn"],
        "c_ident": np.eye(P, dtype=np.float32),
    }
    for w in ("Wq", "Wk", "Wv", "Wo"):
        io[f"L0_{w}T"] = tr(a[f"L0_xattn_{w}"])
        io[f"L3_{w}T"] = tr(a[f"L3_xattn_{w}"])
    for b in ("bq", "bk", "bv", "bo"):
        io[f"L0_{b}"] = a[f"L0_xattn_{b}"]
        io[f"L3_{b}"] = a[f"L3_xattn_{b}"]
    for w in ("q", "k", "v", "o"):
        io[f"L2_W{w}T"] = tr(a[f"L2_xattn_W_{w}"])
    more_layouts(a, io)
    return {k: np.ascontiguousarray(v) for k, v in io.items()}


def kernel(**inputs):
    import concourse.bacc as bacc
    from concourse.bass_utils import run_bass_kernel_spmd

    nc = bacc.Bacc("TRN2", target_bir_lowering=False, num_devices=1)
    arrays = layouts(inputs)
    io = {n: nc.dram_tensor(f"in_{n}", v.shape, mybir.dt.from_np(v.dtype), kind="ExternalInput").ap() for n, v in arrays.items()}
    io["out"] = nc.dram_tensor("out_0", (B * S, D), F32, kind="ExternalOutput").ap()
    build(nc, io)
    got = run_bass_kernel_spmd(nc, [{f"in_{n}": v for n, v in arrays.items()}], core_ids=[0])
    return got.results[0]["out_0"].reshape(B, S, D)
```

```python
from contextlib import ExitStack

import numpy as np

import concourse.bass as bass
from concourse import mybir

P = 128
B, S, S2, D = 8, 256, 512, 128
NTILE = B * S // P
QT = S // P
KT = S2 // P
CHUNK = 512
NCHUNK = B * S // CHUNK
HEADS = 16
BIG = 2.0 ** 100
LN_EPS = 1e-5

F32 = mybir.dt.float32
BF16 = mybir.dt.bfloat16
I32 = mybir.dt.int32
U8 = mybir.dt.uint8
U32 = mybir.dt.uint32
ALU = mybir.AluOpType
ACT = mybir.ActivationFunctionType
AX = mybir.AxisListType


class Phase:

    used = []

    def __init__(self, nc, name):
        self.nc, self.name, self.stack = nc, name, ExitStack()

    def __enter__(self):
        self.stack.__enter__()
        return self

    def __exit__(self, *exc):
        return self.stack.__exit__(*exc)

    def sb(self, name, shape, dt=F32):
        return self.stack.enter_context(self.nc.sbuf_tensor(f"{self.name}_{name}", shape, dt))

    def ps(self, name, shape, dt=F32):
        return self.stack.enter_context(self.nc.psum_tensor(f"{self.name}_{name}", shape, dt))

    def sem(self, name):
        handle = self.nc.alloc_semaphore(f"{self.name}_{name}")
        Phase.used.append(handle)
        return handle

    @staticmethod
    def clear_used(nc):
        nc.clear_and_free_semaphores(Phase.used)
        nc.all_engine_barrier()
        Phase.used.clear()

    def block(self):
        return self.nc.Block(no_gpsimd_drain=True)


class Resident:
    pass


def load_phase(nc, io, res):
    with Phase(nc, "load") as ph:
        loaded, gates_in, gates_done = ph.sem("loaded"), ph.sem("gates_in"), ph.sem("gates_done")
        ones_done, cast_done = ph.sem("ones_done"), ph.sem("cast_done")
        raw_gates = ph.sb("raw_gates", [P, 8])
        with ph.block() as block:
            @block.sync
            def _(sp):
                sp.dma_start(raw_gates[:, 0:4], io["g_xattn"].partition_broadcast(P)).then_inc(gates_in, 16)
                sp.dma_start(raw_gates[:, 4:8], io["g_ffn"].partition_broadcast(P)).then_inc(gates_in, 16)
                sp.dma_start(res.ident[:], io["c_ident"]).then_inc(loaded, 16)
                sp.dma_start(res.X[:], io["x"].rearrange("(t p) d -> p t d", p=P)).then_inc(loaded, 16)
                sp.wait_ge(loaded, 32)

            @block.scalar
            def _(act):
                act.wait_ge(gates_in, 32)
                act.activation(res.gates[:], raw_gates[:], ACT.Tanh).then_inc(gates_done, 1)
                act.wait_ge(gates_done, 1)

            @block.vector
            def _(dve):
                dve.memset(res.ones[:], 1.0).then_inc(ones_done, 1)
                dve.memset(res.onesb[:], 1.0).then_inc(ones_done, 1)
                dve.wait_ge(loaded, 32)
                dve.tensor_copy(res.identb[:], res.ident[:]).then_inc(cast_done, 1)
                dve.wait_ge(cast_done, 1)
                dve.wait_ge(ones_done, 2)


def norm_phase(nc, io, res, name, transposed=True):
    with Phase(nc, name) as ph:
        stats = ph.sb("stats", [P, NTILE, 6])
        mv = ph.sb("mv", [P, NTILE, 2])
        std = ph.sb("std", [P, NTILE])
        r0 = ph.sb("r0", [P, NTILE])
        rr = ph.sb("rr", [P, NTILE])
        rstd = ph.sb("rstd", [P, NTILE])
        var_eps = ph.sb("var_eps", [P, NTILE])
        psT = [ph.ps(f"psT{i}", [P, CHUNK]) for i in range(2)]
        stats_done, aggr_done = ph.sem("stats_done"), ph.sem("aggr_done")
        var_done, std_done, newton = ph.sem("var_done"), ph.sem("std_done"), ph.sem("newton")
        xn_done, turned, copied = ph.sem("xn_done"), ph.sem("turned"), ph.sem("copied")
        with ph.block() as block:
            @block.vector
            def _(dve):
                for t in range(NTILE):
                    dve.bn_stats(stats[:, t, :], res.X[:, t, :]).then_inc(stats_done, 1)
                for t in range(NTILE):
                    dve.wait_ge(stats_done, t + 1)
                    dve.bn_aggr(mv[:, t, :], stats[:, t, :]).then_inc(aggr_done, 1)
                dve.wait_ge(aggr_done, NTILE)
                dve.tensor_scalar(var_eps[:], mv[:, :, 1], LN_EPS, None, ALU.add).then_inc(var_done, 1)
                dve.wait_ge(std_done, 1)
                dve.reciprocal(r0[:], std[:]).then_inc(newton, 1)
                dve.wait_ge(newton, 1)
                dve.tensor_tensor(rr[:], r0[:], r0[:], ALU.mult).then_inc(newton, 1)
                dve.wait_ge(newton, 2)
                dve.tensor_tensor(std[:], rr[:], var_eps[:], ALU.mult).then_inc(newton, 1)
                dve.wait_ge(newton, 3)
                dve.tensor_scalar(rr[:], std[:], -0.5, 1.5, ALU.mult, ALU.add).then_inc(newton, 1)
                dve.wait_ge(newton, 4)
                dve.tensor_tensor(rstd[:], r0[:], rr[:], ALU.mult).then_inc(newton, 1)
                dve.wait_ge(newton, 5)
                for t in range(NTILE):
                    dve.tensor_scalar(res.xn[:, t, :], res.X[:, t, :], mv[:, t, 0:1], rstd[:, t:t + 1],
                                      ALU.subtract, ALU.mult).then_inc(xn_done, 1)
                dve.wait_ge(xn_done, NTILE)

            @block.scalar
            def _(act):
                act.wait_ge(var_done, 1)
                act.activation(std[:], var_eps[:], ACT.Sqrt).then_inc(std_done, 1)
                if transposed:
                    for c in range(NCHUNK):
                        act.wait_ge(turned, c + 1)
                        act.copy(res.xnT[:, c * CHUNK:(c + 1) * CHUNK], psT[c % 2][:]).then_inc(copied, 1)
                    act.wait_ge(copied, NCHUNK)

            @block.tensor
            def _(pe):
                if transposed:
                    for c in range(NCHUNK):
                        if c >= 2:
                            pe.wait_ge(copied, c - 1)
                        for k in range(4):
                            t = 4 * c + k
                            pe.wait_ge(xn_done, t + 1)
                            last = pe.transpose(psT[c % 2][:, k * P:(k + 1) * P], res.xn[:, t, :], res.ident[:])
                        last.then_inc(turned, 1)


def store_phase(nc, io, res):
    with Phase(nc, "store") as ph:
        stored = ph.sem("stored")
        with ph.block() as block:
            @block.sync
            def _(sp):
                sp.dma_start(io["out"].rearrange("(t p) d -> p t d", p=P), res.X[:]).then_inc(stored, 16)
                sp.wait_ge(stored, 16)



L0_GROUPS, L0_HEADS, L0_E = 8, 8, 2
L0_KEYS = 2 * L0_GROUPS
L0_SCORES = L0_GROUPS * L0_HEADS * L0_KEYS


def layer0_attention(nc, io, res):
    scale = 1.0 / float(np.sqrt(L0_E))
    with Phase(nc, "a0") as ph:
        Q = ph.sb("Q", [P, NTILE, D])
        K = ph.sb("K", [P, NTILE, 2, D])
        V = ph.sb("V", [P, NTILE, 2, D])
        O = ph.sb("O", [P, NTILE, D])
        ctxT = ph.sb("ctxT", [P, NTILE, P, 2])
        project_qkv_layer0(nc, io, res, Q, K, V, ctxT)
        attend_layer0(nc, io, res, Q, K, V, O, ctxT, scale)
        with Phase(nc, "a0o") as po:
            project_out(nc, io, res, po, O, "L0_WoT", "L0_bo", res.gates[:, 0:1])


def project_qkv_layer0(nc, io, res, Q, K, V, ctxT):
    with Phase(nc, "a0p") as ph:
        wq = ph.sb("wq", [P, D])
        wkv = ph.sb("wkv", [P, 2 * D])
        bq = ph.sb("bq", [P, D])
        bkv = ph.sb("bkv", [P, 2, 2 * D])
        psQ = [ph.ps(f"psQ{i}", [P, CHUNK]) for i in range(2)]
        psKV = [ph.ps(f"psKV{i}", [P, 2, 2 * D]) for i in range(2)]
        w_in, ctx_in = ph.sem("w_in"), [ph.sem(f"ctx_in{i}") for i in range(4)]
        q_ready, kv_ready, q_out, kv_out = ph.sem("q_ready"), ph.sem("kv_ready"), ph.sem("q_out"), ph.sem("kv_out")
        n_w = 7
        with ph.block() as block:
            @block.sync
            def _(sp):
                sp.dma_start(wq[:], io["L0_WqT"]).then_inc(w_in, 16)
                sp.dma_start(wkv[:, 0:D], io["L0_WkT"]).then_inc(w_in, 16)
                sp.dma_start(wkv[:, D:2 * D], io["L0_WvT"]).then_inc(w_in, 16)
                sp.dma_start(bq[:], io["L0_bq"].partition_broadcast(P)).then_inc(w_in, 16)
                for j, name in enumerate(("L0_bk", "L0_bv")):
                    for two in range(2):
                        if j == 1 and two == 1:
                            continue
                        sp.dma_start(bkv[:, two, j * D:(j + 1) * D], io[name].partition_broadcast(P)).then_inc(w_in, 16)
                sp.dma_start(bkv[:, 1, D:2 * D], io["L0_bv"].partition_broadcast(P)).then_inc(ctx_in[0], 16)
                for i in range(4):
                    sp.dma_start(ctxT[:, 4 * i:4 * i + 4], io["ctxT"].rearrange("d (t n c) -> d t n c", n=P, c=2)[:, 4 * i:4 * i + 4]).then_inc(ctx_in[i], 16)

            @block.tensor
            def _(pe):
                pe.wait_ge(w_in, 16 * n_w)
                for t in range(NTILE):
                    if t % 4 == 0:
                        pe.wait_ge(ctx_in[t // 4], 32 if t == 0 else 16)
                    if t >= 2:
                        pe.wait_ge(q_out, t - 1)
                        pe.wait_ge(kv_out, 2 * (t - 1))
                    pe.matmul(psQ[t % 2][:, 0:D], res.xnT[:, t * P:(t + 1) * P], wq[:], start=True, stop=True).then_inc(q_ready, 1)
                    for two in range(2):
                        last = pe.matmul(psKV[t % 2][:, two, :], ctxT[:, t, :, two], wkv[:], start=True, stop=True)
                    last.then_inc(kv_ready, 1)

            @block.vector
            def _(dve):
                dve.wait_ge(w_in, 16 * n_w)
                dve.wait_ge(ctx_in[0], 32)
                for t in range(NTILE):
                    dve.wait_ge(q_ready, t + 1)
                    dve.tensor_tensor(Q[:, t, :], psQ[t % 2][:, 0:D], bq[:], ALU.add).then_inc(q_out, 1)
                    dve.wait_ge(kv_ready, t + 1)
                    dve.tensor_tensor(K[:, t], psKV[t % 2][:, :, 0:D], bkv[:, :, 0:D], ALU.add).then_inc(kv_out, 1)
                    dve.tensor_tensor(V[:, t], psKV[t % 2][:, :, D:2 * D], bkv[:, :, D:2 * D], ALU.add).then_inc(kv_out, 1)


def attend_layer0(nc, io, res, Q, K, V, O, ctxT, scale):
    n_chunks = B * S2 // CHUNK
    fold_scale = 1.0 / float(np.sqrt(WIDE_E))
    full = [P, L0_GROUPS, L0_HEADS, L0_KEYS]
    rows = L0_GROUPS * L0_HEADS
    with Phase(nc, "a0a") as ph:
        m0 = [ph.sb(f"m0_{i}", full) for i in range(2)]
        sc = [ph.sb(f"sc_{i}", full) for i in range(2)]
        ex = [ph.sb(f"ex_{i}", full) for i in range(2)]
        pv0 = [ph.sb(f"pv0_{i}", full) for i in range(2)]
        pv1 = ph.sb("pv1", full)
        m1 = ph.sb("m1", full)
        mx = [ph.sb(f"mx_{i}", [P, rows]) for i in range(2)]
        den = ph.sb("den", [P, rows])
        rec = ph.sb("rec", [P, rows])
        osum = ph.sb("osum", [P, 2, rows])
        m0_done, m1_done, add_done, max_done = (ph.sem(n) for n in ("m0_done", "m1_done", "add_done", "max_done"))
        sub_done, exp_done, pv0_done, pv1_done = (ph.sem(n) for n in ("sub_done", "exp_done", "pv0_done", "pv1_done"))
        den_done, rec_done, osum_done, norm_done = (ph.sem(n) for n in ("den_done", "rec_done", "osum_done", "norm_done"))

        w1q, w1k = ph.sb("w1q", [WIDE_E, HEADS, D]), ph.sb("w1k", [WIDE_E, HEADS, D])
        b1q, b1v, b1p = ph.sb("b1q", [WIDE_E, HEADS]), ph.sb("b1v", [P, W_PAIRS]), ph.sb("b1p", [1, D])
        wk = [ph.sb(f"wk{i}", [P, D]) for i in range(2)]
        bk = ph.sb("bk", [1, D])
        minus_i = ph.sb("minus_i", [P, P], BF16)
        parts = [ph.sb(f"parts{i}", [P, 3, CHUNK], BF16) for i in range(2)]
        psG = [ph.ps(f"psG{i}", [P, 4, D]) for i in range(2)]
        psB = ph.ps("psB", [P, HEADS])
        psR = ph.ps("psR", [1, D])
        psK = [ph.ps(f"psK{i}", [P, CHUNK]) for i in range(2)]
        w_in, folded, fold_copied = ph.sem("w_in"), ph.sem("folded"), ph.sem("fold_copied")
        minus_done = ph.sem("minus_done")
        k_made, k_cut = [ph.sem(f"k_made{i}") for i in range(2)], [ph.sem(f"k_cut{i}") for i in range(2)]
        k_stored = [ph.sem(f"k_stored{i}") for i in range(2)]
        n_w = 10

        def q_of(t, e):
            v = Q[:, bass.ds(t, 1), :].rearrange("p o (l h e) -> p (o l) h e", h=L0_HEADS, e=L0_E)
            return v[:, :, :, e:e + 1].to_broadcast(full)

        def kv_of(M, t, e):
            v = M[:, bass.ds(t, 1), :, :].rearrange("p o c (s h e) -> p e o h (c s)", h=L0_HEADS, e=L0_E)
            return v[:, e, :, :, :].to_broadcast(full)

        def flat(a):
            return a[:].rearrange("p l h s -> p (l h) s")

        with ph.block() as block:
            @block.gpsimd
            def _(pool):
                def products(t, b):
                    pool.tensor_tensor(m0[b][:], q_of(t, 0), kv_of(K, t, 0), ALU.mult).then_inc(m0_done, 1)

                def subtract(t, b):
                    pool.wait_ge(max_done, t + 1)
                    pool.tensor_tensor(flat(sc[b]), flat(sc[b]), mx[b][:].unsqueeze(2).to_broadcast([P, rows, L0_KEYS]),
                                       ALU.subtract).then_inc(sub_done, 1)

                def weighted(t, b):
                    pool.wait_ge(exp_done, t + 1)
                    pool.tensor_tensor(pv0[b][:], ex[b][:], kv_of(V, t, 0), ALU.mult).then_inc(pv0_done, 1)

                def step(v, b, first=False, last=False):
                    weighted(v - 1, 1 - b)
                    if not last:
                        pool.wait_ge(add_done, v)
                        products(v + 1, 1 - b)
                    subtract(v, b)

                products(0, 0)
                products(1, 1)
                subtract(0, 0)
                with pool.Fori(0, (NTILE - 2) // 2) as i:
                    for k in range(2):
                        step(2 * i + 1 + k, (1 + k) % 2)
                step(NTILE - 1, 1, last=True)
                weighted(NTILE - 1, 1)

            @block.sync
            def _(sp):
                sp.dma_start(w1q[:], io["L1_wq"].rearrange("n e d -> e n d")).then_inc(w_in, 16)
                sp.dma_start(w1k[:], io["L1_wk"].rearrange("n e d -> e n d")).then_inc(w_in, 16)
                sp.dma_start(b1q[:], io["L1_bq"]).then_inc(w_in, 16)
                sp.dma_start(b1v[:], io["L1_bv"]).then_inc(w_in, 16)
                sp.dma_start(b1p[:], io["L1_bp"]).then_inc(w_in, 16)
                sp.dma_start(res.wv1[:], io["L1_wv"]).then_inc(w_in, 16)
                sp.dma_start(res.wo1[:], io["L1_wo"].rearrange("(c p) d -> p c d", p=P)).then_inc(w_in, 16)
                sp.dma_start(wk[0][:], io["L2_WkT"]).then_inc(w_in, 16)
                sp.dma_start(wk[1][:], io["L3_WkT"]).then_inc(w_in, 16)
                sp.dma_start(bk[:], io["L3_bk"].unsqueeze(0)).then_inc(w_in, 16)
                sp.wait_ge(w_in, 16 * n_w)
                with sp.Fori(0, n_chunks) as n:
                    for l in range(2):
                        sp.wait_ge(k_cut[l], 3 * n + 3)
                        sp.dma_start(res.keys[l][bass.ds(n, 1)].rearrange("o c f k -> f (o c) k"), parts[l][:]).then_inc(k_stored[l], 16)
                for l in range(2):
                    sp.wait_ge(k_stored[l], 16 * n_chunks)

            @block.tensor
            def _(pe):
                def chunk(n, first):
                    keys = ctxT[:, bass.ds(2 * n, 2)].rearrange("d t n c -> d (t n c)")
                    for l in range(2):
                        if not first:
                            pe.wait_ge(k_cut[l], 3 * n)
                        last = pe.matmul(psK[l][:], wk[l][:], keys, start=True, stop=False, skip_group_check=True)
                        if l == 1:
                            last = pe.matmul(psK[l][:], bk[:], res.ones[0:1, :].unsqueeze(1).to_broadcast([1, CHUNK // P, P]),
                                             start=False, stop=False, skip_group_check=True)
                        last.then_inc(k_made[l], 1)
                    for part in range(2):
                        for l in range(2):
                            pe.wait_ge(k_cut[l], 3 * n + part + 1)
                            pe.matmul(psK[l][:], minus_i[:], parts[l][:, part, :], start=False, stop=(part == 1), skip_group_check=True).then_inc(k_made[l], 1)

                pe.wait_ge(w_in, 16 * n_w)
                for n in range(HEADS):
                    if n % 4 == 0 and n >= 8:
                        pe.wait_ge(fold_copied, n // 4 - 1)
                    last = pe.matmul(psG[n // 4 % 2][:, n % 4, :], w1q[:, n, :], w1k[:, n, :], start=True, stop=True)
                    if n % 4 == 3:
                        last.then_inc(folded, 1)
                for n in range(HEADS):
                    pe.matmul(psB[:, n:n + 1], w1k[:, n, :], b1q[:, n:n + 1], start=True, stop=True)
                for p in range(W_PAIRS):
                    pe.matmul(psR[:], b1v[:, p:p + 1], res.wo1[:, p, :], start=(p == 0), stop=False)
                pe.matmul(psR[:], res.ones[0:1, 0:1], b1p[:], start=False, stop=True).then_inc(folded, 1)
                pe.wait_ge(minus_done, 1)
                chunk(0, True)
                with pe.Fori(1, n_chunks) as n:
                    chunk(n, False)

            @block.scalar
            def _(act):
                def exponential(t, b):
                    act.wait_ge(sub_done, t + 1)
                    act.activation(ex[b][:], sc[b][:], ACT.Exp, scale=scale).then_inc(exp_done, 1)

                def cut(n, part, first):
                    for l in range(2):
                        if part == 0 and not first:
                            act.wait_ge(k_stored[l], 16 * n)
                        act.wait_ge(k_made[l], 3 * n + part + 1)
                        act.copy(parts[l][:, part, :], psK[l][:]).then_inc(k_cut[l], 1)

                act.activation(minus_i[:], res.ident[:], ACT.Identity, scale=-1.0).then_inc(minus_done, 1)
                exponential(0, 0)
                for c in range(HEADS // 4):
                    act.wait_ge(folded, c + 1)
                    act.activation(res.G[:, 4 * c:4 * c + 4, :], psG[c % 2][:], ACT.Identity, scale=fold_scale).then_inc(fold_copied, 1)
                act.wait_ge(folded, HEADS // 4 + 1)
                act.activation(res.q_bias[:], psB[:], ACT.Identity, scale=fold_scale).then_inc(fold_copied, 1)
                act.copy(res.bias_row1[:], psR[:]).then_inc(fold_copied, 1)
                exponential(1, 1)
                for part in range(3):
                    cut(0, part, True)
                with act.Fori(1, n_chunks) as i:
                    exponential(2 * i, 0)
                    cut(i, 0, False)
                    cut(i, 1, False)
                    exponential(2 * i + 1, 1)
                    cut(i, 2, False)
                act.wait_ge(fold_copied, HEADS // 4 + 2)

            @block.vector
            def _(dve):
                def front(t, b, first=False):
                    dve.tensor_tensor(m1[:], q_of(t, 1), kv_of(K, t, 1), ALU.mult).then_inc(m1_done, 1)
                    dve.wait_ge(m0_done, t + 1)
                    dve.wait_ge(m1_done, t + 1)
                    if not first:
                        dve.wait_ge(exp_done, t - 1)
                    dve.tensor_tensor(sc[b][:], m0[b][:], m1[:], ALU.add).then_inc(add_done, 1)
                    dve.wait_ge(add_done, t + 1)
                    dve.tensor_reduce(mx[b][:], flat(sc[b]), AX.X, ALU.max).then_inc(max_done, 1)

                def back(t, b):
                    dve.wait_ge(exp_done, t + 1)
                    dve.tensor_reduce(den[:], flat(ex[b]), AX.X, ALU.add).then_inc(den_done, 1)
                    dve.tensor_tensor(pv1[:], ex[b][:], kv_of(V, t, 1), ALU.mult).then_inc(pv1_done, 1)
                    dve.wait_ge(den_done, t + 1)
                    dve.reciprocal(rec[:], den[:]).then_inc(rec_done, 1)
                    dve.wait_ge(pv1_done, t + 1)
                    dve.tensor_reduce(osum[:, 1, :], flat(pv1), AX.X, ALU.add).then_inc(osum_done, 1)
                    dve.wait_ge(pv0_done, t + 1)
                    dve.tensor_reduce(osum[:, 0, :], flat(pv0[b]), AX.X, ALU.add).then_inc(osum_done, 1)
                    dve.wait_ge(rec_done, t + 1)
                    dve.wait_ge(osum_done, 2 * (t + 1))
                    dve.tensor_tensor(O[:, bass.ds(t, 1), :].rearrange("p o (r e) -> p (o r) e", e=L0_E),
                                      osum[:].rearrange("p e r -> p r e"),
                                      rec[:].unsqueeze(2).to_broadcast([P, rows, L0_E]), ALU.mult).then_inc(norm_done, 1)

                front(0, 0, first=True)
                front(1, 1, first=True)
                back(0, 0)
                with dve.Fori(0, (NTILE - 2) // 2) as i:
                    for k in range(2):
                        front(2 * i + 2 + k, k)
                        back(2 * i + 1 + k, (1 + k) % 2)
                back(NTILE - 1, 1)
                dve.wait_ge(norm_done, NTILE)


def project_out(nc, io, res, ph, O, wo_name, bo_name, gate):
    wo = ph.sb("wo", [P, D])
    bo = ph.sb("bo", [1, D])
    OT = [ph.sb(f"OT{i}", [P, CHUNK]) for i in range(2)]
    psT = [ph.ps(f"psT{i}", [P, CHUNK]) for i in range(2)]
    psY = [ph.ps(f"psY{i}", [P, CHUNK]) for i in range(2)]
    w_in, turned, copied, projected, added = (ph.sem(n) for n in ("w_in", "turned", "copied", "projected", "added"))
    with ph.block() as block:
        @block.sync
        def _(sp):
            sp.dma_start(wo[:], io[wo_name]).then_inc(w_in, 16)
            sp.dma_start(bo[:], io[bo_name].unsqueeze(0)).then_inc(w_in, 16)

        @block.tensor
        def _(pe):
            def turn(c):
                if c >= 2:
                    pe.wait_ge(copied, c - 1)
                for k in range(4):
                    last = pe.transpose(psT[c % 2][:, k * P:(k + 1) * P], O[:, 4 * c + k, :], res.ident[:])
                last.then_inc(turned, 1)

            turn(0)
            pe.wait_ge(w_in, 32)
            for c in range(NCHUNK):
                if c + 1 < NCHUNK:
                    turn(c + 1)
                pe.wait_ge(copied, c + 1)
                if c >= 2:
                    pe.wait_ge(added, c - 1)
                for k in range(4):
                    y = psY[c % 2][:, k * P:(k + 1) * P]
                    pe.matmul(y, res.ones[0:1, :], bo[:], start=True, stop=False)
                    last = pe.matmul(y, OT[c % 2][:, k * P:(k + 1) * P], wo[:], start=False, stop=True)
                last.then_inc(projected, 1)

        @block.scalar
        def _(act):
            for c in range(NCHUNK):
                act.wait_ge(turned, c + 1)
                if c >= 2:
                    act.wait_ge(projected, c - 1)
                act.copy(OT[c % 2][:], psT[c % 2][:]).then_inc(copied, 1)

        @block.vector
        def _(dve):
            for c in range(NCHUNK):
                dve.wait_ge(projected, c + 1)
                x = res.X[:, 4 * c:4 * c + 4, :].rearrange("p t d -> p (t d)")
                dve.scalar_tensor_tensor(x, psY[c % 2][:], gate, x, ALU.mult, ALU.add).then_inc(added, 1)
            dve.wait_ge(added, NCHUNK)



def experts(nc, io, res, name, E, H, act_fn, weights, biases, out_bias, combine, beside=None):
    HC = H // P
    w1_dram, w2_dram = weights
    HB = max(2, HC)
    with Phase(nc, name) as ph:
        ahead = beside(ph) if beside else None
        w1 = [ph.sb(f"w1_{i}", [P, H]) for i in range(2)]
        w2 = [ph.sb(f"w2_{i}", [P, HC, D]) for i in range(2)]
        b1 = [ph.sb(f"b1_{i}", [P, HC]) for i in range(2)]
        b2 = ph.sb("b2", [E, D])
        hT = [ph.sb(f"hT{i}", [P, HC, CHUNK]) for i in range(2)]
        cT = ph.sb("cT", [E, NTILE, P])
        psH = [ph.ps(f"psH{i}", [P, CHUNK]) for i in range(HB)]
        psY = [ph.ps(f"psY{i}", [P, 4, D]) for i in range(2)]
        w_in = [ph.sem(f"w_in{i}") for i in range(2)]
        b2_in, hidden, acted, made, added = (ph.sem(n) for n in ("b2_in", "hidden", "acted", "made", "added"))
        c_turned, c_copied, b2_made, b2_added = (ph.sem(n) for n in ("c_turned", "c_copied", "b2_made", "b2_added"))
        n_hidden = NCHUNK * HC

        with ph.block() as block:
            @block.sync
            def _(sp):
                def load(e, b):
                    ds = bass.ds(e, 1)
                    sp.dma_start(w1[b][:], w1_dram[ds].rearrange("o p h -> p (o h)")).then_inc(w_in[b], 16)
                    sp.dma_start(w2[b][:], w2_dram[ds].rearrange("o (c p) d -> p (o c) d", p=P)).then_inc(w_in[b], 16)
                    sp.dma_start(b1[b][:], biases[ds].rearrange("o p c -> p (o c)")).then_inc(w_in[b], 16)

                sp.dma_start(b2[:], out_bias).then_inc(b2_in, 16)
                for b in range(2):
                    load(b, b)
                with sp.Fori(1, E // 2) as i:
                    for b in range(2):
                        sp.wait_ge(made, (2 * i + b - 1) * NCHUNK)
                        load(2 * i + b, b)

            @block.tensor
            def _(pe):
                def expert(e, b, first):
                    pe.wait_ge(w_in[b], 48 * (e // 2 + 1) if first else 48 * (first_i[0] + 1))
                    for c in range(NCHUNK + 1):
                        if c < NCHUNK:
                            for k in range(HC):
                                n = c * HC + k
                                bank = n % HB
                                if not first or n >= HB:
                                    pe.wait_ge(acted, e * n_hidden + n - HB + 1)
                                pe.matmul(psH[bank][:], w1[b][:, k * P:(k + 1) * P], res.xnT[:, c * CHUNK:(c + 1) * CHUNK],
                                          start=True, stop=True).then_inc(hidden, 1)
                        if c >= 1:
                            m = c - 1
                            pe.wait_ge(acted, e * n_hidden + c * HC)
                            if not first or m >= 2:
                                pe.wait_ge(added, e * NCHUNK + m - 1)
                            for t in range(4):
                                for k in range(HC):
                                    last = pe.matmul(psY[m % 2][:, t, :], hT[m % 2][:, k, t * P:(t + 1) * P], w2[b][:, k, :],
                                                     start=(k == 0), stop=(k == HC - 1))
                            last.then_inc(made, 1)

                first_i = [0]
                expert(0, 0, True)
                first_i[0] = 0
                expert(1, 1, False)
                with pe.Fori(1, E // 2) as i:
                    first_i[0] = i
                    for b in range(2):
                        expert(2 * i + b, b, False)
                pe.wait_ge(b2_in, 16)
                for c in range(NCHUNK):
                    pe.wait_ge(acted, E * n_hidden)
                    if c >= 2:
                        pe.wait_ge(c_copied, c - 1)
                    for t in range(4):
                        last = pe.transpose(psH[c % 2][0:E, t * P:(t + 1) * P], combine[:, :, 4 * c + t], res.ident[:])
                    last.then_inc(c_turned, 1)
                for c in range(NCHUNK):
                    pe.wait_ge(c_copied, c + 1)
                    pe.wait_ge(added, E * NCHUNK)
                    if c >= 2:
                        pe.wait_ge(b2_added, c - 1)
                    for t in range(4):
                        last = pe.matmul(psY[c % 2][:, t, :], cT[:, 4 * c + t, :], b2[:], start=True, stop=True)
                    last.then_inc(b2_made, 1)

            @block.scalar
            def _(act):
                def expert(e, b, first, i):
                    act.wait_ge(w_in[b], 48 * (i + 1))
                    for c in range(NCHUNK):
                        if not first or c >= 2:
                            act.wait_ge(made, e * NCHUNK + c - 1)
                        for k in range(HC):
                            n = c * HC + k
                            act.wait_ge(hidden, e * n_hidden + n + 1)
                            act.activation(hT[c % 2][:, k, :], psH[n % HB][:], act_fn, bias=b1[b][:, k:k + 1]).then_inc(acted, 1)

                expert(0, 0, True, 0)
                expert(1, 1, False, 0)
                with act.Fori(1, E // 2) as i:
                    for b in range(2):
                        expert(2 * i + b, b, False, i)
                for c in range(NCHUNK):
                    act.wait_ge(c_turned, c + 1)
                    act.copy(cT[:, 4 * c:4 * c + 4, :].rearrange("e t p -> e (t p)"), psH[c % 2][0:E, :]).then_inc(c_copied, 1)

            @block.vector
            def _(dve):
                with dve.Fori(0, E) as e:
                    for c in range(NCHUNK):
                        dve.wait_ge(made, e * NCHUNK + c + 1)
                        for k in range(4):
                            t = 4 * c + k
                            last = dve.scalar_tensor_tensor(res.X[:, t, :], psY[c % 2][:, k, :], combine[:, bass.ds(e, 1), t],
                                                            res.X[:, t, :], ALU.mult, ALU.add)
                        last.then_inc(added, 1)
                for c in range(NCHUNK):
                    dve.wait_ge(b2_made, c + 1)
                    x = res.X[:, 4 * c:4 * c + 4, :]
                    dve.tensor_tensor(x, psY[c % 2][:], x, ALU.add).then_inc(b2_added, 1)
                dve.wait_ge(b2_added, NCHUNK)

            if ahead:
                @block.gpsimd
                def _(pool):
                    ahead.gpsimd(pool)


def route(nc, io, res, name, E, top_k, w_name, b_name, finish):
    EP = max(E, 8)
    with Phase(nc, name) as ph:
        wg = ph.sb("wg", [P, E])
        bg = ph.sb("bg", [P, E])
        iota = ph.sb("iota", [P, E])
        prob = ph.sb("prob", [P, NTILE, E])
        top = ph.sb("top", [P, NTILE])
        den = ph.sb("den", [P, NTILE])
        rec = ph.sb("rec", [P, NTILE])
        val = ph.sb("val", [P, NTILE, 8])
        idx = ph.sb("idx", [P, NTILE, 8], U32)
        idxf = ph.sb("idxf", [P, NTILE, 8])
        onehot = ph.sb("onehot", [P, top_k, NTILE, E])
        psL = ph.ps("psL", [P, NTILE, E])
        w_in, logits, biased, topped, shifted, exped, summed, inverted, normed = (
            ph.sem(n) for n in ("w_in", "logits", "biased", "topped", "shifted", "exped", "summed", "inverted", "normed"))
        sorted_, indexed, floated, hot = (ph.sem(n) for n in ("sorted", "indexed", "floated", "hot"))
        wide = [P, NTILE, E]
        with ph.block() as block:
            @block.sync
            def _(sp):
                sp.dma_start(wg[:], io[w_name]).then_inc(w_in, 16)
                sp.dma_start(iota[:], io["c_iota"][0:E].partition_broadcast(P)).then_inc(w_in, 16)
                if b_name:
                    sp.dma_start(bg[:], io[b_name].partition_broadcast(P)).then_inc(w_in, 16)

            @block.tensor
            def _(pe):
                pe.wait_ge(w_in, 48 if b_name else 32)
                for t in range(NTILE):
                    last = pe.matmul(psL[:, t, :], res.xnT[:, t * P:(t + 1) * P], wg[:], start=True, stop=True)
                last.then_inc(logits, 1)

            @block.scalar
            def _(act):
                act.wait_ge(shifted, 1)
                act.activation(prob[:], prob[:], ACT.Exp).then_inc(exped, 1)

            @block.vector
            def _(dve):
                dve.wait_ge(w_in, 48 if b_name else 32)
                dve.wait_ge(logits, 1)
                if b_name:
                    dve.tensor_tensor(prob[:], psL[:], bg[:].unsqueeze(1).to_broadcast(wide), ALU.add).then_inc(biased, 1)
                else:
                    dve.tensor_copy(prob[:], psL[:]).then_inc(biased, 1)
                dve.wait_ge(biased, 1)
                dve.tensor_reduce(top[:], prob[:], AX.X, ALU.max).then_inc(topped, 1)
                dve.wait_ge(topped, 1)
                dve.tensor_tensor(prob[:], prob[:], top[:].unsqueeze(2).to_broadcast(wide), ALU.subtract).then_inc(shifted, 1)
                dve.wait_ge(exped, 1)
                dve.tensor_reduce(den[:], prob[:], AX.X, ALU.add).then_inc(summed, 1)
                dve.wait_ge(summed, 1)
                dve.reciprocal(rec[:], den[:]).then_inc(inverted, 1)
                dve.wait_ge(inverted, 1)
                dve.tensor_tensor(prob[:], prob[:], rec[:].unsqueeze(2).to_broadcast(wide), ALU.mult).then_inc(normed, 1)
                dve.wait_ge(normed, 1)
                for t in range(NTILE):
                    dve.max(val[:, t, :], prob[:, t, :]).then_inc(sorted_, 1)
                for t in range(NTILE):
                    dve.wait_ge(sorted_, t + 1)
                    dve.max_index(idx[:, t, :], val[:, t, :], prob[:, t, :]).then_inc(indexed, 1)
                dve.wait_ge(indexed, NTILE)
                dve.tensor_copy(idxf[:], idx[:]).then_inc(floated, 1)
                dve.wait_ge(floated, 1)
                for k in range(top_k):
                    dve.tensor_tensor(onehot[:, k], iota[:].unsqueeze(1).to_broadcast(wide),
                                      idxf[:, :, k:k + 1].to_broadcast(wide), ALU.is_equal).then_inc(hot, 1)
                dve.wait_ge(hot, top_k)
        finish(ph, prob, val, idxf, onehot)


L0_EXPERTS, L0_HIDDEN, L0_CAPACITY = 8, 512, 256
ROW_HALVES = L0_CAPACITY // P


def layer0_experts(nc, io, res):
    E = L0_EXPERTS
    with Phase(nc, "f0") as outer:
        xn_dram = nc.dram_tensor("f0_xn", [NTILE * P, D], F32).ap()
        weight = outer.sb("weight", [P, 2, NTILE])
        row = outer.sb("row", [P, 2, NTILE], I32)
        token = outer.sb("token", [P, ROW_HALVES, E], I32)
        route(nc, io, res, "f0r", E, 2, "L0_Wg", None,
              lambda ph, prob, val, idxf, onehot: queue_up(nc, io, res, ph, val, idxf, onehot, xn_dram, weight, row, token))
        queued_experts(nc, io, res, xn_dram, weight, row, token)


def queue_up(nc, io, res, ph, val, idxf, onehot, xn_dram, weight, row, token):
    E, capacity = L0_EXPERTS, L0_CAPACITY
    wide, flat = [P, NTILE, E], [P, 2, NTILE]
    tri = ph.sb("tri", [P, P])
    lane = ph.sb("lane", [P, 1])
    tile_no = ph.sb("tile_no", [P, NTILE])
    place_no_f, place_no = ph.sb("place_no_f", [P, capacity]), ph.sb("place_no", [P, capacity], BF16)
    psC = [ph.ps(f"psC{k}", wide) for k in range(2)]
    psT = ph.ps("psT", [P, E])
    psTab = ph.ps("psTab", [2 * E, capacity])
    psI = ph.ps("psI", [P, ROW_HALVES, 2 * E])
    first, pair, inv = ph.sb("first", [P, E]), ph.sb("pair", [P, NTILE]), ph.sb("inv", [P, NTILE])
    count = ph.sb("count", [P, 2, NTILE, E])
    place, kept, slot = ph.sb("place", flat), ph.sb("kept", flat), ph.sb("slot", flat)
    parts = ph.sb("parts", [P, 2, NTILE, 2, E], BF16)
    hot = ph.sb("hot", [P, 2, NTILE, capacity], BF16)
    table = ph.sb("table", [2 * E, capacity])
    tile_rows = ph.sb("tile_rows", [P, ROW_HALVES, E])
    const_in, xn_out = ph.sem("const_in"), ph.sem("xn_out")
    counted, step, parts_made, hot_made = ph.sem("counted"), ph.sem("step"), ph.sem("parts_made"), ph.sem("hot_made")
    tabled, table_out, table_turned = ph.sem("tabled"), ph.sem("table_out"), ph.sem("table_turned")
    iota_cast, row_made = ph.sem("iota_cast"), ph.sem("row_made")
    with ph.block() as block:
        @block.sync
        def _(sp):
            sp.dma_start(tri[:], io["c_tri"]).then_inc(const_in, 16)
            sp.dma_start(lane[:], io["c_lane"].unsqueeze(1)).then_inc(const_in, 16)
            sp.dma_start(tile_no[:], io["c_iota"].partition_broadcast(P)).then_inc(const_in, 16)
            sp.dma_start(place_no_f[:], io["c_place"].partition_broadcast(P)).then_inc(const_in, 16)
            sp.dma_start(xn_dram.rearrange("(t p) d -> p t d", p=P), res.xn[:]).then_inc(xn_out, 16)
            sp.wait_ge(xn_out, 16)

        @block.scalar
        def _(act):
            act.wait_ge(const_in, 64)
            act.copy(place_no[:], place_no_f[:]).then_inc(iota_cast, 1)

        @block.tensor
        def _(pe):
            pe.wait_ge(const_in, 64)
            for t in range(NTILE):
                last = pe.matmul(psT[:], res.ones[:], onehot[:, 0, t, :], start=(t == 0), stop=(t == NTILE - 1))
            last.then_inc(counted, 1)
            for k in range(2):
                pe.matmul(psC[k][:], tri[:], onehot[:, k], start=True, stop=False, skip_group_check=True)
                for t in range(NTILE - 1):
                    last = pe.matmul(psC[k][:, t + 1:, :], res.ones[:], onehot[:, k, t:t + 1, :].to_broadcast([P, NTILE - 1 - t, E]),
                                     start=False, stop=(t == NTILE - 2), skip_group_check=True)
                last.then_inc(counted, 1)
            pe.wait_ge(parts_made, 4)
            for k in range(2):
                for t in range(NTILE):
                    pe.wait_ge(hot_made, k * NTILE + t + 1)
                    last = pe.matmul(psTab[:], parts[:, k, t].rearrange("p c e -> p (c e)"), hot[:, k, t, :],
                                     start=(k == 0 and t == 0), stop=(k == 1 and t == NTILE - 1))
            last.then_inc(tabled, 1)
            pe.wait_ge(table_out, 1)
            for half in range(ROW_HALVES):
                last = pe.transpose(psI[:, half, :], table[:, half * P:(half + 1) * P], res.ident[0:2 * E, 0:2 * E])
            last.then_inc(table_turned, 1)

        @block.gpsimd
        def _(pool):
            pool.wait_ge(const_in, 64)
            for k in range(2):
                pool.tensor_tensor(parts[:, k, :, 0, :], onehot[:, k], tile_no[:].unsqueeze(2).to_broadcast(wide), ALU.mult).then_inc(parts_made, 1)
                pool.tensor_tensor(parts[:, k, :, 1, :], onehot[:, k], lane[:].unsqueeze(2).to_broadcast(wide), ALU.mult).then_inc(parts_made, 1)

        @block.vector
        def _(dve):
            dve.tensor_tensor(pair[:], val[:, :, 0], val[:, :, 1], ALU.add).then_inc(step, 1)
            dve.wait_ge(step, 1)
            dve.tensor_scalar(pair[:], pair[:], 1e-9, None, ALU.add).then_inc(step, 1)
            dve.wait_ge(step, 2)
            dve.reciprocal(inv[:], pair[:]).then_inc(step, 1)
            dve.wait_ge(step, 3)
            for k in range(2):
                dve.scalar_tensor_tensor(weight[:, k], val[:, :, k], res.gates[:, 4:5], inv[:], ALU.mult, ALU.mult).then_inc(step, 1)
            dve.wait_ge(iota_cast, 1)
            dve.wait_ge(counted, 1)
            dve.tensor_scalar(first[:], psT[:], float(capacity), None, ALU.min).then_inc(step, 1)
            dve.wait_ge(step, 6)
            for k in range(2):
                done = 6 + 4 * k
                dve.wait_ge(counted, 2 + k)
                if k == 0:
                    dve.tensor_tensor(count[:, 0], psC[0][:], onehot[:, 0], ALU.mult).then_inc(step, 1)
                else:
                    dve.tensor_tensor(count[:, 1], psC[1][:], first[:].unsqueeze(1).to_broadcast(wide), ALU.add).then_inc(step, 1)
                    dve.wait_ge(step, done + 1)
                    dve.tensor_tensor(count[:, 1], count[:, 1], onehot[:, 1], ALU.mult).then_inc(step, 1)
                    done += 1
                dve.wait_ge(step, done + 1)
                dve.tensor_reduce(place[:, k], count[:, k], AX.X, ALU.add).then_inc(step, 1)
                dve.wait_ge(step, done + 2)
                dve.tensor_scalar(kept[:, k], place[:, k], float(capacity), None, ALU.is_le).then_inc(step, 1)
                dve.tensor_scalar(slot[:, k], place[:, k], 1.0, None, ALU.subtract).then_inc(step, 1)
                dve.wait_ge(step, done + 4)
                for t in range(NTILE):
                    dve.tensor_scalar(hot[:, k, t, :], place_no[:], slot[:, k, t:t + 1], None, ALU.is_equal).then_inc(hot_made, 1)
            done = 15
            for k in range(2):
                dve.scalar_tensor_tensor(place[:, k], idxf[:, :, k], float(capacity), slot[:, k], ALU.mult, ALU.add).then_inc(step, 1)
                dve.tensor_tensor(weight[:, k], weight[:, k], kept[:, k], ALU.mult).then_inc(step, 1)
            dve.wait_ge(step, done + 4)
            dve.wait_ge(hot_made, 2 * NTILE)
            dve.tensor_tensor(slot[:], place[:], kept[:], ALU.mult).then_inc(step, 1)
            dve.wait_ge(step, done + 5)
            dve.tensor_copy(row[:], slot[:]).then_inc(row_made, 1)
            dve.wait_ge(tabled, 1)
            dve.tensor_copy(table[:], psTab[:]).then_inc(table_out, 1)
            dve.wait_ge(table_turned, 1)
            dve.tensor_scalar(tile_rows[:], psI[:, :, 0:E], float(P), None, ALU.mult).then_inc(step, 1)
            dve.wait_ge(step, done + 6)
            dve.tensor_tensor(tile_rows[:], tile_rows[:], psI[:, :, E:2 * E], ALU.add).then_inc(step, 1)
            dve.wait_ge(step, done + 7)
            dve.tensor_copy(token[:], tile_rows[:]).then_inc(row_made, 1)
            dve.wait_ge(row_made, 2)


def queued_experts(nc, io, res, xn_dram, weight, row, token):
    E, H = L0_EXPERTS, L0_HIDDEN
    HC = H // P
    C = L0_CAPACITY
    GROUP = 4
    with Phase(nc, "f0e") as ph:
        y_dram = nc.dram_tensor("f0_y", [E * C, D], F32).ap()
        w1 = [ph.sb(f"w1_{i}", [P, H]) for i in range(2)]
        w2 = [ph.sb(f"w2_{i}", [P, HC, D]) for i in range(2)]
        b1 = [ph.sb(f"b1_{i}", [P, HC]) for i in range(2)]
        b2 = [ph.sb(f"b2_{i}", [1, D]) for i in range(2)]
        xg = ph.sb("xg", [P, E, ROW_HALVES, D])
        xgT = [ph.sb(f"xgT{i}", [P, C]) for i in range(2)]
        hT = [ph.sb(f"hT{i}", [P, HC, C]) for i in range(2)]
        y = [ph.sb(f"y{i}", [P, ROW_HALVES, D]) for i in range(2)]
        yg = ph.sb("yg", [P, NTILE, 2, D])
        psT = [ph.ps(f"psT{i}", [P, C]) for i in range(2)]
        psH = [ph.ps(f"psH{i}", [P, C]) for i in range(4)]
        psY = [ph.ps(f"psY{i}", [P, ROW_HALVES, D]) for i in range(2)]
        w_in, x_in = [ph.sem(f"w_in{i}") for i in range(2)], [ph.sem(f"x_in{e}") for e in range(E)]
        turned, x_copied, hidden, acted = ph.sem("turned"), ph.sem("x_copied"), ph.sem("hidden"), ph.sem("acted")
        made, y_copied, y_stored = ph.sem("made"), ph.sem("y_copied"), [ph.sem(f"y_stored{i}") for i in range(2)]
        y_in = [ph.sem(f"y_in{g}") for g in range(2 * NTILE // GROUP)]
        added = ph.sem("added")
        with ph.block() as block:
            @block.sync
            def _(sp):
                def load(e, b):
                    one = bass.ds(e, 1)
                    sp.dma_start(w1[b][:], io["L0_W1"][one].rearrange("o d h -> d (o h)")).then_inc(w_in[b], 16)
                    sp.dma_start(w2[b][:], io["L0_W2"][one].rearrange("o (k p) d -> p (o k) d", p=P)).then_inc(w_in[b], 16)
                    sp.dma_start(b1[b][:], io["L0_b1"][one].rearrange("o p k -> p (o k)")).then_inc(w_in[b], 16)
                    sp.dma_start(b2[b][:], io["L0_b2"][one]).then_inc(w_in[b], 16)

                def store(e, b):
                    sp.wait_ge(y_copied, e + 1)
                    sp.dma_start(y_dram[bass.ds(e * C, C)].rearrange("(r p) d -> p r d", p=P), y[b][:]).then_inc(y_stored[b], 16)

                load(0, 0)
                load(1, 1)
                with sp.Fori(1, E // 2) as i:
                    for b in range(2):
                        store(2 * (i - 1) + b, b)
                        load(2 * i + b, b)
                for b in range(2):
                    store(E - 2 + b, b)

            @block.gpsimd
            def _(pool):
                for e in range(E):
                    for r in range(ROW_HALVES):
                        pool.indirect_dma_start(out=xg[:, e, r, :], out_offset=None, in_=xn_dram,
                                                in_offset=bass.IndirectOffsetOnAxis(ap=token[:, r, e:e + 1], axis=0)).then_inc(x_in[e], 16)
                for b in range(2):
                    pool.wait_ge(y_stored[b], 16 * (E // 2))
                for t in range(NTILE):
                    for k in range(2):
                        pool.indirect_dma_start(out=yg[:, t, k, :], out_offset=None, in_=y_dram,
                                                in_offset=bass.IndirectOffsetOnAxis(ap=row[:, k, t:t + 1], axis=0)).then_inc(y_in[(2 * t + k) // GROUP], 16)

            @block.tensor
            def _(pe):
                def turn(e):
                    pe.wait_ge(x_in[e], 16 * ROW_HALVES)
                    if e >= 2:
                        pe.wait_ge(x_copied, e - 1)
                    for r in range(ROW_HALVES):
                        last = pe.transpose(psT[e % 2][:, r * P:(r + 1) * P], xg[:, e, r, :], res.ident[:])
                    last.then_inc(turned, 1)

                turn(0)
                for e in range(E):
                    b = e % 2
                    if e + 1 < E:
                        turn(e + 1)
                    pe.wait_ge(w_in[b], 64 * (e // 2 + 1))
                    pe.wait_ge(x_copied, e + 1)
                    for k in range(HC):
                        if e > 0:
                            pe.wait_ge(acted, (e - 1) * HC + k + 1)
                        pe.matmul(psH[k][:], w1[b][:, k * P:(k + 1) * P], xgT[b][:], start=True, stop=True).then_inc(hidden, 1)
                    if e >= 2:
                        pe.wait_ge(y_copied, e - 1)
                    for r in range(ROW_HALVES):
                        pe.matmul(psY[b][:, r, :], res.ones[0:1, :], b2[b][:], start=True, stop=False)
                        for k in range(HC):
                            pe.wait_ge(acted, e * HC + k + 1)
                            last = pe.matmul(psY[b][:, r, :], hT[b][:, k, r * P:(r + 1) * P], w2[b][:, k, :], start=False, stop=(k == HC - 1))
                    last.then_inc(made, 1)

            @block.scalar
            def _(act):
                for e in range(E):
                    b = e % 2
                    act.wait_ge(w_in[b], 64 * (e // 2 + 1))
                    if e >= 2:
                        act.wait_ge(made, e - 1)
                    for k in range(HC):
                        act.wait_ge(hidden, e * HC + k + 1)
                        act.activation(hT[b][:, k, :], psH[k][:], ACT.Gelu_apprx_tanh, bias=b1[b][:, k:k + 1]).then_inc(acted, 1)

            @block.vector
            def _(dve):
                def copy_x(e):
                    dve.wait_ge(turned, e + 1)
                    if e >= 2:
                        dve.wait_ge(hidden, (e - 1) * HC)
                    dve.tensor_copy(xgT[e % 2][:], psT[e % 2][:]).then_inc(x_copied, 1)

                copy_x(0)
                for e in range(E):
                    if e + 1 < E:
                        copy_x(e + 1)
                    dve.wait_ge(made, e + 1)
                    if e >= 2:
                        dve.wait_ge(y_stored[e % 2], 16 * (e // 2))
                    dve.tensor_copy(y[e % 2][:], psY[e % 2][:]).then_inc(y_copied, 1)
                for t in range(NTILE):
                    for k in range(2):
                        n = 2 * t + k
                        if n % GROUP == 0:
                            dve.wait_ge(y_in[n // GROUP], 16 * GROUP)
                        if k == 1:
                            dve.wait_ge(added, n)
                        dve.scalar_tensor_tensor(res.X[:, t, :], yg[:, t, k, :], weight[:, k, t:t + 1], res.X[:, t, :],
                                                 ALU.mult, ALU.add).then_inc(added, 1)
                dve.wait_ge(added, 2 * NTILE)


def layer2_experts(nc, io, res):
    E, top_k = 15, 3
    with Phase(nc, "f2") as outer:
        combine = outer.sb("combine", [P, E + 1, NTILE])

        def chosen(ph, prob, val, idxf, onehot):
            mask = ph.sb("mask", [P, NTILE, E])
            step = ph.sem("step")
            with ph.block() as block:
                @block.vector
                def _(dve):
                    dve.tensor_copy(combine[:, 0, :], res.gates[:, 6:7].to_broadcast([P, NTILE])).then_inc(step, 1)
                    dve.tensor_tensor(mask[:], onehot[:, 0], onehot[:, 1], ALU.add).then_inc(step, 1)
                    dve.wait_ge(step, 2)
                    dve.tensor_tensor(mask[:], mask[:], onehot[:, 2], ALU.add).then_inc(step, 1)
                    dve.wait_ge(step, 3)
                    dve.scalar_tensor_tensor(combine[:, 1:, :].rearrange("p e t -> p t e"), mask[:], res.gates[:, 6:7], prob[:],
                                             ALU.mult, ALU.mult).then_inc(step, 1)
                    dve.wait_ge(step, 4)

        route(nc, io, res, "f2r", E, top_k, "L2_router_W", "L2_router_b", chosen)
        experts(nc, io, res, "f2e", E + 1, D, ACT.Relu, (io["L2_W1"], io["L2_W2"]), io["L2_b1"], io["L2_b2"], combine,
                beside=lambda ph: MaskConstants(ph, res.narrow, io))



HEAD_E = D // HEADS
PAIRS = HEADS // 2
PAIR_ROWS = 2 * HEAD_E
COMBOS = ((0, 0), (0, 1), (0, 2), (1, 0), (1, 1), (2, 0))
COMBO_ROWS = len(COMBOS) * PAIR_ROWS
RING = 3
V_COLS = 32
SLOT = HEAD_E + 1
QUAD = 4
QUADS = HEADS // QUAD
HALF = HEADS // 2


class LayerTwo:
    name, weights, keys, q_bias = "a2", "L2", 0, False
    scale = 1.0 / float(np.sqrt(HEAD_E))
    gate, sink, slopes = 2, 1.0, True


class LayerThree:
    name, weights, keys, q_bias = "a3", "L3", 1, True
    scale = float(D) ** -0.5
    gate, sink, slopes = 3, 0.0, False


class NarrowBuffers:

    def __init__(self, nc, ph):
        self.k_op = [ph.sb(f"k_op{i}", [P, PAIRS, S2], BF16) for i in range(RING)]
        self.q_op = [ph.sb(f"q_op{i}", [P, HEADS, S], BF16) for i in range(RING)]
        self.values = [ph.sb(f"values{i}", [P, KT, HEADS, V_COLS]) for i in range(RING)]
        self.wq, self.wv, self.wo = ([ph.sb(f"{n}{i}", [P, D]) for i in range(2)] for n in ("wq", "wv", "wo"))
        self.bq, self.bv, self.bo = ph.sb("bq", [P, 1]), ph.sb("bv", [P, 1]), ph.sb("bo", [1, D])
        self.pos_scr = nc.dram_tensor("pos_parts", [B, 3, S2], BF16).ap()

    def add_masks(self, ph):
        self.tri, self.triT = ph.sb("tri", [P, QT, S2], BF16), ph.sb("triT", [P, KT, S], BF16)
        self.padT, self.pad = ph.sb("padT", [P, B, KT]), ph.sb("pad", [P, B, S2], BF16)


class NarrowConstants:

    def __init__(self, ph, nb):
        self.nb = nb
        self.slopes, self.slopes_b = ph.sb("slopes", [9, HEADS, S]), ph.sb("slopes_b", [9, HEADS, S], BF16)
        self.pos = ph.sb("pos", [B, S2], I32)
        self.posf, self.posr = ph.sb("posf", [B, S2]), ph.sb("posr", [B, S2])
        self.pos_parts = ph.sb("pos_parts", [B, 3, S2], BF16)
        self.const_in, self.zeroed, self.filled, self.ones_set = (ph.sem(n) for n in ("const_in", "zeroed", "filled", "ones_set"))
        self.slopes_cut, self.pos_cut, self.placed, self.weights_in = (ph.sem(n) for n in ("slopes_cut", "pos_cut", "placed", "weights_in"))

    def sync(self, sp, io):
        nb = self.nb
        sp.dma_start(self.pos[:], io["key_pos"]).then_inc(self.const_in, 16)
        sp.dma_start(self.slopes[:], io["c_slopes"]).then_inc(self.const_in, 16)
        for i, w in enumerate(("L2", "L3")):
            for tile, name in ((nb.wq, "_WqT"), (nb.wv, "_WvT"), (nb.wo, "_WoT")):
                sp.dma_start(tile[i][:], io[w + name]).then_inc(self.weights_in, 16)
        sp.dma_start(nb.bq[:], io["L3_bq"].unsqueeze(1)).then_inc(self.weights_in, 16)
        sp.dma_start(nb.bv[:], io["L3_bv"].unsqueeze(1)).then_inc(self.weights_in, 16)
        sp.dma_start(nb.bo[:], io["L3_bo"].unsqueeze(0)).then_inc(self.weights_in, 16)
        sp.wait_ge(self.pos_cut, 5)
        sp.dma_start(nb.pos_scr, self.pos_parts[:]).then_inc(self.placed, 16)
        sp.wait_ge(self.slopes_cut, 1)
        sp.wait_ge(self.zeroed, RING)
        for r in range(RING):
            sp.dma_start(nb.q_op[r][COMBO_ROWS:COMBO_ROWS + 9], self.slopes_b[:]).then_inc(self.placed, 16)
        sp.wait_ge(self.placed, 16 * (RING + 1))
        sp.wait_ge(self.weights_in, 16 * 9)

    def scalar(self, act):
        act.wait_ge(self.const_in, 32)
        act.copy(self.slopes_b[:], self.slopes[:]).then_inc(self.slopes_cut, 1)
        act.wait_ge(self.slopes_cut, 1)

    def vector(self, dve):
        p0, p1, p2 = (self.pos_parts[:, k, :] for k in range(3))
        cut = self.pos_cut
        for r in range(RING):
            dve.memset(self.nb.q_op[r][:], 0.0).then_inc(self.zeroed, 1)
        dve.wait_ge(self.const_in, 32)
        dve.tensor_copy(self.posf[:], self.pos[:]).then_inc(cut, 1)
        dve.wait_ge(cut, 1)
        dve.tensor_copy(p0, self.posf[:]).then_inc(cut, 1)
        dve.wait_ge(cut, 2)
        dve.tensor_tensor(self.posr[:], self.posf[:], p0, ALU.subtract).then_inc(cut, 1)
        dve.wait_ge(cut, 3)
        dve.tensor_copy(p1, self.posr[:]).then_inc(cut, 1)
        dve.wait_ge(cut, 4)
        dve.tensor_tensor(p2, self.posr[:], p1, ALU.subtract).then_inc(cut, 1)

    def gpsimd(self, pool):
        nb = self.nb
        for r in range(RING):
            pool.memset(nb.values[r][:], 0.0).then_inc(self.filled, 1)
            pool.memset(nb.k_op[r][:], 1.0).then_inc(self.filled, 1)
        pool.wait_ge(self.filled, 2 * RING)
        for r in range(RING):
            for s in range(2):
                heads = nb.values[r][:].rearrange("p k (g s j) m -> p (k g) s j m", g=2, s=2)[:, :, s, :, s * SLOT + HEAD_E]
                pool.memset(heads, 1.0).then_inc(self.ones_set, 1)
        pool.wait_ge(self.ones_set, 2 * RING)


class MaskConstants:

    def __init__(self, ph, nb, io):
        self.nb, self.io = nb, io
        self.tri_i, self.triT_i = ph.sb("tri_i", [P, QT, S2], U8), ph.sb("triT_i", [P, KT, S], U8)
        self.padT_i, self.pad_i = ph.sb("padT_i", [P, B, KT], U8), ph.sb("pad_i", [P, B, S2], U8)
        self.mask_in, self.mask_done = ph.sem("mask_in"), ph.sem("mask_done")

    def gpsimd(self, pool):
        nb, io = self.nb, self.io
        pool.dma_start(self.tri_i[:], io["tri"].rearrange("(t p) k -> p t k", p=P)).then_inc(self.mask_in, 16)
        pool.dma_start(self.triT_i[:], io["triT"].rearrange("(t p) q -> p t q", p=P)).then_inc(self.mask_in, 16)
        pool.dma_start(self.padT_i[:], io["padT"]).then_inc(self.mask_in, 16)
        pool.dma_start(self.pad_i[:].rearrange("p b k -> p (b k)"), io["pad"].partition_broadcast(P)).then_inc(self.mask_in, 16)
        for r in range(RING):
            pool.memset(nb.k_op[r][COMBO_ROWS:P], 1.0).then_inc(self.mask_done, 1)
        pool.wait_ge(self.mask_done, RING)
        pool.wait_ge(self.mask_in, 64)
        pool.tensor_scalar(nb.tri[:], self.tri_i[:], BIG, None, ALU.mult).then_inc(self.mask_done, 1)
        pool.tensor_scalar(nb.triT[:], self.triT_i[:], BIG, None, ALU.mult).then_inc(self.mask_done, 1)
        pool.tensor_copy(nb.padT[:], self.padT_i[:]).then_inc(self.mask_done, 1)
        pool.tensor_copy(nb.pad[:], self.pad_i[:]).then_inc(self.mask_done, 1)
        pool.wait_ge(self.mask_done, RING + 4)


def narrow_attention(nc, io, res, cfg):
    rows = COMBO_ROWS + (9 if cfg.slopes else 0)
    with Phase(nc, cfg.name) as ph:
        qs = nc.dram_tensor(cfg.name + "_qs", [B, 3, D, S], BF16).ap()
        ks = res.keys[cfg.keys]
        nb = res.narrow
        k_op, q_op, values, wq, wv, wo = nb.k_op, nb.q_op, nb.values, nb.wq[cfg.keys], nb.wv[cfg.keys], nb.wo[cfg.keys]
        bias_row, bqs = ph.sb("bias_row", [1, D]), ph.sb("bqs", [P, 1])
        y = [ph.sb(f"y{i}", [P, CHUNK]) for i in range(2)]
        y_rest = ph.sb("y_rest", [P, CHUNK])
        y_parts = [ph.sb(f"y_parts{i}", [P, 3, CHUNK], BF16) for i in range(2)]
        cT = [ph.sb(f"cT{i}", [P, S2]) for i in range(RING)]
        madd = [ph.sb(f"madd{i}", [P, QT, S2], BF16) for i in range(RING)]
        maddT = [ph.sb(f"maddT{i}", [P, KT, S], BF16) for i in range(RING)]
        mx = [ph.sb(f"mx{i}", [P, HEADS * QT]) for i in range(RING)]
        max_rest = ph.sb("max_rest", [HALF * QT, P])
        max_parts = [ph.sb(f"max_parts{i}", [HALF * QT, 3, P], BF16) for i in range(2)]
        probs = [ph.sb(f"probs{i}", [P, KT, S]) for i in range(2 * QUAD)]
        OT = ph.sb("OT", [P, 2, S])
        den, rec = ph.sb("den", [P, 4, 4, 2]), ph.sb("rec", [P, 4, 4, 2])
        A = ph.sb("A", [P, QT, D])
        AT = ph.sb("AT", [P, S])
        junk = [ph.sb(f"junk{i}", [P, S2], BF16) for i in range(2)]
        carrier = [ph.sb(f"carrier{i}", [P, 1]) for i in range(2)]
        if cfg.slopes:
            mask_i = [ph.sb(f"mask{i}", [P, QT, S2], I32) for i in range(RING)]
            maskT_i = [ph.sb(f"maskT{i}", [P, KT, S], I32) for i in range(RING)]
        else:
            tri, triT, padT, pad = nb.tri, nb.triT, nb.padT, nb.pad
            padT_now = [ph.sb(f"padT_now{i}", [P, KT]) for i in range(RING)]

        psM = [ph.ps(f"psM{i}", [P, S2]) for i in range(2)]
        psE = [ph.ps(f"psE{i}", [P, KT, S]) for i in range(2)]
        psO = ph.ps("psO", [P, 2, S])
        psX = ph.ps("psX", [P, CHUNK])

        n_loads = 3 * len(COMBOS) + 1 + 3 * cfg.slopes
        biased, split, stored = ph.sem("biased"), ph.sem("split"), [ph.sem(f"stored{i}") for i in range(2)]
        query_made, bias_scaled, bias_made, row_done = (ph.sem(n) for n in ("query_made", "bias_scaled", "bias_made", "row_done"))
        mask_in = [ph.sem(f"mask_in{i}") for i in range(RING)]
        loaded = [ph.sem(f"loaded{i}") for i in range(RING)]
        masked = ph.sem("masked")
        max_scored, max_read = ph.sem("max_scored"), ph.sem("max_read")
        max_turned, max_split = ph.sem("max_turned"), ph.sem("max_split")
        max_in = [ph.sem(f"max_in{i}") for i in range(2)]
        v_made, v_out = ph.sem("v_made"), ph.sem("v_out")
        scored, exped, weighted = ph.sem("scored"), ph.sem("exped"), ph.sem("weighted")
        out_read, out_turned, den_done, rec_done, normed = (ph.sem(n) for n in ("out_read", "out_turned", "den_done", "rec_done", "normed"))
        back_turned, back_copied, projected, added = (ph.sem(n) for n in ("back_turned", "back_copied", "projected", "added"))
        pad_taken, pad_mixed = ph.sem("pad_taken"), ph.sem("pad_mixed")

        MAX_SLOTS, READ_SLOT, OUT_SLOT, BACK_SLOT, PROJECT_SLOT, V_SLOT = (10, 1), 3, 5, 7, 9, 12
        n_split = 4

        def steps(eng, step):
            step(0, 0, 0)
            step(1, 1, 0)
            with eng.Fori(0, (B - 2) // RING) as i:
                for k in range(RING):
                    step(RING * i + 2 + k, (2 + k) % RING, i + (2 + k) // RING, inner=True)
            step(B, B % RING, 0)

        with ph.block() as block:
            @block.sync
            def _(sp):
                def load_masks(u, r):
                    if cfg.slopes:
                        one = bass.ds(u, 1)
                        sp.dma_start(mask_i[r][:], io["mask"][one].rearrange("o (t p) k -> p (o t) k", p=P)).then_inc(mask_in[r], 16)
                        sp.dma_start(maskT_i[r][:], io["maskT"][one].rearrange("o (t p) q -> p (o t) q", p=P)).then_inc(mask_in[r], 16)

                def load_keys(u, r):
                    one = bass.ds(u, 1)
                    for c, (cq, ck) in enumerate(COMBOS):
                        rows_c = slice(c * PAIR_ROWS, (c + 1) * PAIR_ROWS)
                        sp.dma_start(k_op[r][rows_c], ks[one, ck].rearrange("o (t r) k -> (o r) t k", r=PAIR_ROWS)).then_inc(loaded[r], 16)
                    if cfg.slopes:
                        for a in range(3):
                            at = COMBO_ROWS + 3 * a
                            sp.dma_start(k_op[r][at:at + 3], nb.pos_scr[one].rearrange("o c k -> (o c) k").unsqueeze(1).to_broadcast([3, PAIRS, S2])).then_inc(loaded[r], 16)
                    sp.dma_start(cT[r][:], io["ctxT"][:, bass.ds(u * S2, S2)]).then_inc(loaded[r], 16)

                def load_queries(u, r):
                    one = bass.ds(u, 1)
                    for c, (cq, ck) in enumerate(COMBOS):
                        for j in range(2):
                            rows_j = slice(c * PAIR_ROWS + j * HEAD_E, c * PAIR_ROWS + (j + 1) * HEAD_E)
                            sp.dma_start(q_op[r][rows_j, j::2, :],
                                         qs[one, cq].rearrange("o (t j e) q -> j (o e) t q", j=2, e=HEAD_E)[j]).then_inc(loaded[r], 16)

                def store_queries(n):
                    sp.wait_ge(split, 4 * n + 4)
                    for b in range(2):
                        sp.dma_start(qs[2 * n + b].rearrange("c f q -> f c q"), y_parts[n % 2][:, :, b * S:(b + 1) * S]).then_inc(stored[n % 2], 16)

                def maxima(v, r, half):
                    sp.wait_ge(max_split, (2 * v + half + 1) * n_split)
                    for c in range(3):
                        sp.dma_start(q_op[r][rows + c:rows + c + 1, half * HALF:(half + 1) * HALF, :].rearrange("o h (t q) -> o (h t) q", q=P),
                                     max_parts[half][:, c, :]).then_inc(max_in[half], 16)

                load_masks(0, 0)
                load_keys(0, 0)
                store_queries(0)
                sp.wait_ge(stored[0], 32)
                load_queries(0, 0)
                load_masks(1, 1)
                load_keys(1, 1)
                load_queries(1, 1)
                for n in range(1, NCHUNK):
                    store_queries(n)
                for i in range(2):
                    sp.wait_ge(stored[i], 16 * NCHUNK)
                maxima(0, 0, 0)
                maxima(0, 0, 1)
                with sp.Fori(0, (B - 2) // RING) as i:
                    for k in range(RING):
                        v, r = RING * i + 2 + k, (2 + k) % RING
                        sp.wait_ge(exped, (v - 2) * HEADS + 1)
                        load_masks(v, r)
                        load_keys(v, r)
                        load_queries(v, r)
                        maxima(v - 1, (r - 1) % RING, 0)
                        maxima(v - 1, (r - 1) % RING, 1)
                maxima(B - 1, (B - 1) % RING, 0)
                maxima(B - 1, (B - 1) % RING, 1)

            @block.gpsimd
            def _(pool):
                def masks(u, r, turn, first):
                    if cfg.slopes:
                        pool.wait_ge(mask_in[r], 32 * (turn + 1))
                    if not first:
                        pool.wait_ge(exped, (u - RING + 1) * HEADS)
                    if cfg.slopes:
                        pool.tensor_scalar(madd[r][:], mask_i[r][:], 0.0, -BIG, ALU.is_equal, ALU.mult).then_inc(masked, 1)
                        pool.tensor_scalar(maddT[r][:], maskT_i[r][:], 0.0, -BIG, ALU.is_equal, ALU.mult).then_inc(masked, 1)
                    else:
                        pool.tensor_copy(padT_now[r][:], padT[:, bass.ds(u, 1), :].rearrange("p o k -> p (o k)")).then_inc(pad_taken, 1)
                        pool.tensor_tensor(madd[r][:], tri[:], pad[:, bass.ds(u, 1), :].to_broadcast([P, QT, S2]), ALU.mult).then_inc(pad_mixed, 1)
                        pool.wait_ge(pad_mixed, u + 1)
                        pool.tensor_scalar(madd[r][:], madd[r][:], BIG, None, ALU.subtract).then_inc(masked, 1)
                        pool.wait_ge(pad_taken, u + 1)
                        for t in range(KT):
                            last = pool.tensor_scalar(maddT[r][:, t, :], triT[:, t, :], padT_now[r][:, t:t + 1], BIG, ALU.mult, ALU.subtract)
                        last.then_inc(masked, 1)

                for u in range(RING):
                    masks(u, u, 0, True)
                with pool.Fori(1, 2) as i:
                    for r in range(RING):
                        masks(RING * i + r, r, i, False)
                for u in range(2 * RING, B):
                    masks(u, u % RING, u // RING, False)

            @block.tensor
            def _(pe):
                for n in range(NCHUNK):
                    if n >= 2:
                        pe.wait_ge(biased, n - 1)
                    pe.matmul(psM[n % 2][:], wq[:], res.xnT[:, n * CHUNK:(n + 1) * CHUNK], start=True, stop=True).then_inc(query_made, 1)
                if cfg.q_bias:
                    pe.matmul(psX[0:1, 0:D], nb.bv[:], wo[:], start=True, stop=True).then_inc(bias_made, 1)
                pe.wait_ge(biased, NCHUNK)

                def turn_out(u):
                    pe.wait_ge(out_read, u + 1)
                    for t in range(QT):
                        for g in range(2):
                            n = t * 2 + g
                            last = pe.transpose(psX[:, n * P:(n + 1) * P], OT[:, g, t * P:(t + 1) * P], res.ident[:])
                    last.then_inc(out_turned, 1)

                def turn_back(u):
                    pe.wait_ge(normed, 2 * u + 2)
                    for t in range(QT):
                        last = pe.transpose(psX[:, t * P:(t + 1) * P], A[:, t, :], res.ident[:])
                    last.then_inc(back_turned, 1)

                def project(u):
                    pe.wait_ge(back_copied, u + 1)
                    for t in range(QT):
                        y = psX[:, t * P:(t + 1) * P]
                        if cfg.q_bias:
                            if t == 0:
                                pe.wait_ge(row_done, 1)
                            pe.matmul(y, res.ones[0:1, :], bias_row[:], start=True, stop=False)
                        last = pe.matmul(y, AT[:, t * P:(t + 1) * P], wo[:], start=not cfg.q_bias, stop=True)
                    last.then_inc(projected, 1)

                def maximum(v, r, h, t, first):
                    n = QT * h + t
                    if not (first and n < 2):
                        pe.wait_ge(max_read, v * HEADS * QT + n - 1)
                    pe.matmul(psM[t][:], q_op[r][0:rows, h, t * P:(t + 1) * P], k_op[r][0:rows, h // 2, :],
                              start=True, stop=True).then_inc(max_scored, 1)

                def turn_maxima(v, r, half):
                    pe.wait_ge(max_read, (v * HEADS + (half + 1) * HALF) * QT)
                    pe.transpose(psX[0:HALF * QT, 0:P], mx[r][:, half * HALF * QT:(half + 1) * HALF * QT], res.ident[:]).then_inc(max_turned, 1)

                def score(w, r, h, ts, first):
                    if ts[0] == 0:
                        if h % HALF == 0:
                            pe.wait_ge(max_in[h // HALF], 48 * (w + 1))
                        if not (first and h < 2):
                            pe.wait_ge(exped, w * HEADS + h - 1)
                    for t in ts:
                        out = psE[h % 2][:, t, :]
                        pe.matmul(out, k_op[r][0:rows + 3, h // 2, t * P:(t + 1) * P], q_op[r][0:rows + 3, h, :], start=True, stop=False)
                        last = pe.matmul(out, res.identb[:], maddT[r][:, t, :], start=False, stop=True)
                    if ts[-1] == KT - 1:
                        last.then_inc(scored, 1)

                def weigh(w, r, quad, t, first):
                    if t == 0:
                        pe.wait_ge(exped, w * HEADS + (quad + 1) * QUAD)
                        if quad == 0 and not first:
                            pe.wait_ge(out_read, w)
                    g, s = quad // 2, quad % 2
                    for j in range(QUAD):
                        h = quad * QUAD + j
                        last = pe.matmul(psO[32 * j:32 * j + 32, g, :], values[r][:, t, h, :], probs[h % (2 * QUAD)][:, t, :],
                                         start=(s == 0 and t == 0), stop=(s == 1 and t == KT - 1),
                                         tile_position=(0, 32 * j), skip_group_check=True)
                    if t == KT - 1:
                        last.then_inc(weighted, 1)

                def step(v, r, turn, inner=False):
                    take_max, take_exp, finish = inner or v < B, inner or v >= 1, inner or v >= 2
                    before, first = (r - 1) % RING, not inner and v <= 1
                    if take_max:
                        pe.wait_ge(loaded[r], 16 * n_loads * (turn + 1))
                    if take_exp:
                        pe.wait_ge(masked, v * 2)
                        pe.wait_ge(v_out, 2 * v)
                    for s in range(HEADS):
                        if take_max:
                            maximum(v, r, s, 0, first and v == 0)
                        if take_exp:
                            score(v - 1, before, s, (0, 1), first)
                        if take_max:
                            maximum(v, r, s, 1, first and v == 0)
                        if take_exp:
                            score(v - 1, before, s, (2, 3), first)
                        quad, t = s // QUAD - 1, s % QUAD
                        if quad >= 0 and take_exp:
                            weigh(v - 1, before, quad, t, first)
                        if quad < 0 and finish:
                            weigh(v - 2, (r - 2) % RING, QUADS - 1, t, False)
                        if take_exp and s == MAX_SLOTS[1]:
                            turn_maxima(v - 1, before, 1)
                        if finish:
                            if s == OUT_SLOT:
                                pe.wait_ge(max_split, 2 * n_split * v)
                                turn_out(v - 2)
                            if s == BACK_SLOT:
                                turn_back(v - 2)
                            if s == PROJECT_SLOT:
                                project(v - 2)
                        if take_max:
                            if s == MAX_SLOTS[0]:
                                if finish:
                                    pe.wait_ge(added, v - 1)
                                elif v >= 1:
                                    pe.wait_ge(max_split, 2 * n_split * v)
                                turn_maxima(v, r, 0)
                            if s == V_SLOT:
                                pe.wait_ge(max_split, 2 * n_split * v + n_split)
                                for t in range(KT):
                                    last = pe.matmul(psX[:, t * P:(t + 1) * P], cT[r][:, t * P:(t + 1) * P], wv[:], start=True, stop=True)
                                last.then_inc(v_made, 1)

                steps(pe, step)
                for t in range(KT):
                    weigh(B - 1, (B - 1) % RING, QUADS - 1, t, False)
                pe.wait_ge(added, B - 1)
                turn_out(B - 1)
                turn_back(B - 1)
                project(B - 1)

            @block.scalar
            def _(act):
                if cfg.q_bias:
                    act.wait_ge(bias_scaled, 1)
                for n in range(NCHUNK):
                    act.wait_ge(query_made, n + 1)
                    if n >= 2:
                        act.wait_ge(split, 4 * (n - 1))
                    act.activation(y[n % 2][:], psM[n % 2][:], ACT.Identity, bias=bqs[:] if cfg.q_bias else 0.0, scale=cfg.scale).then_inc(biased, 1)

                def read_out(u):
                    act.wait_ge(weighted, (u + 1) * QUADS)
                    act.copy(OT[:], psO[:]).then_inc(out_read, 1)

                def copy_back(u):
                    act.wait_ge(back_turned, u + 1)
                    act.copy(AT[:], psX[:, 0:S]).then_inc(back_copied, 1)

                def copy_values(v, r):
                    act.wait_ge(v_made, v + 1)
                    for s in range(2):
                        act.copy(values[r][:].rearrange("p k (g s j) m -> p (k g) s j m", g=2, s=2)[:, :, s, :, s * SLOT:s * SLOT + HEAD_E],
                                 psX[:].rearrange("p (n s j c) -> p n s j c", s=2, j=4, c=HEAD_E)[:, :, s]).then_inc(v_out, 1)

                def step(v, r, turn, inner=False):
                    take_max, take_exp, finish = inner or v < B, inner or v >= 1, inner or v >= 2
                    for s in range(HEADS):
                        if take_exp:
                            n = (v - 1) * HEADS + s
                            act.wait_ge(scored, n + 1)
                            if not (not inner and v == 1 and s < 2 * QUAD):
                                act.wait_ge(weighted, (v - 1) * QUADS + s // QUAD - 1)
                            act.activation(probs[s % (2 * QUAD)][:], psE[s % 2][:], ACT.Exp).then_inc(exped, 1)
                        if finish:
                            if s == READ_SLOT:
                                read_out(v - 2)
                            if s == BACK_SLOT:
                                copy_back(v - 2)
                        if take_max and s == V_SLOT:
                            copy_values(v, r)

                steps(act, step)
                read_out(B - 1)
                copy_back(B - 1)

            @block.vector
            def _(dve):
                if cfg.q_bias:
                    dve.tensor_scalar(bqs[:], nb.bq[:], cfg.scale, None, ALU.mult).then_inc(bias_scaled, 1)
                for n in range(NCHUNK):
                    dve.wait_ge(biased, n + 1)
                    if n >= 2:
                        dve.wait_ge(stored[n % 2], 32 * (n // 2))
                    p0, p1, p2 = (y_parts[n % 2][:, k, :] for k in range(3))
                    dve.tensor_copy(p0, y[n % 2][:]).then_inc(split, 1)
                    dve.wait_ge(split, 4 * n + 1)
                    dve.tensor_tensor(y_rest[:], y[n % 2][:], p0, ALU.subtract).then_inc(split, 1)
                    dve.wait_ge(split, 4 * n + 2)
                    dve.tensor_copy(p1, y_rest[:]).then_inc(split, 1)
                    dve.wait_ge(split, 4 * n + 3)
                    dve.tensor_tensor(p2, y_rest[:], p1, ALU.subtract).then_inc(split, 1)
                if cfg.q_bias:
                    dve.wait_ge(bias_made, 1)
                    dve.tensor_tensor(bias_row[:], psX[0:1, 0:D], nb.bo[:], ALU.add).then_inc(row_done, 1)

                def normalise(u):
                    dve.wait_ge(out_turned, u + 1)
                    turned = psX[:].rearrange("p (n j m) -> p n j m", n=4, j=4)
                    dve.tensor_scalar(den[:], turned[:, :, :, HEAD_E:2 * SLOT:SLOT], cfg.sink, None, ALU.add).then_inc(den_done, 1)
                    dve.wait_ge(den_done, u + 1)
                    dve.reciprocal(rec[:], den[:]).then_inc(rec_done, 1)
                    dve.wait_ge(rec_done, u + 1)
                    for s in range(2):
                        dve.tensor_tensor(A[:].rearrange("p t (g s j c) -> p (t g) s j c", g=2, s=2, j=4)[:, :, s],
                                          turned[:, :, :, s * SLOT:s * SLOT + HEAD_E],
                                          rec[:, :, :, s:s + 1].to_broadcast([P, 4, 4, HEAD_E]), ALU.mult).then_inc(normed, 1)

                def add(u):
                    dve.wait_ge(projected, u + 1)
                    x = res.X[:, bass.ds(u * QT, QT), :].rearrange("p t d -> p (t d)")
                    dve.scalar_tensor_tensor(x, psX[:, 0:S], res.gates[:, cfg.gate:cfg.gate + 1], x, ALU.mult, ALU.add).then_inc(added, 1)

                def maximum(v, r, h):
                    for t in range(QT):
                        n = QT * h + t
                        dve.wait_ge(max_scored, v * HEADS * QT + n + 1)
                        dve.memset(carrier[t][:], 0.0)
                        dve.tensor_tensor_reduce(junk[t][:], psM[t][:], madd[r][:, t, :], 1.0, -3.0e38, ALU.add, ALU.max,
                                                 mx[r][:, n:n + 1]).then_inc(max_read, 1)

                def split_max(v, half):
                    done = (2 * v + half) * n_split
                    dve.wait_ge(max_turned, 2 * v + half + 1)
                    m, parts = psX[0:HALF * QT, 0:P], max_parts[half]
                    dve.tensor_scalar(parts[:, 0, :], m, -1.0, None, ALU.mult).then_inc(max_split, 1)
                    dve.wait_ge(max_split, done + 1)
                    dve.scalar_tensor_tensor(max_rest[:], m, -1.0, parts[:, 0, :], ALU.mult, ALU.subtract).then_inc(max_split, 1)
                    dve.wait_ge(max_split, done + 2)
                    dve.tensor_copy(parts[:, 1, :], max_rest[:]).then_inc(max_split, 1)
                    dve.wait_ge(max_split, done + 3)
                    dve.tensor_tensor(parts[:, 2, :], max_rest[:], parts[:, 1, :], ALU.subtract).then_inc(max_split, 1)

                def step(v, r, turn, inner=False):
                    take_max, take_exp, finish = inner or v < B, inner or v >= 1, inner or v >= 2
                    if take_max:
                        dve.wait_ge(masked, 2 * v + 1)
                    for s in range(HEADS):
                        if take_max:
                            maximum(v, r, s)
                        if take_exp and s == MAX_SLOTS[1]:
                            if inner or v >= 2:
                                dve.wait_ge(max_in[1], 48 * (v - 1))
                            split_max(v - 1, 1)
                        if finish:
                            if s == OUT_SLOT:
                                normalise(v - 2)
                            if s == PROJECT_SLOT:
                                add(v - 2)
                        if take_max and s == MAX_SLOTS[0]:
                            if inner or v >= 1:
                                dve.wait_ge(max_in[0], 48 * v)
                            split_max(v, 0)

                steps(dve, step)
                normalise(B - 1)
                add(B - 1)
                dve.wait_ge(added, B)



WIDE_E = 64
WIDE_V = HEADS * WIDE_E
W_PAIRS = HEADS // 2
VC = WIDE_V // CHUNK


def layer1_attention(nc, io, res):
    halves = 2
    with Phase(nc, "a1") as ph:
        max_scr = nc.dram_tensor("a1_max", [RING, HEADS * QT, P], BF16).ap()
        G, q_bias, wv, wo, bias_row = res.G, res.q_bias, res.wv1, res.wo1, res.bias_row1

        cT = [ph.sb(f"cT{i}", [P, S2]) for i in range(RING)]
        cTb = [ph.sb(f"cTb{i}", [P, S2], BF16) for i in range(RING)]
        q_op = [ph.sb(f"q_op{i}", [P, HEADS, S]) for i in range(RING)]
        q_b = [ph.sb(f"q_b{i}", [P, S], BF16) for i in range(4)]
        values = [ph.sb(f"values{i}", [P, KT, WIDE_V]) for i in range(RING)]
        max_row = [ph.sb(f"max_row{i}", [P, HEADS * S], BF16) for i in range(RING)]
        mx = [ph.sb(f"mx{i}", [P, HEADS * QT]) for i in range(RING)]
        max_b = ph.sb("max_b", [HEADS * QT, P], BF16)
        probs = [ph.sb(f"probs{i}", [P, KT, S]) for i in range(4)]
        half_sum = [ph.sb(f"half_sum{i}", [P, 2, S]) for i in range(2)]
        key_sum = [ph.sb(f"key_sum{i}", [P, S]) for i in range(4)]
        rec = ph.sb("rec", [P, S])
        OT = ph.sb("OT", [P, W_PAIRS, S])

        psM = [ph.ps(f"psM{i}", [P, S2]) for i in range(2)]
        psE = [ph.ps(f"psE{i}", [P, 2, S]) for i in range(halves)]
        psO = ph.ps("psO", [P, 2, S])
        psQ = [ph.ps(f"psQ{i}", [P, CHUNK]) for i in range(2)]
        psY = ph.ps("psY", [P, CHUNK])

        loaded = [ph.sem(f"loaded{i}") for i in range(RING)]
        cast, zeroed, q_cast = ph.sem("cast"), ph.sem("zeroed"), ph.sem("q_cast")
        q_made, q_out = ph.sem("q_made"), ph.sem("q_out")
        max_scored, max_read = ph.sem("max_scored"), ph.sem("max_read")
        max_turned, max_cast, max_stored = ph.sem("max_turned"), ph.sem("max_cast"), ph.sem("max_stored")
        max_in = [ph.sem(f"max_in{i}") for i in range(RING)]
        v_made, v_out = ph.sem("v_made"), ph.sem("v_out")
        scored, exped, weighted = ph.sem("scored"), ph.sem("exped"), ph.sem("weighted")
        halved, summed = ph.sem("halved"), ph.sem("summed")
        inverted, normed = ph.sem("inverted"), ph.sem("normed")
        projected, added = ph.sem("projected"), ph.sem("added")
        n_v = KT * VC

        max_slots = [[h for h in range(4 * s // 3, 4 * (s + 1) // 3) if h < HEADS] for s in range(HEADS)]
        OUT_SLOT, V_SLOT, MAX_SLOT = 2, 3, 12

        def steps(eng, step):
            step(0, 0, 0)
            step(1, 1, 0)
            with eng.Fori(0, (B - 2) // RING) as i:
                for k in range(RING):
                    step(RING * i + 2 + k, (2 + k) % RING, i + (2 + k) // RING, inner=True)
            step(B, B % RING, B // RING)

        with ph.block() as block:
            @block.sync
            def _(sp):
                def load(u, r):
                    sp.dma_start(cT[r][:], io["ctxT"][:, bass.ds(u * S2, S2)]).then_inc(loaded[r], 16)

                def maxima(v, r):
                    sp.wait_ge(max_cast, v + 1)
                    sp.dma_start(max_scr[r], max_b[:]).then_inc(max_stored, 16)
                    sp.wait_ge(max_stored, v * 16 + 16)
                    sp.dma_start(max_row[r][0:1, :], max_scr[r].rearrange("n q -> (n q)").unsqueeze(0)).then_inc(max_in[r], 16)

                load(0, 0)
                load(1, 1)
                sp.wait_ge(zeroed, RING)
                maxima(0, 0)
                with sp.Fori(0, (B - 2) // RING) as i:
                    for k in range(RING):
                        v, r = RING * i + 2 + k, (2 + k) % RING
                        sp.wait_ge(weighted, (v - 2) * W_PAIRS + 1)
                        load(v, r)
                        maxima(v - 1, (r - 1) % RING)
                maxima(B - 1, (B - 1) % RING)

            @block.gpsimd
            def _(pool):
                for r in range(RING):
                    pool.memset(max_row[r][:], 0.0).then_inc(zeroed, 1)

                def heads(w, first):
                    for h in range(HEADS):
                        n = w * HEADS + h
                        pool.wait_ge(exped, (n + 1) * halves)
                        pool.tensor_tensor(half_sum[h % 2][:], probs[h % 4][:, 0:2, :], probs[h % 4][:, 2:4, :], ALU.add).then_inc(halved, 1)
                        if not (first and h < 4):
                            pool.wait_ge(weighted, w * W_PAIRS + (h - 4) // 2 + 1)
                        pool.wait_ge(halved, n + 1)
                        pool.tensor_tensor(key_sum[h % 4][:], half_sum[h % 2][:, 0, :], half_sum[h % 2][:, 1, :], ALU.add).then_inc(summed, 1)

                heads(0, True)
                with pool.Fori(1, B) as w:
                    heads(w, False)

            @block.tensor
            def _(pe):
                def query(v, r, h, first):
                    if not (first and h < 2):
                        pe.wait_ge(q_cast, v * HEADS + h - 1)
                    pe.matmul(psQ[h % 2][:, 0:S], G[:, h, :], res.xnT[:, bass.ds(v * S, S)], start=True, stop=True).then_inc(q_made, 1)

                def maximum(v, r, h, first):
                    pe.wait_ge(q_cast, v * HEADS + h + 1)
                    for t in range(QT):
                        n = QT * h + t
                        if not (first and n < 2):
                            pe.wait_ge(max_read, v * HEADS * QT + n - 1)
                        pe.matmul(psM[t][:], q_b[h % 4][:, t * P:(t + 1) * P], cTb[r][:], start=True, stop=True).then_inc(max_scored, 1)

                def score(w, r, h, first):
                    for half in range(halves):
                        if not (first and h == 0):
                            pe.wait_ge(exped, (w * HEADS + h - 1) * halves + half + 1)
                        for t in range(2):
                            k = (2 * half + t) * P
                            pe.matmul(psE[half][:, t, :], cT[r][:, k:k + P], q_op[r][:, h, :], start=(t == 0), stop=False, skip_group_check=True)
                        pe.matmul(psE[half][:], res.onesb[:], max_row[r][:, h * S:(h + 1) * S].unsqueeze(1).to_broadcast([P, 2, S]),
                                  start=False, stop=True, skip_group_check=True).then_inc(scored, 1)

                def weigh(w, r, pair, first):
                    pe.wait_ge(exped, (w * HEADS + 2 * pair + 2) * halves)
                    if not first:
                        pe.wait_ge(normed, w * W_PAIRS + pair)
                    for t in range(KT):
                        for i in range(2):
                            h = 2 * pair + i
                            pe.matmul(psO[i * WIDE_E:(i + 1) * WIDE_E, 0, :], values[r][:, t, h * WIDE_E:(h + 1) * WIDE_E], probs[h % 4][:, t, :],
                                      start=(t == 0), stop=False, tile_position=(0, i * WIDE_E), skip_group_check=True)

                def total(w, pair):
                    pe.wait_ge(summed, w * HEADS + 2 * pair + 2)
                    for i in range(2):
                        last = pe.matmul(psO[i * WIDE_E:(i + 1) * WIDE_E, 1, :], res.ones[:, 0:WIDE_E], key_sum[(2 * pair + i) % 4][:],
                                         start=False, stop=True, tile_position=(0, i * WIDE_E), skip_group_check=True)
                    last.then_inc(weighted, 1)

                def project(u):
                    pe.wait_ge(normed, (u + 1) * W_PAIRS)
                    for t in range(QT):
                        y = psY[:, t * P:(t + 1) * P]
                        pe.matmul(y, res.ones[0:1, :], bias_row[:], start=True, stop=False)
                        for p in range(W_PAIRS):
                            last = pe.matmul(y, OT[:, p, t * P:(t + 1) * P], wo[:, p, :], start=False, stop=(p == W_PAIRS - 1))
                    last.then_inc(projected, 1)

                def value(v, r, n, wait):
                    if n > 0:
                        pe.wait_ge(v_out, v * n_v + n)
                    t, c = n // VC, n % VC
                    pe.matmul(psY[:], cT[r][:, t * P:(t + 1) * P], wv[:, c * CHUNK:(c + 1) * CHUNK], start=True, stop=True).then_inc(v_made, 1)

                def step(v, r, turn, inner=False):
                    take_max, take_exp, finish = inner or v < B, inner or v >= 1, inner or v >= 2
                    first, before = not inner and v == 0, (r - 1) % RING
                    if take_max:
                        pe.wait_ge(loaded[r], 16 * (turn + 1))
                        query(v, r, 0, first)
                        query(v, r, 1, first)
                    if take_exp:
                        turn_before = turn - (r == 0) if inner else (v - 1) // RING
                        pe.wait_ge(q_out, v * HEADS)
                        pe.wait_ge(max_in[before], 16 * (turn_before + 1))
                        pe.wait_ge(v_out, v * n_v)
                    for s in range(HEADS):
                        if finish and s == OUT_SLOT:
                            pe.wait_ge(max_cast, v)
                            project(v - 2)
                        if take_max:
                            if V_SLOT <= s < V_SLOT + n_v:
                                if s == V_SLOT:
                                    if finish:
                                        pe.wait_ge(added, v - 1)
                                    elif not first:
                                        pe.wait_ge(max_cast, v)
                                value(v, r, s - V_SLOT, first)
                            for h in max_slots[s]:
                                if h + 2 < HEADS:
                                    query(v, r, h + 2, first)
                                if h == 0:
                                    pe.wait_ge(cast, v + 1)
                                maximum(v, r, h, first)
                        if take_exp:
                            score(v - 1, before, s, not inner and v == 1)
                            if s >= 2 and s % 2 == 0:
                                weigh(v - 1, before, s // 2 - 1, not inner and v == 1 and s == 2)
                            if s >= 3 and s % 2 == 1:
                                total(v - 1, (s - 3) // 2)
                        if finish and s == 0:
                            weigh(v - 2, (r - 2) % RING, W_PAIRS - 1, False)
                        if finish and s == 1:
                            total(v - 2, W_PAIRS - 1)
                        if take_max and s == MAX_SLOT:
                            pe.wait_ge(max_read, (v + 1) * HEADS * QT)
                            pe.wait_ge(v_out, (v + 1) * n_v)
                            pe.transpose(psY[0:HEADS * QT, 0:P], mx[r][:], res.ident[:]).then_inc(max_turned, 1)

                steps(pe, step)
                weigh(B - 1, (B - 1) % RING, W_PAIRS - 1, False)
                total(B - 1, W_PAIRS - 1)
                project(B - 1)

            @block.scalar
            def _(act):
                def query(v, r, h, first):
                    act.wait_ge(q_made, v * HEADS + h + 1)
                    act.activation(q_op[r][:, h, :], psQ[h % 2][:, 0:S], ACT.Identity, bias=q_bias[:, h:h + 1]).then_inc(q_out, 1)
                    if not (first and h < 4):
                        act.wait_ge(max_scored, (v * HEADS + h - 3) * QT)
                    act.activation(q_b[h % 4][:], psQ[h % 2][:, 0:S], ACT.Identity, bias=q_bias[:, h:h + 1]).then_inc(q_cast, 1)

                def step(v, r, turn, inner=False):
                    take_max, take_exp = inner or v < B, inner or v >= 1
                    first = not inner and v == 0
                    if take_max:
                        query(v, r, 0, first)
                        query(v, r, 1, first)
                    for s in range(HEADS):
                        if take_max:
                            if V_SLOT <= s < V_SLOT + n_v:
                                n = s - V_SLOT
                                act.wait_ge(v_made, v * n_v + n + 1)
                                act.copy(values[r][:, n // VC, n % VC * CHUNK:(n % VC + 1) * CHUNK], psY[:]).then_inc(v_out, 1)
                            for h in max_slots[s]:
                                if h + 2 < HEADS:
                                    query(v, r, h + 2, first)
                        if take_exp:
                            w = v - 1
                            if not (not inner and v == 1 and s < 4):
                                act.wait_ge(weighted, w * W_PAIRS + (s - 4) // 2 + 1)
                            for half in range(halves):
                                act.wait_ge(scored, (w * HEADS + s) * halves + half + 1)
                                act.activation(probs[s % 4][:, 2 * half:2 * half + 2, :], psE[half][:], ACT.Exp).then_inc(exped, 1)

                steps(act, step)

            @block.vector
            def _(dve):
                def normalise(w, pair):
                    dve.wait_ge(weighted, w * W_PAIRS + pair + 1)
                    dve.reciprocal(rec[:], psO[:, 1, :]).then_inc(inverted, 1)
                    dve.wait_ge(inverted, w * W_PAIRS + pair + 1)
                    dve.tensor_tensor(OT[:, pair, :], psO[:, 0, :], rec[:], ALU.mult).then_inc(normed, 1)

                def add(u):
                    dve.wait_ge(projected, u + 1)
                    x = res.X[:, bass.ds(u * QT, QT), :].rearrange("p t d -> p (t d)")
                    dve.scalar_tensor_tensor(x, psY[:, 0:S], res.gates[:, 1:2], x, ALU.mult, ALU.add).then_inc(added, 1)

                def step(v, r, turn, inner=False):
                    take_max, take_exp, finish = inner or v < B, inner or v >= 1, inner or v >= 2
                    if take_max:
                        dve.wait_ge(loaded[r], 16 * (turn + 1))
                        dve.tensor_copy(cTb[r][:], cT[r][:]).then_inc(cast, 1)
                    for s in range(HEADS):
                        if finish and s == OUT_SLOT:
                            add(v - 2)
                        if take_max:
                            for h in max_slots[s]:
                                for t in range(QT):
                                    n = QT * h + t
                                    dve.wait_ge(max_scored, v * HEADS * QT + n + 1)
                                    dve.tensor_reduce(mx[r][:, n:n + 1], psM[t][:], AX.X, ALU.max).then_inc(max_read, 1)
                        if take_exp and s >= 3 and s % 2 == 1:
                            normalise(v - 1, (s - 3) // 2)
                        if finish and s == 1:
                            normalise(v - 2, W_PAIRS - 1)
                        if take_max and s == MAX_SLOT:
                            dve.wait_ge(max_turned, v + 1)
                            if inner or v >= 1:
                                dve.wait_ge(max_stored, 16 * v)
                            dve.tensor_scalar(max_b[:], psY[0:HEADS * QT, 0:P], -1.0, None, ALU.mult).then_inc(max_cast, 1)

                steps(dve, step)
                normalise(B - 1, W_PAIRS - 1)
                add(B - 1)
                dve.wait_ge(added, B)



ROUND = 1.5 * 2.0 ** 23
INT8_MAX = 127.0


def layer1_int8(nc, io, res):
    with Phase(nc, "q1") as ph:
        ahead = NarrowConstants(ph, res.narrow)
        wT = ph.sb("wT", [P, D])
        w_max, w_scale, w_inv = (ph.sb(n, [P, 1]) for n in ("w_max", "w_scale", "w_inv"))
        wr = ph.sb("wr", [P, D])
        wq = ph.sb("wq", [P, D], BF16)
        diag = ph.sb("diag", [P, P])
        col_scale = ph.sb("col_scale", [P, D])
        x_max, x_scale, x_inv, x_gate = (ph.sb(n, [P, NTILE]) for n in ("x_max", "x_scale", "x_inv", "x_gate"))
        xr = ph.sb("xr", [P, NTILE, D])
        tmp = [ph.sb(f"tmp{i}", [P, D]) for i in range(2)]
        xq = ph.sb("xq", [P, NTILE * P], BF16)
        psW = ph.ps("psW", [P, CHUNK])
        psT = [ph.ps(f"psT{i}", [P, CHUNK]) for i in range(2)]
        psY = [ph.ps(f"psY{i}", [P, 4, D]) for i in range(2)]
        w_in, step, w_turned, w_copied = (ph.sem(n) for n in ("w_in", "step", "w_turned", "w_copied"))
        rounded, turned, copied, made, scaled, added = (ph.sem(n) for n in ("rounded", "turned", "copied", "made", "scaled", "added"))
        with ph.block() as block:
            @block.sync
            def _(sp):
                sp.dma_start(wT[:], io["L1_rhsT"]).then_inc(w_in, 16)
                ahead.sync(sp, io)

            @block.gpsimd
            def _(pool):
                ahead.gpsimd(pool)

            @block.vector
            def _(dve):
                dve.tensor_reduce(x_max[:], res.xn[:], AX.X, ALU.max, apply_absolute_value=True).then_inc(step, 1)
                dve.wait_ge(step, 1)
                dve.tensor_scalar(x_scale[:], x_max[:], 1e-12, 1.0 / INT8_MAX, ALU.max, ALU.mult).then_inc(step, 1)
                dve.wait_ge(step, 2)
                dve.reciprocal(x_inv[:], x_scale[:]).then_inc(step, 1)
                dve.tensor_scalar(x_gate[:], x_scale[:], res.gates[:, 5:6], None, ALU.mult).then_inc(step, 1)
                dve.wait_ge(step, 4)
                for t in range(NTILE):
                    dve.tensor_scalar(xr[:, t, :], res.xn[:, t, :], x_inv[:, t:t + 1], ROUND, ALU.mult, ALU.add).then_inc(step, 1)
                dve.wait_ge(step, 4 + NTILE)
                dve.tensor_scalar(xr[:], xr[:], ROUND, INT8_MAX, ALU.subtract, ALU.min).then_inc(step, 1)
                dve.wait_ge(step, 5 + NTILE)
                dve.tensor_scalar(xr[:], xr[:], -INT8_MAX, None, ALU.max).then_inc(rounded, 1)
                dve.wait_ge(w_in, 16)
                dve.tensor_reduce(w_max[:], wT[:], AX.X, ALU.max, apply_absolute_value=True).then_inc(step, 1)
                dve.wait_ge(step, 6 + NTILE)
                dve.tensor_scalar(w_scale[:], w_max[:], 1e-12, 1.0 / INT8_MAX, ALU.max, ALU.mult).then_inc(step, 1)
                dve.wait_ge(step, 7 + NTILE)
                dve.reciprocal(w_inv[:], w_scale[:]).then_inc(step, 1)
                dve.tensor_scalar(diag[:], res.ident[:], w_scale[:], None, ALU.mult).then_inc(step, 1)
                dve.wait_ge(step, 9 + NTILE)
                dve.tensor_scalar(wr[:], wT[:], w_inv[:], ROUND, ALU.mult, ALU.add).then_inc(step, 1)
                dve.wait_ge(step, 10 + NTILE)
                dve.tensor_scalar(wr[:], wr[:], ROUND, INT8_MAX, ALU.subtract, ALU.min).then_inc(step, 1)
                dve.wait_ge(step, 11 + NTILE)
                dve.tensor_scalar(wr[:], wr[:], -INT8_MAX, None, ALU.max).then_inc(rounded, 1)
                dve.wait_ge(w_turned, 1)
                dve.tensor_copy(wq[:], psW[:, 0:D]).then_inc(w_copied, 1)
                dve.tensor_copy(col_scale[:], psW[:, D:2 * D]).then_inc(w_copied, 1)
                dve.wait_ge(w_copied, 2)
                for c in range(NCHUNK):
                    dve.wait_ge(made, c + 1)
                    for k in range(4):
                        t = 4 * c + k
                        dve.scalar_tensor_tensor(tmp[k % 2][:], psY[c % 2][:, k, :], x_gate[:, t:t + 1], col_scale[:],
                                                 ALU.mult, ALU.mult).then_inc(scaled, 1)
                        dve.wait_ge(scaled, t + 1)
                        dve.tensor_tensor(res.X[:, t, :], res.X[:, t, :], tmp[k % 2][:], ALU.add).then_inc(added, 1)
                ahead.vector(dve)
                dve.wait_ge(added, NTILE)

            @block.tensor
            def _(pe):
                pe.wait_ge(rounded, 1)
                for c in range(NCHUNK):
                    if c >= 2:
                        pe.wait_ge(copied, c - 1)
                    for k in range(4):
                        last = pe.transpose(psT[c % 2][:, k * P:(k + 1) * P], xr[:, 4 * c + k, :], res.ident[:])
                    last.then_inc(turned, 1)
                pe.wait_ge(rounded, 2)
                pe.transpose(psW[:, 0:D], wr[:], res.ident[:])
                pe.matmul(psW[:, D:2 * D], res.ones[:], diag[:], start=True, stop=True).then_inc(w_turned, 1)
                pe.wait_ge(w_copied, 2)
                for c in range(NCHUNK):
                    pe.wait_ge(copied, c + 1)
                    if c >= 2:
                        pe.wait_ge(scaled, 4 * (c - 1))
                    for k in range(4):
                        t = 4 * c + k
                        last = pe.matmul(psY[c % 2][:, k, :], xq[:, t * P:(t + 1) * P], wq[:], start=True, stop=True)
                    last.then_inc(made, 1)

            @block.scalar
            def _(act):
                for c in range(NCHUNK):
                    act.wait_ge(turned, c + 1)
                    act.copy(xq[:, c * CHUNK:(c + 1) * CHUNK], psT[c % 2][:]).then_inc(copied, 1)
                ahead.scalar(act)


def layer3_ternary(nc, io, res):
    with Phase(nc, "q3") as ph:
        w = ph.sb("w", [P, D])
        w_abs, w_mean, w_low, x_abs, x_scale, x_inv, out_scale = (
            ph.sb(n, [P, 1]) for n in ("w_abs", "w_mean", "w_low", "x_abs", "x_scale", "x_inv", "out_scale"))
        w_half = ph.sb("w_half", [P, 1])
        over, under = ph.sb("over", [P, D]), ph.sb("under", [P, D])
        wq = ph.sb("wq", [P, D], BF16)
        bias = ph.sb("bias", [P, D])
        x_top = ph.sb("x_top", [1, 1])
        xr = ph.sb("xr", [P, NTILE, D])
        tmp = [ph.sb(f"tmp{i}", [P, D]) for i in range(2)]
        xq = ph.sb("xq", [P, NTILE * P], BF16)
        psS = ph.ps("psS", [P, CHUNK])
        psT = [ph.ps(f"psT{i}", [P, CHUNK]) for i in range(2)]
        psY = [ph.ps(f"psY{i}", [P, 4, D]) for i in range(2)]
        w_in, step, x_reduced, x_turned, x_topped, w_reduced, w_summed = (
            ph.sem(n) for n in ("w_in", "step", "x_reduced", "x_turned", "x_topped", "w_reduced", "w_summed"))
        rounded, ternary, turned, copied, made, scaled, added = (
            ph.sem(n) for n in ("rounded", "ternary", "turned", "copied", "made", "scaled", "added"))
        with ph.block() as block:
            @block.sync
            def _(sp):
                sp.dma_start(w[:], io["L3_wT"]).then_inc(w_in, 16)
                sp.dma_start(bias[:], io["L3_bias"].partition_broadcast(P)).then_inc(w_in, 16)

            @block.vector
            def _(dve):
                dve.tensor_reduce(x_abs[:], res.xn[:], AX.XY, ALU.max, apply_absolute_value=True).then_inc(x_reduced, 1)
                dve.wait_ge(w_in, 32)
                dve.tensor_reduce(w_abs[:], w[:], AX.X, ALU.add, apply_absolute_value=True).then_inc(w_reduced, 1)
                dve.wait_ge(x_turned, 1)
                dve.tensor_reduce(x_top[:], psS[0:1, 0:P], AX.X, ALU.max).then_inc(x_topped, 1)
                dve.wait_ge(w_summed, 1)
                dve.tensor_scalar(w_mean[:], psS[:, P:P + 1], 1.0 / (D * D), None, ALU.mult).then_inc(step, 1)
                dve.tensor_scalar(w_half[:], psS[:, P:P + 1], 0.5 / (D * D), None, ALU.mult).then_inc(step, 1)
                dve.tensor_scalar(w_low[:], psS[:, P:P + 1], -0.5 / (D * D), None, ALU.mult).then_inc(step, 1)
                dve.tensor_scalar(x_scale[:], psS[:, P + 1:P + 2], 1.0 / INT8_MAX, None, ALU.mult).then_inc(step, 1)
                dve.wait_ge(step, 4)
                dve.reciprocal(x_inv[:], x_scale[:]).then_inc(step, 1)
                dve.tensor_scalar(over[:], w[:], w_half[:], None, ALU.is_gt).then_inc(step, 1)
                dve.tensor_scalar(under[:], w[:], w_low[:], None, ALU.is_lt).then_inc(step, 1)
                dve.scalar_tensor_tensor(out_scale[:], w_mean[:], res.gates[:, 7:8], x_scale[:], ALU.mult, ALU.mult).then_inc(step, 1)
                dve.wait_ge(step, 8)
                dve.tensor_tensor(wq[:], over[:], under[:], ALU.subtract).then_inc(ternary, 1)
                dve.tensor_scalar(bias[:], bias[:], res.gates[:, 7:8], None, ALU.mult).then_inc(step, 1)
                dve.tensor_scalar(xr[:], res.xn[:], x_inv[:], ROUND, ALU.mult, ALU.add).then_inc(step, 1)
                dve.wait_ge(step, 10)
                dve.tensor_scalar(xr[:], xr[:], ROUND, INT8_MAX, ALU.subtract, ALU.min).then_inc(step, 1)
                dve.wait_ge(step, 11)
                dve.tensor_scalar(xr[:], xr[:], -INT8_MAX - 1.0, None, ALU.max).then_inc(rounded, 1)
                for c in range(NCHUNK):
                    dve.wait_ge(made, c + 1)
                    for k in range(4):
                        t = 4 * c + k
                        dve.scalar_tensor_tensor(tmp[k % 2][:], psY[c % 2][:, k, :], out_scale[:], bias[:],
                                                 ALU.mult, ALU.add).then_inc(scaled, 1)
                        dve.wait_ge(scaled, t + 1)
                        dve.tensor_tensor(res.X[:, t, :], res.X[:, t, :], tmp[k % 2][:], ALU.add).then_inc(added, 1)
                dve.wait_ge(added, NTILE)

            @block.tensor
            def _(pe):
                pe.wait_ge(x_reduced, 1)
                pe.transpose(psS[0:1, 0:P], x_abs[:], res.ident[:]).then_inc(x_turned, 1)
                pe.wait_ge(w_reduced, 1)
                pe.wait_ge(x_topped, 1)
                pe.matmul(psS[:, P:P + 1], res.ones[:], w_abs[:], start=True, stop=True)
                pe.matmul(psS[:, P + 1:P + 2], res.ones[0:1, :], x_top[:], start=True, stop=True).then_inc(w_summed, 1)
                pe.wait_ge(rounded, 1)
                for c in range(NCHUNK):
                    if c >= 2:
                        pe.wait_ge(copied, c - 1)
                    for k in range(4):
                        last = pe.transpose(psT[c % 2][:, k * P:(k + 1) * P], xr[:, 4 * c + k, :], res.ident[:])
                    last.then_inc(turned, 1)
                pe.wait_ge(ternary, 1)
                for c in range(NCHUNK):
                    pe.wait_ge(copied, c + 1)
                    if c >= 2:
                        pe.wait_ge(scaled, 4 * (c - 1))
                    for k in range(4):
                        t = 4 * c + k
                        last = pe.matmul(psY[c % 2][:, k, :], xq[:, t * P:(t + 1) * P], wq[:], start=True, stop=True)
                    last.then_inc(made, 1)

            @block.scalar
            def _(act):
                for c in range(NCHUNK):
                    act.wait_ge(turned, c + 1)
                    act.copy(xq[:, c * CHUNK:(c + 1) * CHUNK], psT[c % 2][:]).then_inc(copied, 1)


def more_layouts(a, io):
    io["c_iota"] = np.arange(16, dtype=np.float32)
    io["c_tri"] = np.triu(np.ones((P, P), np.float32))
    io["c_lane"] = np.arange(P, dtype=np.float32)
    io["c_place"] = np.arange(L0_CAPACITY, dtype=np.float32)
    io["L0_Wg"] = a["L0_ffn_Wg"]
    io["L0_W1"], io["L0_W2"], io["L0_b2"] = a["L0_ffn_W1"], a["L0_ffn_W2"], a["L0_ffn_b2"]
    io["L0_b1"] = a["L0_ffn_b1"].reshape(8, 4, P).transpose(0, 2, 1)
    shared = lambda s, e: np.concatenate([a["L2_ffn_" + s][None], a["L2_ffn_" + e]])
    io["L2_router_W"], io["L2_router_b"] = a["L2_ffn_router_W"], a["L2_ffn_router_b"]
    io["L2_W1"], io["L2_W2"], io["L2_b2"] = shared("sW1", "eW1"), shared("sW2", "eW2"), shared("sb2", "eb2")
    io["L2_b1"] = shared("sb1", "eb1").reshape(16, 1, P).transpose(0, 2, 1)
    io["L1_rhsT"] = a["L1_ffn_rhs"].T
    io["L3_wT"], io["L3_bias"] = a["L3_ffn_weight"].T, a["L3_ffn_bias"]

    io["key_pos"] = a["itok_BxS2_1_8191"]
    io["mask"] = a["mask_BxSxS2_if1"]
    io["maskT"] = a["mask_BxSxS2_if1"].transpose(0, 2, 1)
    io["tri"] = a["mask_SxS2_bk0"]
    io["triT"] = np.ascontiguousarray(a["mask_SxS2_bk0"].T)
    io["pad"] = a["mask_BxS2_bk1"].reshape(B * S2)
    io["padT"] = np.ascontiguousarray(a["mask_BxS2_bk1"].reshape(B, KT, P).transpose(2, 0, 1))
    ratio = 2.0 ** (-8.0 / HEADS)
    rest = np.array([ratio ** i for i in range(1, HEADS + 1)], np.float32)
    io["c_slopes"] = np.zeros((9, HEADS, S), np.float32)
    for part in range(3):
        top = (rest.view(np.uint32) & np.uint32(0xFFFF0000)).view(np.float32)
        io["c_slopes"][3 * part:3 * part + 3] = top[None, :, None]
        rest = rest - top

    io["L1_wq"] = a["L1_xattn_w_query"].transpose(1, 2, 0)
    io["L1_wk"] = a["L1_xattn_w_key"].transpose(1, 2, 0)
    io["L1_wv"] = a["L1_xattn_w_value"].reshape(D, WIDE_V)
    io["L1_wo"] = a["L1_xattn_w_projection"].transpose(0, 2, 1).reshape(WIDE_V, D)
    io["L1_bq"] = a["L1_xattn_b_query"].reshape(HEADS, WIDE_E).T
    io["L1_bv"] = a["L1_xattn_b_value"].reshape(W_PAIRS, P).T
    io["L1_bp"] = a["L1_xattn_b_projection"]



def build(nc, io):
    res = Resident()
    with Phase(nc, "res") as ph:
        res.X = ph.sb("X", [P, NTILE, D])
        res.xn = ph.sb("xn", [P, NTILE, D])
        res.xnT = ph.sb("xnT", [P, NTILE * P])
        res.gates = ph.sb("gates", [P, 8])
        res.ident = ph.sb("ident", [P, P])
        res.identb = ph.sb("identb", [P, P], BF16)
        res.ones = ph.sb("ones", [P, P])
        res.onesb = ph.sb("onesb", [P, P], BF16)
        load_phase(nc, io, res)
        with Phase(nc, "ahead") as pa:
            res.G = pa.sb("G", [P, HEADS, D])
            res.q_bias = pa.sb("q_bias", [P, HEADS])
            res.wv1 = pa.sb("wv1", [P, WIDE_V])
            res.wo1 = pa.sb("wo1", [P, W_PAIRS, D])
            res.bias_row1 = pa.sb("bias_row1", [1, D])
            res.keys = [nc.dram_tensor(f"keys{i}", [B, 3, D, S2], BF16).ap() for i in (2, 3)]
            norm_phase(nc, io, res, "n0")
            layer0_attention(nc, io, res)
            norm_phase(nc, io, res, "n1")
            layer0_experts(nc, io, res)
            norm_phase(nc, io, res, "n2")
            layer1_attention(nc, io, res)
        Phase.clear_used(nc)
        with Phase(nc, "narrow") as pn:
            res.narrow = NarrowBuffers(nc, pn)
            norm_phase(nc, io, res, "n3", transposed=False)
            layer1_int8(nc, io, res)
            norm_phase(nc, io, res, "n4")
            narrow_attention(nc, io, res, LayerTwo)
            Phase.clear_used(nc)
            with Phase(nc, "masks") as pm:
                res.narrow.add_masks(pm)
                norm_phase(nc, io, res, "n5")
                layer2_experts(nc, io, res)
                norm_phase(nc, io, res, "n6")
                narrow_attention(nc, io, res, LayerThree)
        Phase.clear_used(nc)
        norm_phase(nc, io, res, "n7", transposed=False)
        layer3_ternary(nc, io, res)
        store_phase(nc, io, res)



def layouts(inputs):
    a = {k: np.asarray(v) for k, v in inputs.items()}
    tr = lambda w: np.ascontiguousarray(w.T)
    io = {
        "x": a["x"].reshape(B * S, D),
        "ctxT": np.ascontiguousarray(a["ctx_1024"].reshape(B * S2, D).T),
        "g_xattn": a["g_xattn"], "g_ffn": a["g_ffn"],
        "c_ident": np.eye(P, dtype=np.float32),
    }
    for w in ("Wq", "Wk", "Wv", "Wo"):
        io[f"L0_{w}T"] = tr(a[f"L0_xattn_{w}"])
        io[f"L3_{w}T"] = tr(a[f"L3_xattn_{w}"])
    for b in ("bq", "bk", "bv", "bo"):
        io[f"L0_{b}"] = a[f"L0_xattn_{b}"]
        io[f"L3_{b}"] = a[f"L3_xattn_{b}"]
    for w in ("q", "k", "v", "o"):
        io[f"L2_W{w}T"] = tr(a[f"L2_xattn_W_{w}"])
    more_layouts(a, io)
    return {k: np.ascontiguousarray(v) for k, v in io.items()}


def kernel(**inputs):
    import concourse.bacc as bacc
    from concourse.bass_utils import run_bass_kernel_spmd

    nc = bacc.Bacc("TRN2", target_bir_lowering=False, num_devices=1)
    arrays = layouts(inputs)
    io = {n: nc.dram_tensor(f"in_{n}", v.shape, mybir.dt.from_np(v.dtype), kind="ExternalInput").ap() for n, v in arrays.items()}
    io["out"] = nc.dram_tensor("out_0", (B * S, D), F32, kind="ExternalOutput").ap()
    build(nc, io)
    got = run_bass_kernel_spmd(nc, [{f"in_{n}": v for n, v in arrays.items()}], core_ids=[0])
    return got.results[0]["out_0"].reshape(B, S, D)
```

```python
from contextlib import ExitStack

import numpy as np

import concourse.bass as bass
from concourse import mybir

P = 128
B, S, S2, D = 8, 256, 512, 128
NTILE = B * S // P
QT = S // P
KT = S2 // P
CHUNK = 512
NCHUNK = B * S // CHUNK
HEADS = 16
BIG = 2.0 ** 100
LN_EPS = 1e-5

F32 = mybir.dt.float32
BF16 = mybir.dt.bfloat16
I32 = mybir.dt.int32
U8 = mybir.dt.uint8
U32 = mybir.dt.uint32
ALU = mybir.AluOpType
ACT = mybir.ActivationFunctionType
AX = mybir.AxisListType


class Phase:

    used = []

    def __init__(self, nc, name):
        self.nc, self.name, self.stack = nc, name, ExitStack()

    def __enter__(self):
        self.stack.__enter__()
        return self

    def __exit__(self, *exc):
        return self.stack.__exit__(*exc)

    def sb(self, name, shape, dt=F32):
        return self.stack.enter_context(self.nc.sbuf_tensor(f"{self.name}_{name}", shape, dt))

    def ps(self, name, shape, dt=F32):
        return self.stack.enter_context(self.nc.psum_tensor(f"{self.name}_{name}", shape, dt))

    def sem(self, name):
        handle = self.nc.alloc_semaphore(f"{self.name}_{name}")
        Phase.used.append(handle)
        return handle

    @staticmethod
    def clear_used(nc):
        nc.clear_and_free_semaphores(Phase.used)
        nc.all_engine_barrier()
        Phase.used.clear()

    def block(self):
        return self.nc.Block(no_gpsimd_drain=True)


class Resident:
    pass


CTX_LOADS = 4


def load_phase(nc, io, res):
    with Phase(nc, "load") as ph:
        loaded, gates_in, gates_done = ph.sem("loaded"), ph.sem("gates_in"), ph.sem("gates_done")
        ones_done, cast_done = ph.sem("ones_done"), ph.sem("cast_done")
        raw_gates = ph.sb("raw_gates", [P, 8])
        res.qkv_in, res.ctx_in = ph.sem("qkv_in"), [ph.sem(f"ctx_in{i}") for i in range(CTX_LOADS)]
        x_in = [ph.sem(f"x_in{c}") for c in range(NCHUNK)]
        stats_done, aggr_done, zeroed = ph.sem("stats_done"), ph.sem("aggr_done"), ph.sem("zeroed")
        with ph.block() as block:
            @block.sync
            def _(sp):
                sp.dma_start(raw_gates[:, 0:4], io["g_xattn"].partition_broadcast(P)).then_inc(gates_in, 16)
                sp.dma_start(raw_gates[:, 4:8], io["g_ffn"].partition_broadcast(P)).then_inc(gates_in, 16)
                sp.dma_start(res.ident[:], io["c_ident"]).then_inc(loaded, 16)
                for c in range(NCHUNK):
                    sp.dma_start(res.X[:, 4 * c:4 * c + 4, :], io["x"].rearrange("(t p) d -> p t d", p=P)[:, 4 * c:4 * c + 4]).then_inc(x_in[c], 16)
                sp.wait_ge(zeroed, 1)
                for k, w in enumerate("qkv"):
                    sp.dma_start(res.w_qkv[:, k * D:(k + 1) * D], io[f"L0_W{w}T"]).then_inc(res.qkv_in, 16)
                    sp.dma_start(res.b_qkv[0:1, k * D:(k + 1) * D], io[f"L0_b{w}"].unsqueeze(0)).then_inc(res.qkv_in, 16)
                for i in range(CTX_LOADS):
                    n = NTILE // CTX_LOADS
                    sp.dma_start(res.ctxT[:, n * i:n * i + n], io["ctxT"].rearrange("d (t n c) -> d t n c", n=P, c=2)[:, n * i:n * i + n]).then_inc(res.ctx_in[i], 16)
                sp.wait_ge(loaded, 16)

            @block.scalar
            def _(act):
                act.wait_ge(gates_in, 32)
                act.activation(res.gates[:], raw_gates[:], ACT.Tanh).then_inc(gates_done, 1)
                act.wait_ge(gates_done, 1)

            @block.vector
            def _(dve):
                dve.memset(res.b_qkv[:], 0.0).then_inc(zeroed, 1)
                dve.memset(res.ones[:], 1.0).then_inc(ones_done, 1)
                dve.memset(res.onesb[:], 1.0).then_inc(ones_done, 1)
                dve.wait_ge(loaded, 16)
                dve.tensor_copy(res.identb[:], res.ident[:]).then_inc(cast_done, 1)
                dve.wait_ge(cast_done, 1)
                dve.wait_ge(ones_done, 2)
                for c in range(NCHUNK):
                    dve.wait_ge(x_in[c], 16)
                    tile_stats(dve, res, 4 * c, 4, 4 * c, stats_done, aggr_done)
                dve.wait_ge(aggr_done, NTILE)


def tile_stats(dve, res, t, n, base, stats_done, aggr_done):
    for k in range(n):
        tile = bass.ds(t + k, 1)
        dve.bn_stats(res.stats[:, tile, :].rearrange("p o s -> p (o s)"), res.X[:, tile, :].rearrange("p o d -> p (o d)")).then_inc(stats_done, 1)
    dve.wait_ge(stats_done, base + n)
    for k in range(n):
        tile = bass.ds(t + k, 1)
        dve.bn_aggr(res.mv[:, tile, :].rearrange("p o s -> p (o s)"), res.stats[:, tile, :].rearrange("p o s -> p (o s)")).then_inc(aggr_done, 1)


def norm_phase(nc, io, res, name, transposed=True):
    with Phase(nc, name) as ph:
        std = ph.sb("std", [P, NTILE])
        r0 = ph.sb("r0", [P, NTILE])
        rr = ph.sb("rr", [P, NTILE])
        rstd = ph.sb("rstd", [P, NTILE])
        var_eps = ph.sb("var_eps", [P, NTILE])
        psT = [ph.ps(f"psT{i}", [P, CHUNK]) for i in range(2)]
        var_done, std_done, newton = ph.sem("var_done"), ph.sem("std_done"), ph.sem("newton")
        xn_done, xn_pool, turned, copied = ph.sem("xn_done"), ph.sem("xn_pool"), ph.sem("turned"), ph.sem("copied")
        with ph.block() as block:
            @block.vector
            def _(dve):
                dve.tensor_scalar(var_eps[:], res.mv[:, :, 1], LN_EPS, None, ALU.add).then_inc(var_done, 1)
                dve.wait_ge(std_done, 1)
                dve.reciprocal(r0[:], std[:]).then_inc(newton, 1)
                dve.wait_ge(newton, 1)
                dve.tensor_tensor(rr[:], r0[:], r0[:], ALU.mult).then_inc(newton, 1)
                dve.wait_ge(newton, 2)
                dve.tensor_tensor(std[:], rr[:], var_eps[:], ALU.mult).then_inc(newton, 1)
                dve.wait_ge(newton, 3)
                dve.tensor_scalar(rr[:], std[:], -0.5, 1.5, ALU.mult, ALU.add).then_inc(newton, 1)
                dve.wait_ge(newton, 4)
                dve.tensor_tensor(rstd[:], r0[:], rr[:], ALU.mult).then_inc(newton, 1)
                dve.wait_ge(newton, 5)
                for c in range(NCHUNK):
                    for k in range(3):
                        t = 4 * c + k
                        dve.tensor_scalar(res.xn[:, t, :], res.X[:, t, :], res.mv[:, t, 0:1], rstd[:, t:t + 1],
                                          ALU.subtract, ALU.mult).then_inc(xn_done, 1)
                dve.wait_ge(xn_done, 3 * NCHUNK)

            @block.gpsimd
            def _(pool):
                pool.wait_ge(newton, 5)
                for c in range(NCHUNK):
                    t = 4 * c + 3
                    pool.tensor_scalar(res.xn[:, t, :], res.X[:, t, :], res.mv[:, t, 0:1], rstd[:, t:t + 1],
                                       ALU.subtract, ALU.mult).then_inc(xn_pool, 1)
                pool.wait_ge(xn_pool, NCHUNK)

            @block.scalar
            def _(act):
                act.wait_ge(var_done, 1)
                act.activation(std[:], var_eps[:], ACT.Sqrt).then_inc(std_done, 1)
                if transposed:
                    for c in range(NCHUNK):
                        act.wait_ge(turned, c + 1)
                        act.copy(res.xnT[:, c * CHUNK:(c + 1) * CHUNK], psT[c % 2][:]).then_inc(copied, 1)
                    act.wait_ge(copied, NCHUNK)

            @block.tensor
            def _(pe):
                if transposed:
                    for c in range(NCHUNK):
                        if c >= 2:
                            pe.wait_ge(copied, c - 1)
                        pe.wait_ge(xn_done, 3 * c + 3)
                        pe.wait_ge(xn_pool, c + 1)
                        for k in range(4):
                            last = pe.transpose(psT[c % 2][:, k * P:(k + 1) * P], res.xn[:, 4 * c + k, :], res.ident[:])
                        last.then_inc(turned, 1)


def store_phase(nc, io, res):
    with Phase(nc, "store") as ph:
        stored = ph.sem("stored")
        with ph.block() as block:
            @block.sync
            def _(sp):
                sp.dma_start(io["out"].rearrange("(t p) d -> p t d", p=P), res.X[:]).then_inc(stored, 16)
                sp.wait_ge(stored, 16)



L0_GROUPS, L0_HEADS, L0_E = 8, 8, 2
L0_KEYS = 2 * L0_GROUPS
L0_SCORES = L0_GROUPS * L0_HEADS * L0_KEYS


def layer0_attention(nc, io, res):
    scale = 1.0 / float(np.sqrt(L0_E))
    with Phase(nc, "a0") as ph:
        Q = ph.sb("Q", [P, NTILE, D])
        K = ph.sb("K", [P, NTILE, 2, D])
        V = ph.sb("V", [P, NTILE, 2, D])
        O = ph.sb("O", [P, NTILE, D])
        attend_layer0(nc, io, res, Q, K, V, O, scale)
        with Phase(nc, "a0o") as po:
            project_out(nc, io, res, po, O, "L0_WoT", "L0_bo", res.gates[:, 0:1])


def attend_layer0(nc, io, res, Q, K, V, O, scale):
    n_chunks = B * S2 // CHUNK
    ctxT = res.ctxT
    LEAD = 4
    fold_scale = 1.0 / float(np.sqrt(WIDE_E))
    full = [P, L0_GROUPS, L0_HEADS, L0_KEYS]
    rows = L0_GROUPS * L0_HEADS
    with Phase(nc, "a0a") as ph:
        m0 = [ph.sb(f"m0_{i}", full) for i in range(2)]
        sc = [ph.sb(f"sc_{i}", full) for i in range(2)]
        ex = [ph.sb(f"ex_{i}", full) for i in range(2)]
        pv0 = [ph.sb(f"pv0_{i}", full) for i in range(2)]
        pv1 = ph.sb("pv1", full)
        m1 = ph.sb("m1", full)
        mx = [ph.sb(f"mx_{i}", [P, rows]) for i in range(2)]
        den = ph.sb("den", [P, rows])
        rec = ph.sb("rec", [P, rows])
        osum = ph.sb("osum", [P, 2, rows])
        m0_done, m1_done, add_done, max_done = (ph.sem(n) for n in ("m0_done", "m1_done", "add_done", "max_done"))
        sub_done, exp_done, pv0_done, pv1_done = (ph.sem(n) for n in ("sub_done", "exp_done", "pv0_done", "pv1_done"))
        den_done, rec_done, osum_done, norm_done = (ph.sem(n) for n in ("den_done", "rec_done", "osum_done", "norm_done"))

        w1q, w1k = ph.sb("w1q", [WIDE_E, HEADS, D]), ph.sb("w1k", [WIDE_E, HEADS, D])
        b1q, b1v, b1p = ph.sb("b1q", [WIDE_E, HEADS]), ph.sb("b1v", [P, W_PAIRS]), ph.sb("b1p", [1, D])
        wk = [ph.sb(f"wk{i}", [P, D]) for i in range(2)]
        bk = ph.sb("bk", [1, D])
        minus_i = ph.sb("minus_i", [P, P], BF16)
        parts = [ph.sb(f"parts{i}", [P, 3, CHUNK], BF16) for i in range(2)]
        psQ, psKV = ph.ps("psQ", [P, D]), ph.ps("psKV", [P, 2, 2 * D])
        qkv_made, qkv_out = ph.sem("qkv_made"), ph.sem("qkv_out")
        psG = [ph.ps(f"psG{i}", [P, 4, D]) for i in range(2)]
        psB = ph.ps("psB", [P, HEADS])
        psR = ph.ps("psR", [1, D])
        psK = [ph.ps(f"psK{i}", [P, CHUNK]) for i in range(2)]
        w_in, folded, fold_copied = ph.sem("w_in"), ph.sem("folded"), ph.sem("fold_copied")
        minus_done = ph.sem("minus_done")
        k_made, k_cut = [ph.sem(f"k_made{i}") for i in range(2)], [ph.sem(f"k_cut{i}") for i in range(2)]
        k_stored = [ph.sem(f"k_stored{i}") for i in range(2)]
        n_w = 10

        def q_of(t, e):
            v = Q[:, bass.ds(t, 1), :].rearrange("p o (l h e) -> p (o l) h e", h=L0_HEADS, e=L0_E)
            return v[:, :, :, e:e + 1].to_broadcast(full)

        def kv_of(M, t, e):
            v = M[:, bass.ds(t, 1), :, :].rearrange("p o c (s h e) -> p e o h (c s)", h=L0_HEADS, e=L0_E)
            return v[:, e, :, :, :].to_broadcast(full)

        def flat(a):
            return a[:].rearrange("p l h s -> p (l h) s")

        with ph.block() as block:
            @block.gpsimd
            def _(pool):
                def products(t, b):
                    pool.wait_ge(qkv_out, 3 * t + 3)
                    pool.tensor_tensor(m0[b][:], q_of(t, 0), kv_of(K, t, 0), ALU.mult).then_inc(m0_done, 1)

                def subtract(t, b):
                    pool.wait_ge(max_done, t + 1)
                    pool.tensor_tensor(flat(sc[b]), flat(sc[b]), mx[b][:].unsqueeze(2).to_broadcast([P, rows, L0_KEYS]),
                                       ALU.subtract).then_inc(sub_done, 1)

                def weighted(t, b):
                    pool.wait_ge(exp_done, t + 1)
                    pool.tensor_tensor(pv0[b][:], ex[b][:], kv_of(V, t, 0), ALU.mult).then_inc(pv0_done, 1)

                def step(v, b, first=False, last=False):
                    weighted(v - 1, 1 - b)
                    if not last:
                        pool.wait_ge(add_done, v)
                        products(v + 1, 1 - b)
                    subtract(v, b)

                products(0, 0)
                products(1, 1)
                subtract(0, 0)
                with pool.Fori(0, (NTILE - 2) // 2) as i:
                    for k in range(2):
                        step(2 * i + 1 + k, (1 + k) % 2)
                step(NTILE - 1, 1, last=True)
                weighted(NTILE - 1, 1)

            @block.sync
            def _(sp):
                sp.dma_start(w1q[:], io["L1_wq"].rearrange("n e d -> e n d")).then_inc(w_in, 16)
                sp.dma_start(w1k[:], io["L1_wk"].rearrange("n e d -> e n d")).then_inc(w_in, 16)
                sp.dma_start(b1q[:], io["L1_bq"]).then_inc(w_in, 16)
                sp.dma_start(b1v[:], io["L1_bv"]).then_inc(w_in, 16)
                sp.dma_start(b1p[:], io["L1_bp"]).then_inc(w_in, 16)
                sp.dma_start(res.wv1[:], io["L1_wv"]).then_inc(w_in, 16)
                sp.dma_start(res.wo1[:], io["L1_wo"].rearrange("(c p) d -> p c d", p=P)).then_inc(w_in, 16)
                sp.dma_start(wk[0][:], io["L2_WkT"]).then_inc(w_in, 16)
                sp.dma_start(wk[1][:], io["L3_WkT"]).then_inc(w_in, 16)
                sp.dma_start(bk[:], io["L3_bk"].unsqueeze(0)).then_inc(w_in, 16)
                sp.wait_ge(w_in, 16 * n_w)
                with sp.Fori(0, n_chunks) as n:
                    for l in range(2):
                        sp.wait_ge(k_cut[l], 3 * n + 3)
                        for part in range(3):
                            sp.dma_start(res.keys[l][bass.ds(n, 1), :, part].rearrange("o j e t k -> (o j) (e t) k"), parts[l][:, part, :]).then_inc(k_stored[l], 16)
                for l in range(2):
                    sp.wait_ge(k_stored[l], 48 * n_chunks)

            @block.tensor
            def _(pe):
                def chunk(n, first):
                    keys = ctxT[:, bass.ds(2 * n, 2)].rearrange("d t n c -> d (t n c)")
                    for l in range(2):
                        if not first:
                            pe.wait_ge(k_cut[l], 3 * n)
                        last = pe.matmul(psK[l][:], wk[l][:], keys, start=True, stop=False, skip_group_check=True)
                        if l == 1:
                            last = pe.matmul(psK[l][:], bk[:], res.ones[0:1, :].unsqueeze(1).to_broadcast([1, CHUNK // P, P]),
                                             start=False, stop=False, skip_group_check=True)
                        last.then_inc(k_made[l], 1)
                    for part in range(2):
                        for l in range(2):
                            pe.wait_ge(k_cut[l], 3 * n + part + 1)
                            pe.matmul(psK[l][:], minus_i[:], parts[l][:, part, :], start=False, stop=(part == 1), skip_group_check=True).then_inc(k_made[l], 1)

                def project(t):
                    if t > 0:
                        pe.wait_ge(qkv_out, 3 * t)
                    if t % (NTILE // CTX_LOADS) == 0:
                        pe.wait_ge(res.ctx_in[t * CTX_LOADS // NTILE], 16)
                    pe.matmul(psQ[:], res.ones[:], res.b_qkv[:, 0:D], start=True, stop=False)
                    pe.matmul(psQ[:], res.xnT[:, t * P:(t + 1) * P], res.w_qkv[:, 0:D], start=False, stop=True)
                    for two in range(2):
                        pe.matmul(psKV[:, two, :], res.ones[:], res.b_qkv[:, D:], start=True, stop=False)
                        last = pe.matmul(psKV[:, two, :], ctxT[:, t, :, two], res.w_qkv[:, D:], start=False, stop=True)
                    last.then_inc(qkv_made, 1)

                pe.wait_ge(res.qkv_in, 96)
                for t in range(LEAD):
                    project(t)
                pe.wait_ge(w_in, 16 * n_w)
                for n in range(HEADS):
                    if n % 4 == 0 and n >= 8:
                        pe.wait_ge(fold_copied, n // 4 - 1)
                    last = pe.matmul(psG[n // 4 % 2][:, n % 4, :], w1q[:, n, :], w1k[:, n, :], start=True, stop=True)
                    if n % 4 == 3:
                        last.then_inc(folded, 1)
                for n in range(HEADS):
                    pe.matmul(psB[:, n:n + 1], w1k[:, n, :], b1q[:, n:n + 1], start=True, stop=True)
                for p in range(W_PAIRS):
                    pe.matmul(psR[:], b1v[:, p:p + 1], res.wo1[:, p, :], start=(p == 0), stop=False)
                pe.matmul(psR[:], res.ones[0:1, 0:1], b1p[:], start=False, stop=True).then_inc(folded, 1)
                pe.wait_ge(minus_done, 1)
                for n in range(n_chunks):
                    chunk(n, n == 0)
                    for t in range(2 * n + LEAD, min(2 * n + LEAD + 2, NTILE)):
                        project(t)

            @block.scalar
            def _(act):
                def exponential(t, b):
                    act.wait_ge(sub_done, t + 1)
                    act.activation(ex[b][:], sc[b][:], ACT.Exp, scale=scale).then_inc(exp_done, 1)

                def copy_qkv(t):
                    act.wait_ge(qkv_made, t + 1)
                    tile = bass.ds(t, 1)
                    act.copy(Q[:, tile, :].rearrange("p o d -> p (o d)"), psQ[:]).then_inc(qkv_out, 1)
                    act.copy(K[:, tile].rearrange("p o c d -> p (o c) d"), psKV[:, :, 0:D]).then_inc(qkv_out, 1)
                    act.copy(V[:, tile].rearrange("p o c d -> p (o c) d"), psKV[:, :, D:2 * D]).then_inc(qkv_out, 1)

                def cut(n, part, first):
                    for l in range(2):
                        if part == 0 and not first:
                            act.wait_ge(k_stored[l], 48 * n)
                        act.wait_ge(k_made[l], 3 * n + part + 1)
                        act.copy(parts[l][:, part, :], psK[l][:]).then_inc(k_cut[l], 1)

                act.activation(minus_i[:], res.ident[:], ACT.Identity, scale=-1.0).then_inc(minus_done, 1)
                for t in range(LEAD - 1):
                    copy_qkv(t)
                exponential(0, 0)
                copy_qkv(LEAD - 1)
                for c in range(HEADS // 4):
                    act.wait_ge(folded, c + 1)
                    act.activation(res.G[:, 4 * c:4 * c + 4, :], psG[c % 2][:], ACT.Identity, scale=fold_scale).then_inc(fold_copied, 1)
                exponential(1, 1)
                act.wait_ge(folded, HEADS // 4 + 1)
                act.activation(res.q_bias[:], psB[:], ACT.Identity, scale=fold_scale).then_inc(fold_copied, 1)
                act.copy(res.bias_row1[:], psR[:]).then_inc(fold_copied, 1)
                for part in range(3):
                    cut(0, part, True)
                copy_qkv(LEAD)
                copy_qkv(LEAD + 1)

                def pair(i, ahead):
                    exponential(2 * i, 0)
                    cut(i, 0, False)
                    cut(i, 1, False)
                    if ahead:
                        copy_qkv(2 * i + LEAD)
                    exponential(2 * i + 1, 1)
                    cut(i, 2, False)
                    if ahead:
                        copy_qkv(2 * i + LEAD + 1)

                with act.Fori(1, n_chunks - LEAD // 2) as i:
                    pair(i, True)
                for i in range(n_chunks - LEAD // 2, n_chunks):
                    pair(i, False)
                act.wait_ge(fold_copied, HEADS // 4 + 2)

            @block.vector
            def _(dve):
                def front(t, b, first=False):
                    dve.wait_ge(qkv_out, 3 * t + 3)
                    dve.tensor_tensor(m1[:], q_of(t, 1), kv_of(K, t, 1), ALU.mult).then_inc(m1_done, 1)
                    dve.wait_ge(m0_done, t + 1)
                    dve.wait_ge(m1_done, t + 1)
                    if not first:
                        dve.wait_ge(exp_done, t - 1)
                    dve.tensor_tensor(sc[b][:], m0[b][:], m1[:], ALU.add).then_inc(add_done, 1)
                    dve.wait_ge(add_done, t + 1)
                    dve.tensor_reduce(mx[b][:], flat(sc[b]), AX.X, ALU.max).then_inc(max_done, 1)

                def back(t, b):
                    dve.wait_ge(exp_done, t + 1)
                    dve.tensor_reduce(den[:], flat(ex[b]), AX.X, ALU.add).then_inc(den_done, 1)
                    dve.tensor_tensor(pv1[:], ex[b][:], kv_of(V, t, 1), ALU.mult).then_inc(pv1_done, 1)
                    dve.wait_ge(den_done, t + 1)
                    dve.reciprocal(rec[:], den[:]).then_inc(rec_done, 1)
                    dve.wait_ge(pv1_done, t + 1)
                    dve.tensor_reduce(osum[:, 1, :], flat(pv1), AX.X, ALU.add).then_inc(osum_done, 1)
                    dve.wait_ge(pv0_done, t + 1)
                    dve.tensor_reduce(osum[:, 0, :], flat(pv0[b]), AX.X, ALU.add).then_inc(osum_done, 1)
                    dve.wait_ge(rec_done, t + 1)
                    dve.wait_ge(osum_done, 2 * (t + 1))
                    dve.tensor_tensor(O[:, bass.ds(t, 1), :].rearrange("p o (r e) -> p (o r) e", e=L0_E),
                                      osum[:].rearrange("p e r -> p r e"),
                                      rec[:].unsqueeze(2).to_broadcast([P, rows, L0_E]), ALU.mult).then_inc(norm_done, 1)

                front(0, 0, first=True)
                front(1, 1, first=True)
                back(0, 0)
                with dve.Fori(0, (NTILE - 2) // 2) as i:
                    for k in range(2):
                        front(2 * i + 2 + k, k)
                        back(2 * i + 1 + k, (1 + k) % 2)
                back(NTILE - 1, 1)
                dve.wait_ge(norm_done, NTILE)


def project_out(nc, io, res, ph, O, wo_name, bo_name, gate):
    wo = ph.sb("wo", [P, D])
    bo = ph.sb("bo", [P, D])
    OT = [ph.sb(f"OT{i}", [P, CHUNK]) for i in range(2)]
    psT = [ph.ps(f"psT{i}", [P, CHUNK]) for i in range(2)]
    psY = [ph.ps(f"psY{i}", [P, CHUNK]) for i in range(2)]
    w_in, turned, copied, projected, added = (ph.sem(n) for n in ("w_in", "turned", "copied", "projected", "added"))
    stats_done, aggr_done, zeroed = ph.sem("stats_done"), ph.sem("aggr_done"), ph.sem("zeroed")
    with ph.block() as block:
        @block.sync
        def _(sp):
            sp.dma_start(wo[:], io[wo_name]).then_inc(w_in, 16)
            sp.wait_ge(zeroed, 1)
            sp.dma_start(bo[0:1, :], io[bo_name].unsqueeze(0)).then_inc(w_in, 16)

        @block.tensor
        def _(pe):
            def turn(c):
                if c >= 2:
                    pe.wait_ge(copied, c - 1)
                for k in range(4):
                    last = pe.transpose(psT[c % 2][:, k * P:(k + 1) * P], O[:, 4 * c + k, :], res.ident[:])
                last.then_inc(turned, 1)

            turn(0)
            pe.wait_ge(w_in, 32)
            for c in range(NCHUNK):
                if c + 1 < NCHUNK:
                    turn(c + 1)
                pe.wait_ge(copied, c + 1)
                if c >= 2:
                    pe.wait_ge(added, c - 1)
                for k in range(4):
                    y = psY[c % 2][:, k * P:(k + 1) * P]
                    pe.matmul(y, res.ones[:], bo[:], start=True, stop=False)
                    last = pe.matmul(y, OT[c % 2][:, k * P:(k + 1) * P], wo[:], start=False, stop=True)
                last.then_inc(projected, 1)

        @block.scalar
        def _(act):
            for c in range(NCHUNK):
                act.wait_ge(turned, c + 1)
                if c >= 2:
                    act.wait_ge(projected, c - 1)
                act.copy(OT[c % 2][:], psT[c % 2][:]).then_inc(copied, 1)

        @block.vector
        def _(dve):
            dve.memset(bo[:], 0.0).then_inc(zeroed, 1)
            for c in range(NCHUNK):
                dve.wait_ge(projected, c + 1)
                x = res.X[:, 4 * c:4 * c + 4, :].rearrange("p t d -> p (t d)")
                dve.scalar_tensor_tensor(x, psY[c % 2][:], gate, x, ALU.mult, ALU.add).then_inc(added, 1)
                dve.wait_ge(added, c + 1)
                tile_stats(dve, res, 4 * c, 4, 4 * c, stats_done, aggr_done)
            dve.wait_ge(aggr_done, NTILE)



def experts(nc, io, res, name, E, H, act_fn, weights, biases, out_bias, combine, router, beside):
    HC = H // P
    w1_dram, w2_dram = weights
    HB = max(2, HC)
    with Phase(nc, name) as ph:
        router = router(ph)
        ahead = beside(ph)
        stats_done, aggr_done = ph.sem("stats_done"), ph.sem("aggr_done")
        w1 = [ph.sb(f"w1_{i}", [P, H]) for i in range(2)]
        w2 = [ph.sb(f"w2_{i}", [P, HC, D]) for i in range(2)]
        b1 = [ph.sb(f"b1_{i}", [P, HC]) for i in range(2)]
        b2 = ph.sb("b2", [E, D])
        hT = [ph.sb(f"hT{i}", [P, HC, CHUNK]) for i in range(2)]
        cT = ph.sb("cT", [E, NTILE, P])
        psH = [ph.ps(f"psH{i}", [P, CHUNK]) for i in range(HB)]
        psY = [ph.ps(f"psY{i}", [P, 4, D]) for i in range(2)]
        w_in = [ph.sem(f"w_in{i}") for i in range(2)]
        b2_in, hidden, acted, made, added = (ph.sem(n) for n in ("b2_in", "hidden", "acted", "made", "added"))
        c_turned, c_copied, b2_made, b2_added = (ph.sem(n) for n in ("c_turned", "c_copied", "b2_made", "b2_added"))
        n_hidden = NCHUNK * HC

        with ph.block() as block:
            @block.sync
            def _(sp):
                router.sync(sp)
                def load(e, b):
                    ds = bass.ds(e, 1)
                    sp.dma_start(w1[b][:], w1_dram[ds].rearrange("o p h -> p (o h)")).then_inc(w_in[b], 16)
                    sp.dma_start(w2[b][:], w2_dram[ds].rearrange("o (c p) d -> p (o c) d", p=P)).then_inc(w_in[b], 16)
                    sp.dma_start(b1[b][:], biases[ds].rearrange("o p c -> p (o c)")).then_inc(w_in[b], 16)

                sp.dma_start(b2[:], out_bias).then_inc(b2_in, 16)
                for b in range(2):
                    load(b, b)
                with sp.Fori(1, E // 2) as i:
                    for b in range(2):
                        sp.wait_ge(made, (2 * i + b - 1) * NCHUNK)
                        load(2 * i + b, b)

            @block.tensor
            def _(pe):
                def expert(e, b, first):
                    pe.wait_ge(w_in[b], 48 * (e // 2 + 1) if first else 48 * (first_i[0] + 1))
                    for c in range(NCHUNK + 1):
                        if c < NCHUNK:
                            for k in range(HC):
                                n = c * HC + k
                                bank = n % HB
                                if not first or n >= HB:
                                    pe.wait_ge(acted, e * n_hidden + n - HB + 1)
                                pe.matmul(psH[bank][:], w1[b][:, k * P:(k + 1) * P], res.xnT[:, c * CHUNK:(c + 1) * CHUNK],
                                          start=True, stop=True).then_inc(hidden, 1)
                        if c >= 1:
                            m = c - 1
                            pe.wait_ge(acted, e * n_hidden + c * HC)
                            if not first or m >= 2:
                                pe.wait_ge(added, e * NCHUNK + m - 1)
                            for t in range(4):
                                for k in range(HC):
                                    last = pe.matmul(psY[m % 2][:, t, :], hT[m % 2][:, k, t * P:(t + 1) * P], w2[b][:, k, :],
                                                     start=(k == 0), stop=(k == HC - 1))
                            last.then_inc(made, 1)

                first_i = [0]
                router.tensor(pe)
                expert(0, 0, True)
                first_i[0] = 0
                expert(1, 1, False)
                with pe.Fori(1, E // 2) as i:
                    first_i[0] = i
                    for b in range(2):
                        expert(2 * i + b, b, False)
                pe.wait_ge(b2_in, 16)
                for c in range(NCHUNK):
                    pe.wait_ge(acted, E * n_hidden)
                    if c >= 2:
                        pe.wait_ge(c_copied, c - 1)
                    for t in range(4):
                        last = pe.transpose(psH[c % 2][0:E, t * P:(t + 1) * P], combine[:, :, 4 * c + t], res.ident[:])
                    last.then_inc(c_turned, 1)
                for c in range(NCHUNK):
                    pe.wait_ge(c_copied, c + 1)
                    pe.wait_ge(added, E * NCHUNK)
                    if c >= 2:
                        pe.wait_ge(b2_added, c - 1)
                    for t in range(4):
                        last = pe.matmul(psY[c % 2][:, t, :], cT[:, 4 * c + t, :], b2[:], start=True, stop=True)
                    last.then_inc(b2_made, 1)

            @block.scalar
            def _(act):
                def expert(e, b, first, i):
                    act.wait_ge(w_in[b], 48 * (i + 1))
                    for c in range(NCHUNK):
                        if not first or c >= 2:
                            act.wait_ge(made, e * NCHUNK + c - 1)
                        for k in range(HC):
                            n = c * HC + k
                            act.wait_ge(hidden, e * n_hidden + n + 1)
                            act.activation(hT[c % 2][:, k, :], psH[n % HB][:], act_fn, bias=b1[b][:, k:k + 1]).then_inc(acted, 1)

                expert(0, 0, True, 0)
                router.scalar(act)
                expert(1, 1, False, 0)
                with act.Fori(1, E // 2) as i:
                    for b in range(2):
                        expert(2 * i + b, b, False, i)
                for c in range(NCHUNK):
                    act.wait_ge(c_turned, c + 1)
                    act.copy(cT[:, 4 * c:4 * c + 4, :].rearrange("e t p -> e (t p)"), psH[c % 2][0:E, :]).then_inc(c_copied, 1)

            @block.vector
            def _(dve):
                def expert(e):
                    for c in range(NCHUNK):
                        dve.wait_ge(made, e * NCHUNK + c + 1)
                        for k in range(4):
                            t = 4 * c + k
                            last = dve.scalar_tensor_tensor(res.X[:, t, :], psY[c % 2][:, k, :], combine[:, bass.ds(e, 1), t],
                                                            res.X[:, t, :], ALU.mult, ALU.add)
                        last.then_inc(added, 1)
                router.shared(dve)
                expert(0)
                router.vector(dve)
                with dve.Fori(1, E) as e:
                    expert(e)
                for c in range(NCHUNK):
                    dve.wait_ge(b2_made, c + 1)
                    x = res.X[:, 4 * c:4 * c + 4, :]
                    dve.tensor_tensor(x, psY[c % 2][:], x, ALU.add).then_inc(b2_added, 1)
                    dve.wait_ge(b2_added, c + 1)
                    tile_stats(dve, res, 4 * c, 4, 4 * c, stats_done, aggr_done)
                dve.wait_ge(aggr_done, NTILE)

            @block.gpsimd
            def _(pool):
                ahead.gpsimd(pool)


class Router:

    def __init__(self, ph, io, res, E, top_k, w_name, b_name):
        self.io, self.res, self.E, self.top_k, self.w_name, self.b_name = io, res, E, top_k, w_name, b_name
        self.wide = [P, NTILE, E]
        self.wg, self.bg, self.iota = ph.sb("wg", [P, E]), ph.sb("bg", [P, E]), ph.sb("iota", [P, E])
        self.prob = ph.sb("prob", [P, NTILE, E])
        self.top, self.den, self.rec = ph.sb("top", [P, NTILE]), ph.sb("den", [P, NTILE]), ph.sb("rec", [P, NTILE])
        self.val, self.idx, self.idxf = ph.sb("val", [P, NTILE, 8]), ph.sb("idx", [P, NTILE, 8], U32), ph.sb("idxf", [P, NTILE, 8])
        self.onehot = ph.sb("onehot", [P, top_k, NTILE, E])
        self.psL = ph.ps("psL", [P, NTILE, E])
        self.w_in, self.logits, self.biased, self.topped, self.shifted, self.exped, self.summed, self.inverted, self.normed = (
            ph.sem(n) for n in ("router_in", "logits", "biased", "topped", "shifted", "exped", "summed", "inverted", "normed"))
        self.sorted_, self.indexed, self.floated, self.hot = (ph.sem(n) for n in ("sorted", "indexed", "floated", "hot"))

    def sync(self, sp):
        io, E, w_name, b_name = self.io, self.E, self.w_name, self.b_name
        sp.dma_start(self.wg[:], io[w_name]).then_inc(self.w_in, 16)
        sp.dma_start(self.iota[:], io["c_iota"][0:E].partition_broadcast(P)).then_inc(self.w_in, 16)
        if b_name:
            sp.dma_start(self.bg[:], io[b_name].partition_broadcast(P)).then_inc(self.w_in, 16)

    def tensor(self, pe):
        res, b_name = self.res, self.b_name
        pe.wait_ge(self.w_in, 48 if b_name else 32)
        for t in range(NTILE):
            last = pe.matmul(self.psL[:, t, :], res.xnT[:, t * P:(t + 1) * P], self.wg[:], start=True, stop=True)
        last.then_inc(self.logits, 1)

    def scalar(self, act):
        act.wait_ge(self.shifted, 1)
        act.activation(self.prob[:], self.prob[:], ACT.Exp).then_inc(self.exped, 1)

    def vector(self, dve):
        wide, b_name, top_k = self.wide, self.b_name, self.top_k
        dve.wait_ge(self.w_in, 48 if b_name else 32)
        dve.wait_ge(self.logits, 1)
        if b_name:
            dve.tensor_tensor(self.prob[:], self.psL[:], self.bg[:].unsqueeze(1).to_broadcast(wide), ALU.add).then_inc(self.biased, 1)
        else:
            dve.tensor_copy(self.prob[:], self.psL[:]).then_inc(self.biased, 1)
        dve.wait_ge(self.biased, 1)
        dve.tensor_reduce(self.top[:], self.prob[:], AX.X, ALU.max).then_inc(self.topped, 1)
        dve.wait_ge(self.topped, 1)
        dve.tensor_tensor(self.prob[:], self.prob[:], self.top[:].unsqueeze(2).to_broadcast(wide), ALU.subtract).then_inc(self.shifted, 1)
        dve.wait_ge(self.exped, 1)
        dve.tensor_reduce(self.den[:], self.prob[:], AX.X, ALU.add).then_inc(self.summed, 1)
        dve.wait_ge(self.summed, 1)
        dve.reciprocal(self.rec[:], self.den[:]).then_inc(self.inverted, 1)
        dve.wait_ge(self.inverted, 1)
        dve.tensor_tensor(self.prob[:], self.prob[:], self.rec[:].unsqueeze(2).to_broadcast(wide), ALU.mult).then_inc(self.normed, 1)
        dve.wait_ge(self.normed, 1)
        for t in range(NTILE):
            dve.max(self.val[:, t, :], self.prob[:, t, :]).then_inc(self.sorted_, 1)
        for t in range(NTILE):
            dve.wait_ge(self.sorted_, t + 1)
            dve.max_index(self.idx[:, t, :], self.val[:, t, :], self.prob[:, t, :]).then_inc(self.indexed, 1)
        dve.wait_ge(self.indexed, NTILE)
        dve.tensor_copy(self.idxf[:], self.idx[:]).then_inc(self.floated, 1)
        dve.wait_ge(self.floated, 1)
        for k in range(top_k):
            dve.tensor_tensor(self.onehot[:, k], self.iota[:].unsqueeze(1).to_broadcast(wide),
                              self.idxf[:, :, k:k + 1].to_broadcast(wide), ALU.is_equal).then_inc(self.hot, 1)
        dve.wait_ge(self.hot, top_k)


def route(nc, io, res, name, E, top_k, w_name, b_name, finish):
    with Phase(nc, name) as ph:
        router = Router(ph, io, res, E, top_k, w_name, b_name)
        with ph.block() as block:
            @block.sync
            def _(sp):
                router.sync(sp)

            @block.tensor
            def _(pe):
                router.tensor(pe)

            @block.scalar
            def _(act):
                router.scalar(act)

            @block.vector
            def _(dve):
                router.vector(dve)
        finish(ph, router.prob, router.val, router.idxf, router.onehot)


L0_EXPERTS, L0_HIDDEN, L0_CAPACITY = 8, 512, 256
ROW_HALVES = L0_CAPACITY // P


def layer0_experts(nc, io, res):
    E = L0_EXPERTS
    with Phase(nc, "f0") as outer:
        xn_dram = nc.dram_tensor("f0_xn", [NTILE * P, D], F32).ap()
        weight = outer.sb("weight", [P, 2, NTILE])
        row = outer.sb("row", [P, 2, NTILE], I32)
        token = outer.sb("token", [P, ROW_HALVES, E], I32)
        route(nc, io, res, "f0r", E, 2, "L0_Wg", None,
              lambda ph, prob, val, idxf, onehot: queue_up(nc, io, res, ph, val, idxf, onehot, xn_dram, weight, row, token))
        queued_experts(nc, io, res, xn_dram, weight, row, token)


def queue_up(nc, io, res, ph, val, idxf, onehot, xn_dram, weight, row, token):
    E, capacity = L0_EXPERTS, L0_CAPACITY
    wide, flat = [P, NTILE, E], [P, 2, NTILE]
    tri_f, tri = ph.sb("tri_f", [P, P]), ph.sb("tri", [P, P], BF16)
    chose = ph.sb("chose", [P, 2, NTILE, E], BF16)
    lane = ph.sb("lane", [P, 1])
    tile_no = ph.sb("tile_no", [P, NTILE])
    place_no_f, place_no = ph.sb("place_no_f", [P, capacity]), ph.sb("place_no", [P, capacity], BF16)
    psC = [ph.ps(f"psC{k}", wide) for k in range(2)]
    psT = ph.ps("psT", [P, E])
    psTab = ph.ps("psTab", [2 * E, capacity])
    psI = ph.ps("psI", [P, ROW_HALVES, 2 * E])
    first, pair, inv = ph.sb("first", [P, E]), ph.sb("pair", [P, NTILE]), ph.sb("inv", [P, NTILE])
    count = ph.sb("count", [P, 2, NTILE, E])
    place, kept, slot = ph.sb("place", flat), ph.sb("kept", flat), ph.sb("slot", flat)
    parts = ph.sb("parts", [P, 2, NTILE, 2, E], BF16)
    hot = ph.sb("hot", [P, 2, NTILE, capacity], BF16)
    table = ph.sb("table", [2 * E, capacity])
    tile_rows = ph.sb("tile_rows", [P, ROW_HALVES, E])
    const_in, xn_out = ph.sem("const_in"), ph.sem("xn_out")
    counted, step, parts_made, hot_made = ph.sem("counted"), ph.sem("step"), ph.sem("parts_made"), ph.sem("hot_made")
    tabled, table_out, table_turned = ph.sem("tabled"), ph.sem("table_out"), ph.sem("table_turned")
    iota_cast, row_made, ones_cast = ph.sem("iota_cast"), ph.sem("row_made"), ph.sem("ones_cast")
    with ph.block() as block:
        @block.sync
        def _(sp):
            sp.dma_start(tri_f[:], io["c_tri"]).then_inc(const_in, 16)
            sp.dma_start(lane[:], io["c_lane"].unsqueeze(1)).then_inc(const_in, 16)
            sp.dma_start(tile_no[:], io["c_iota"].partition_broadcast(P)).then_inc(const_in, 16)
            sp.dma_start(place_no_f[:], io["c_place"].partition_broadcast(P)).then_inc(const_in, 16)
            sp.dma_start(xn_dram.rearrange("(t p) d -> p t d", p=P), res.xn[:]).then_inc(xn_out, 16)
            sp.wait_ge(xn_out, 16)

        @block.scalar
        def _(act):
            act.copy(chose[:], onehot[:]).then_inc(ones_cast, 1)
            act.wait_ge(const_in, 64)
            act.copy(tri[:], tri_f[:]).then_inc(ones_cast, 1)
            act.copy(place_no[:], place_no_f[:]).then_inc(iota_cast, 1)

        @block.tensor
        def _(pe):
            pe.wait_ge(ones_cast, 1)
            for t in range(NTILE):
                last = pe.matmul(psT[:], res.onesb[:], chose[:, 0, t, :], start=(t == 0), stop=(t == NTILE - 1))
            last.then_inc(counted, 1)
            pe.wait_ge(ones_cast, 2)
            for k in range(2):
                pe.matmul(psC[k][:], tri[:], chose[:, k], start=True, stop=False, skip_group_check=True)
                for t in range(NTILE - 1):
                    last = pe.matmul(psC[k][:, t + 1:, :], res.onesb[:], chose[:, k, t:t + 1, :].to_broadcast([P, NTILE - 1 - t, E]),
                                     start=False, stop=(t == NTILE - 2), skip_group_check=True)
                last.then_inc(counted, 1)
            pe.wait_ge(parts_made, 4)
            for k in range(2):
                for t in range(NTILE):
                    pe.wait_ge(hot_made, k * NTILE + t + 1)
                    last = pe.matmul(psTab[:], parts[:, k, t].rearrange("p c e -> p (c e)"), hot[:, k, t, :],
                                     start=(k == 0 and t == 0), stop=(k == 1 and t == NTILE - 1))
            last.then_inc(tabled, 1)
            pe.wait_ge(table_out, 1)
            for half in range(ROW_HALVES):
                last = pe.transpose(psI[:, half, :], table[:, half * P:(half + 1) * P], res.ident[0:2 * E, 0:2 * E])
            last.then_inc(table_turned, 1)

        @block.gpsimd
        def _(pool):
            pool.wait_ge(const_in, 64)
            for k in range(2):
                pool.tensor_tensor(parts[:, k, :, 0, :], onehot[:, k], tile_no[:].unsqueeze(2).to_broadcast(wide), ALU.mult).then_inc(parts_made, 1)
                pool.tensor_tensor(parts[:, k, :, 1, :], onehot[:, k], lane[:].unsqueeze(2).to_broadcast(wide), ALU.mult).then_inc(parts_made, 1)

        @block.vector
        def _(dve):
            dve.tensor_tensor(pair[:], val[:, :, 0], val[:, :, 1], ALU.add).then_inc(step, 1)
            dve.wait_ge(step, 1)
            dve.tensor_scalar(pair[:], pair[:], 1e-9, None, ALU.add).then_inc(step, 1)
            dve.wait_ge(step, 2)
            dve.reciprocal(inv[:], pair[:]).then_inc(step, 1)
            dve.wait_ge(step, 3)
            for k in range(2):
                dve.scalar_tensor_tensor(weight[:, k], val[:, :, k], res.gates[:, 4:5], inv[:], ALU.mult, ALU.mult).then_inc(step, 1)
            dve.wait_ge(iota_cast, 1)
            dve.wait_ge(counted, 1)
            dve.tensor_scalar(first[:], psT[:], float(capacity), None, ALU.min).then_inc(step, 1)
            dve.wait_ge(step, 6)
            for k in range(2):
                done = 6 + 4 * k
                dve.wait_ge(counted, 2 + k)
                if k == 0:
                    dve.tensor_tensor(count[:, 0], psC[0][:], onehot[:, 0], ALU.mult).then_inc(step, 1)
                else:
                    dve.tensor_tensor(count[:, 1], psC[1][:], first[:].unsqueeze(1).to_broadcast(wide), ALU.add).then_inc(step, 1)
                    dve.wait_ge(step, done + 1)
                    dve.tensor_tensor(count[:, 1], count[:, 1], onehot[:, 1], ALU.mult).then_inc(step, 1)
                    done += 1
                dve.wait_ge(step, done + 1)
                dve.tensor_reduce(place[:, k], count[:, k], AX.X, ALU.add).then_inc(step, 1)
                dve.wait_ge(step, done + 2)
                dve.tensor_scalar(kept[:, k], place[:, k], float(capacity), None, ALU.is_le).then_inc(step, 1)
                dve.tensor_scalar(slot[:, k], place[:, k], 1.0, None, ALU.subtract).then_inc(step, 1)
                dve.wait_ge(step, done + 4)
                for t in range(NTILE):
                    dve.tensor_scalar(hot[:, k, t, :], place_no[:], slot[:, k, t:t + 1], None, ALU.is_equal).then_inc(hot_made, 1)
            done = 15
            for k in range(2):
                dve.scalar_tensor_tensor(place[:, k], idxf[:, :, k], float(capacity), slot[:, k], ALU.mult, ALU.add).then_inc(step, 1)
                dve.tensor_tensor(weight[:, k], weight[:, k], kept[:, k], ALU.mult).then_inc(step, 1)
            dve.wait_ge(step, done + 4)
            dve.wait_ge(hot_made, 2 * NTILE)
            dve.tensor_tensor(slot[:], place[:], kept[:], ALU.mult).then_inc(step, 1)
            dve.wait_ge(step, done + 5)
            dve.tensor_copy(row[:], slot[:]).then_inc(row_made, 1)
            dve.wait_ge(tabled, 1)
            dve.tensor_copy(table[:], psTab[:]).then_inc(table_out, 1)
            dve.wait_ge(table_turned, 1)
            dve.tensor_scalar(tile_rows[:], psI[:, :, 0:E], float(P), None, ALU.mult).then_inc(step, 1)
            dve.wait_ge(step, done + 6)
            dve.tensor_tensor(tile_rows[:], tile_rows[:], psI[:, :, E:2 * E], ALU.add).then_inc(step, 1)
            dve.wait_ge(step, done + 7)
            dve.tensor_copy(token[:], tile_rows[:]).then_inc(row_made, 1)
            dve.wait_ge(row_made, 2)


def queued_experts(nc, io, res, xn_dram, weight, row, token):
    E, H = L0_EXPERTS, L0_HIDDEN
    HC = H // P
    C = L0_CAPACITY
    GROUP = 4
    with Phase(nc, "f0e") as ph:
        y_dram = nc.dram_tensor("f0_y", [E * C, D], F32).ap()
        w1 = [ph.sb(f"w1_{i}", [P, H]) for i in range(2)]
        w2 = [ph.sb(f"w2_{i}", [P, HC, D]) for i in range(2)]
        b1 = [ph.sb(f"b1_{i}", [P, HC]) for i in range(2)]
        b2 = [ph.sb(f"b2_{i}", [P, D]) for i in range(2)]
        xg = ph.sb("xg", [P, E, ROW_HALVES, D])
        xgT = [ph.sb(f"xgT{i}", [P, C]) for i in range(2)]
        hT = [ph.sb(f"hT{i}", [P, HC, C]) for i in range(2)]
        y = [ph.sb(f"y{i}", [P, ROW_HALVES, D]) for i in range(2)]
        yg = ph.sb("yg", [P, NTILE, 2, D])
        psT = [ph.ps(f"psT{i}", [P, C]) for i in range(2)]
        psH = [ph.ps(f"psH{i}", [P, C]) for i in range(4)]
        psY = [ph.ps(f"psY{i}", [P, ROW_HALVES, D]) for i in range(2)]
        w_in, x_in = [ph.sem(f"w_in{i}") for i in range(2)], [ph.sem(f"x_in{e}") for e in range(E)]
        turned, x_copied, hidden, acted = ph.sem("turned"), ph.sem("x_copied"), ph.sem("hidden"), ph.sem("acted")
        made, y_copied, y_stored = ph.sem("made"), ph.sem("y_copied"), [ph.sem(f"y_stored{i}") for i in range(2)]
        y_in = [ph.sem(f"y_in{g}") for g in range(2 * NTILE // GROUP)]
        added, zeroed, stats_done, aggr_done = ph.sem("added"), ph.sem("zeroed"), ph.sem("stats_done"), ph.sem("aggr_done")
        with ph.block() as block:
            @block.sync
            def _(sp):
                def load(e, b):
                    one = bass.ds(e, 1)
                    sp.dma_start(w1[b][:], io["L0_W1"][one].rearrange("o d h -> d (o h)")).then_inc(w_in[b], 16)
                    sp.dma_start(w2[b][:], io["L0_W2"][one].rearrange("o (k p) d -> p (o k) d", p=P)).then_inc(w_in[b], 16)
                    sp.dma_start(b1[b][:], io["L0_b1"][one].rearrange("o p k -> p (o k)")).then_inc(w_in[b], 16)
                    sp.dma_start(b2[b][0:1, :], io["L0_b2"][one]).then_inc(w_in[b], 16)

                def store(e, b):
                    sp.wait_ge(y_copied, e + 1)
                    sp.dma_start(y_dram[bass.ds(e * C, C)].rearrange("(r p) d -> p r d", p=P), y[b][:]).then_inc(y_stored[b], 16)

                sp.wait_ge(zeroed, 2)
                load(0, 0)
                load(1, 1)
                with sp.Fori(1, E // 2) as i:
                    for b in range(2):
                        store(2 * (i - 1) + b, b)
                        load(2 * i + b, b)
                for b in range(2):
                    store(E - 2 + b, b)

            @block.gpsimd
            def _(pool):
                for e in range(E):
                    for r in range(ROW_HALVES):
                        pool.indirect_dma_start(out=xg[:, e, r, :], out_offset=None, in_=xn_dram,
                                                in_offset=bass.IndirectOffsetOnAxis(ap=token[:, r, e:e + 1], axis=0)).then_inc(x_in[e], 16)
                for b in range(2):
                    pool.wait_ge(y_stored[b], 16 * (E // 2))
                for t in range(NTILE):
                    for k in range(2):
                        pool.indirect_dma_start(out=yg[:, t, k, :], out_offset=None, in_=y_dram,
                                                in_offset=bass.IndirectOffsetOnAxis(ap=row[:, k, t:t + 1], axis=0)).then_inc(y_in[(2 * t + k) // GROUP], 16)

            @block.tensor
            def _(pe):
                def turn(e):
                    pe.wait_ge(x_in[e], 16 * ROW_HALVES)
                    if e >= 2:
                        pe.wait_ge(x_copied, e - 1)
                    for r in range(ROW_HALVES):
                        last = pe.transpose(psT[e % 2][:, r * P:(r + 1) * P], xg[:, e, r, :], res.ident[:])
                    last.then_inc(turned, 1)

                turn(0)
                for e in range(E):
                    b = e % 2
                    if e + 1 < E:
                        turn(e + 1)
                    pe.wait_ge(w_in[b], 64 * (e // 2 + 1))
                    pe.wait_ge(x_copied, e + 1)
                    for k in range(HC):
                        if e > 0:
                            pe.wait_ge(acted, (e - 1) * HC + k + 1)
                        pe.matmul(psH[k][:], w1[b][:, k * P:(k + 1) * P], xgT[b][:], start=True, stop=True).then_inc(hidden, 1)
                    if e >= 2:
                        pe.wait_ge(y_copied, e - 1)
                    for r in range(ROW_HALVES):
                        pe.matmul(psY[b][:, r, :], res.ones[:], b2[b][:], start=True, stop=False)
                        for k in range(HC):
                            pe.wait_ge(acted, e * HC + k + 1)
                            last = pe.matmul(psY[b][:, r, :], hT[b][:, k, r * P:(r + 1) * P], w2[b][:, k, :], start=False, stop=(k == HC - 1))
                    last.then_inc(made, 1)

            @block.scalar
            def _(act):
                for e in range(E):
                    b = e % 2
                    act.wait_ge(w_in[b], 64 * (e // 2 + 1))
                    if e >= 2:
                        act.wait_ge(made, e - 1)
                    for k in range(HC):
                        act.wait_ge(hidden, e * HC + k + 1)
                        act.activation(hT[b][:, k, :], psH[k][:], ACT.Gelu_apprx_tanh, bias=b1[b][:, k:k + 1]).then_inc(acted, 1)

            @block.vector
            def _(dve):
                def copy_x(e):
                    dve.wait_ge(turned, e + 1)
                    if e >= 2:
                        dve.wait_ge(hidden, (e - 1) * HC)
                    dve.tensor_copy(xgT[e % 2][:], psT[e % 2][:]).then_inc(x_copied, 1)

                for b in range(2):
                    dve.memset(b2[b][:], 0.0).then_inc(zeroed, 1)
                copy_x(0)
                for e in range(E):
                    if e + 1 < E:
                        copy_x(e + 1)
                    dve.wait_ge(made, e + 1)
                    if e >= 2:
                        dve.wait_ge(y_stored[e % 2], 16 * (e // 2))
                    dve.tensor_copy(y[e % 2][:], psY[e % 2][:]).then_inc(y_copied, 1)
                for t in range(NTILE):
                    for k in range(2):
                        n = 2 * t + k
                        if n % GROUP == 0:
                            dve.wait_ge(y_in[n // GROUP], 16 * GROUP)
                        if k == 1:
                            dve.wait_ge(added, n)
                        dve.scalar_tensor_tensor(res.X[:, t, :], yg[:, t, k, :], weight[:, k, t:t + 1], res.X[:, t, :],
                                                 ALU.mult, ALU.add).then_inc(added, 1)
                    dve.wait_ge(added, 2 * t + 2)
                    tile_stats(dve, res, t, 1, t, stats_done, aggr_done)
                dve.wait_ge(aggr_done, NTILE)


class SharedRouter(Router):

    def __init__(self, ph, io, res, combine):
        super().__init__(ph, io, res, 15, 3, "L2_router_W", "L2_router_b")
        self.combine = combine
        self.mask = ph.sb("mask", [P, NTILE, 15])
        self.shared_done, self.step = ph.sem("shared_done"), ph.sem("route_step")

    def shared(self, dve):
        dve.tensor_copy(self.combine[:, 0, :], self.res.gates[:, 6:7].to_broadcast([P, NTILE])).then_inc(self.shared_done, 1)
        dve.wait_ge(self.shared_done, 1)

    def vector(self, dve):
        super().vector(dve)
        mask, onehot, step = self.mask, self.onehot, self.step
        dve.tensor_tensor(mask[:], onehot[:, 0], onehot[:, 1], ALU.add).then_inc(step, 1)
        dve.wait_ge(step, 1)
        dve.tensor_tensor(mask[:], mask[:], onehot[:, 2], ALU.add).then_inc(step, 1)
        dve.wait_ge(step, 2)
        dve.scalar_tensor_tensor(self.combine[:, 1:, :].rearrange("p e t -> p t e"), mask[:], self.res.gates[:, 6:7], self.prob[:],
                                 ALU.mult, ALU.mult).then_inc(step, 1)
        dve.wait_ge(step, 3)


def layer2_experts(nc, io, res):
    E = 16
    with Phase(nc, "f2") as outer:
        combine = outer.sb("combine", [P, E, NTILE])
        experts(nc, io, res, "f2e", E, D, ACT.Relu, (io["L2_W1"], io["L2_W2"]), io["L2_b1"], io["L2_b2"], combine,
                router=lambda ph: SharedRouter(ph, io, res, combine),
                beside=lambda ph: MaskConstants(ph, res.narrow, io))



HEAD_E = D // HEADS
PAIRS = HEADS // 2
COMBOS = ((0, 0), (0, 1), (0, 2), (1, 0), (1, 1), (2, 0))
HEAD_ROWS = len(COMBOS) * HEAD_E
COMBO_ROWS = 2 * HEAD_ROWS
RUNS = ((0, 3), (3, 5), (5, 6))
RING = 3
V_COLS = 32
SLOT = HEAD_E + 1
QUAD = 4
QUADS = HEADS // QUAD
HALF = HEADS // 2


class LayerTwo:
    name, weights, keys, q_bias = "a2", "L2", 0, False
    scale = 1.0 / float(np.sqrt(HEAD_E))
    gate, sink, slopes = 2, 1.0, True


class LayerThree:
    name, weights, keys, q_bias = "a3", "L3", 1, True
    scale = float(D) ** -0.5
    gate, sink, slopes = 3, 0.0, False


def op_place(h):
    return h % 2 * PAIRS + h // 2


def max_place(h, t):
    return (h // HALF * HALF + h % 2 * (HALF // 2) + h % HALF // 2) * QT + t


class NarrowBuffers:

    def __init__(self, nc, ph):
        self.k_op = [ph.sb(f"k_op{i}", [P, PAIRS, S2], BF16) for i in range(RING)]
        self.q_op = [ph.sb(f"q_op{i}", [P, HEADS, S], BF16) for i in range(RING)]
        self.values = [ph.sb(f"values{i}", [P, KT, HEADS, V_COLS]) for i in range(RING)]
        self.wq, self.wv, self.wo = ([ph.sb(f"{n}{i}", [P, D]) for i in range(2)] for n in ("wq", "wv", "wo"))
        self.bq, self.bv, self.bo = ph.sb("bq", [P, 1]), ph.sb("bv", [P, 1]), ph.sb("bo", [1, D])
        self.pos_scr = nc.dram_tensor("pos_parts", [B, 3, S2], BF16).ap()

    def add_masks(self, ph):
        self.tri, self.triT = ph.sb("tri", [P, QT, S2], BF16), ph.sb("triT", [P, KT, S], BF16)
        self.padT, self.pad = ph.sb("padT", [P, B, KT]), ph.sb("pad", [P, B, S2], BF16)


class NarrowConstants:

    def __init__(self, ph, nb):
        self.nb = nb
        self.slopes, self.slopes_b = ph.sb("slopes", [9, HEADS, S]), ph.sb("slopes_b", [9, HEADS, S], BF16)
        self.zeros = ph.sb("zeros", [P, S], BF16)
        self.pos = ph.sb("pos", [B, S2], I32)
        self.posf, self.posr = ph.sb("posf", [B, S2]), ph.sb("posr", [B, S2])
        self.pos_parts = ph.sb("pos_parts", [B, 3, S2], BF16)
        self.const_in, self.zeroed, self.filled, self.ones_set = (ph.sem(n) for n in ("const_in", "zeroed", "filled", "ones_set"))
        self.slopes_cut, self.pos_cut, self.placed, self.weights_in = (ph.sem(n) for n in ("slopes_cut", "pos_cut", "placed", "weights_in"))

    def sync(self, sp, io):
        nb = self.nb
        sp.dma_start(self.pos[:], io["key_pos"]).then_inc(self.const_in, 16)
        sp.dma_start(self.slopes[:], io["c_slopes"]).then_inc(self.const_in, 16)
        for i, w in enumerate(("L2", "L3")):
            for tile, name in ((nb.wq, "_WqT"), (nb.wv, "_WvT"), (nb.wo, "_WoT")):
                sp.dma_start(tile[i][:], io[w + name]).then_inc(self.weights_in, 16)
        sp.dma_start(nb.bq[:], io["L3_bq"].unsqueeze(1)).then_inc(self.weights_in, 16)
        sp.dma_start(nb.bv[:], io["L3_bv"].unsqueeze(1)).then_inc(self.weights_in, 16)
        sp.dma_start(nb.bo[:], io["L3_bo"].unsqueeze(0)).then_inc(self.weights_in, 16)
        sp.wait_ge(self.pos_cut, 5)
        sp.dma_start(nb.pos_scr, self.pos_parts[:]).then_inc(self.placed, 16)
        sp.wait_ge(self.slopes_cut, 1)
        sp.wait_ge(self.zeroed, RING)
        for r in range(RING):
            sp.dma_start(nb.q_op[r][COMBO_ROWS:COMBO_ROWS + 9], self.slopes_b[:]).then_inc(self.placed, 16)
        sp.wait_ge(self.placed, 16 * (RING + 1))
        sp.wait_ge(self.weights_in, 16 * 9)

    def scalar_zeros(self, act):
        act.wait_ge(self.filled, 1)
        for r in range(RING):
            act.copy(self.nb.q_op[r][:], self.zeros[:].unsqueeze(1).to_broadcast([P, HEADS, S])).then_inc(self.zeroed, 1)

    def scalar(self, act):
        act.wait_ge(self.const_in, 32)
        act.copy(self.slopes_b[:], self.slopes[:]).then_inc(self.slopes_cut, 1)
        act.wait_ge(self.slopes_cut, 1)

    def vector(self, dve):
        p0, p1, p2 = (self.pos_parts[:, k, :] for k in range(3))
        cut = self.pos_cut
        dve.wait_ge(self.const_in, 32)
        dve.tensor_copy(self.posf[:], self.pos[:]).then_inc(cut, 1)
        dve.wait_ge(cut, 1)
        dve.tensor_copy(p0, self.posf[:]).then_inc(cut, 1)
        dve.wait_ge(cut, 2)
        dve.tensor_tensor(self.posr[:], self.posf[:], p0, ALU.subtract).then_inc(cut, 1)
        dve.wait_ge(cut, 3)
        dve.tensor_copy(p1, self.posr[:]).then_inc(cut, 1)
        dve.wait_ge(cut, 4)
        dve.tensor_tensor(p2, self.posr[:], p1, ALU.subtract).then_inc(cut, 1)

    def gpsimd(self, pool):
        nb = self.nb
        pool.memset(self.zeros[:], 0.0).then_inc(self.filled, 1)
        for r in range(RING):
            pool.memset(nb.values[r][:], 0.0).then_inc(self.filled, 1)
            pool.memset(nb.k_op[r][:], 1.0).then_inc(self.filled, 1)
        pool.wait_ge(self.filled, 2 * RING + 1)
        for r in range(RING):
            for s in range(2):
                heads = nb.values[r][:].rearrange("p k (g s j) m -> p (k g) s j m", g=2, s=2)[:, :, s, :, s * SLOT + HEAD_E]
                pool.memset(heads, 1.0).then_inc(self.ones_set, 1)
        pool.wait_ge(self.ones_set, 2 * RING)


class MaskConstants:

    def __init__(self, ph, nb, io):
        self.nb, self.io = nb, io
        self.tri_i, self.triT_i = ph.sb("tri_i", [P, QT, S2], U8), ph.sb("triT_i", [P, KT, S], U8)
        self.padT_i, self.pad_i = ph.sb("padT_i", [P, B, KT], U8), ph.sb("pad_i", [P, B, S2], U8)
        self.mask_in, self.mask_done = ph.sem("mask_in"), ph.sem("mask_done")

    def gpsimd(self, pool):
        nb, io = self.nb, self.io
        pool.dma_start(self.tri_i[:], io["tri"].rearrange("(t p) k -> p t k", p=P)).then_inc(self.mask_in, 16)
        pool.dma_start(self.triT_i[:], io["triT"].rearrange("(t p) q -> p t q", p=P)).then_inc(self.mask_in, 16)
        pool.dma_start(self.padT_i[:], io["padT"]).then_inc(self.mask_in, 16)
        pool.dma_start(self.pad_i[:].rearrange("p b k -> p (b k)"), io["pad"].partition_broadcast(P)).then_inc(self.mask_in, 16)
        for r in range(RING):
            pool.memset(nb.k_op[r][COMBO_ROWS:P], 1.0).then_inc(self.mask_done, 1)
        pool.wait_ge(self.mask_done, RING)
        pool.wait_ge(self.mask_in, 64)
        pool.tensor_scalar(nb.tri[:], self.tri_i[:], BIG, None, ALU.mult).then_inc(self.mask_done, 1)
        pool.tensor_scalar(nb.triT[:], self.triT_i[:], BIG, None, ALU.mult).then_inc(self.mask_done, 1)
        pool.tensor_copy(nb.padT[:], self.padT_i[:]).then_inc(self.mask_done, 1)
        pool.tensor_copy(nb.pad[:], self.pad_i[:]).then_inc(self.mask_done, 1)
        pool.wait_ge(self.mask_done, RING + 4)


def narrow_attention(nc, io, res, cfg):
    rows = COMBO_ROWS + (9 if cfg.slopes else 0)
    with Phase(nc, cfg.name) as ph:
        qs = nc.dram_tensor(cfg.name + "_qs", [B, 2, 3, HEAD_E, PAIRS, S], BF16).ap()
        ks = res.keys[cfg.keys]
        nb = res.narrow
        k_op, q_op, values, wq, wv, wo = nb.k_op, nb.q_op, nb.values, nb.wq[cfg.keys], nb.wv[cfg.keys], nb.wo[cfg.keys]
        bias_row, bqs = ph.sb("bias_row", [1, D]), ph.sb("bqs", [P, 1])
        y = [ph.sb(f"y{i}", [P, CHUNK]) for i in range(2)]
        y_rest = ph.sb("y_rest", [P, CHUNK])
        y_parts = [ph.sb(f"y_parts{i}", [P, 3, CHUNK], BF16) for i in range(NCHUNK)]
        cT = [ph.sb(f"cT{i}", [P, S2]) for i in range(RING)]
        madd = [ph.sb(f"madd{i}", [P, QT, S2], BF16) for i in range(RING)]
        maddT = [ph.sb(f"maddT{i}", [P, KT, S], BF16) for i in range(RING)]
        mx = [ph.sb(f"mx{i}", [P, HEADS * QT]) for i in range(RING)]
        max_rest = ph.sb("max_rest", [HALF * QT, P])
        max_parts = [ph.sb(f"max_parts{i}", [HALF * QT, 3, P], BF16) for i in range(2)]
        probs = [ph.sb(f"probs{i}", [P, KT, S]) for i in range(2 * QUAD)]
        OT = ph.sb("OT", [P, 2, S])
        den, rec = ph.sb("den", [P, 4, 4, 2]), ph.sb("rec", [P, 4, 4, 2])
        A = ph.sb("A", [P, QT, D])
        AT = ph.sb("AT", [P, S])
        junk = [ph.sb(f"junk{i}", [P, S2], BF16) for i in range(2)]
        carrier = [ph.sb(f"carrier{i}", [P, 1]) for i in range(2)]
        if cfg.slopes:
            mask_i = [ph.sb(f"mask{i}", [P, QT, S2], I32) for i in range(RING)]
            maskT_i = [ph.sb(f"maskT{i}", [P, KT, S], I32) for i in range(RING)]
        else:
            tri, triT, padT, pad = nb.tri, nb.triT, nb.padT, nb.pad
            padT_now = [ph.sb(f"padT_now{i}", [P, KT]) for i in range(RING)]

        psM = [ph.ps(f"psM{i}", [P, S2]) for i in range(2)]
        psE = [ph.ps(f"psE{i}", [P, KT, S]) for i in range(2)]
        psO = ph.ps("psO", [P, 2, S])
        psX = ph.ps("psX", [P, CHUNK])

        stats_done, aggr_done = ph.sem("stats_done"), ph.sem("aggr_done")
        n_loads, n_stores = 4 * len(RUNS) + 1 + 3 * cfg.slopes, 2 * 3 * 16
        biased, split, stored = ph.sem("biased"), ph.sem("split"), [ph.sem(f"stored{i}") for i in range(2)]
        query_made, bias_scaled, bias_made, row_done = (ph.sem(n) for n in ("query_made", "bias_scaled", "bias_made", "row_done"))
        mask_in = [ph.sem(f"mask_in{i}") for i in range(RING)]
        loaded = [ph.sem(f"loaded{i}") for i in range(RING)]
        masked = ph.sem("masked")
        max_scored, max_read = ph.sem("max_scored"), ph.sem("max_read")
        max_turned, max_split = ph.sem("max_turned"), ph.sem("max_split")
        max_in = [ph.sem(f"max_in{i}") for i in range(2)]
        v_made, v_out = ph.sem("v_made"), ph.sem("v_out")
        scored, exped, weighted = ph.sem("scored"), ph.sem("exped"), ph.sem("weighted")
        out_read, out_turned, den_done, rec_done, normed = (ph.sem(n) for n in ("out_read", "out_turned", "den_done", "rec_done", "normed"))
        back_turned, back_copied, projected, added = (ph.sem(n) for n in ("back_turned", "back_copied", "projected", "added"))
        pad_taken, pad_mixed = ph.sem("pad_taken"), ph.sem("pad_mixed")

        MAX_SLOTS, READ_SLOT, OUT_SLOT, BACK_SLOT, PROJECT_SLOT, V_SLOT = (10, 1), 3, 5, 7, 9, 12
        STATS_SLOT = PROJECT_SLOT - 1
        n_split = 4

        def steps(eng, step):
            step(0, 0, 0)
            step(1, 1, 0)
            with eng.Fori(0, (B - 2) // RING) as i:
                for k in range(RING):
                    step(RING * i + 2 + k, (2 + k) % RING, i + (2 + k) // RING, inner=True)
            step(B, B % RING, 0)

        with ph.block() as block:
            @block.sync
            def _(sp):
                def load_masks(u, r):
                    if cfg.slopes:
                        one = bass.ds(u, 1)
                        sp.dma_start(mask_i[r][:], io["mask"][one].rearrange("o (t p) k -> p (o t) k", p=P)).then_inc(mask_in[r], 16)
                        sp.dma_start(maskT_i[r][:], io["maskT"][one].rearrange("o (t p) q -> p (o t) q", p=P)).then_inc(mask_in[r], 16)

                def load_keys(u, r):
                    one = bass.ds(u, 1)
                    for j in range(2):
                        for first, end in RUNS:
                            rows_j = slice(j * HEAD_ROWS + first * HEAD_E, j * HEAD_ROWS + end * HEAD_E)
                            sp.dma_start(k_op[r][rows_j].rearrange("p t k -> p (t k)"),
                                         ks[one, j, 0:end - first].rearrange("o c e t k -> (o c e) (t k)")).then_inc(loaded[r], 16)
                    if cfg.slopes:
                        for a in range(3):
                            at = COMBO_ROWS + 3 * a
                            sp.dma_start(k_op[r][at:at + 3], nb.pos_scr[one].rearrange("o c k -> (o c) k").unsqueeze(1).to_broadcast([3, PAIRS, S2])).then_inc(loaded[r], 16)
                    sp.dma_start(cT[r][:], io["ctxT"][:, bass.ds(u * S2, S2)]).then_inc(loaded[r], 16)

                def load_queries(u, r):
                    one = bass.ds(u, 1)
                    for j in range(2):
                        for part, (first, end) in enumerate(RUNS):
                            rows_j = slice(j * HEAD_ROWS + first * HEAD_E, j * HEAD_ROWS + end * HEAD_E)
                            sp.dma_start(q_op[r][rows_j, j * PAIRS:(j + 1) * PAIRS, :].rearrange("p t q -> p (t q)"),
                                         qs[one, j, part].rearrange("o e t q -> o e (t q)").to_broadcast([end - first, HEAD_E, PAIRS * S])).then_inc(loaded[r], 16)

                def store_queries(n):
                    sp.wait_ge(split, 4 * n + 4)
                    for b in range(2):
                        for part in range(3):
                            sp.dma_start(qs[2 * n + b, :, part].rearrange("j e t q -> j (e t) q"),
                                         y_parts[n][:, part, b * S:(b + 1) * S]).then_inc(stored[min(n, 1)], 16)

                def maxima(v, r, half):
                    sp.wait_ge(max_split, (2 * v + half + 1) * n_split)
                    n = HALF // 2
                    for c in range(3):
                        for j in range(2):
                            heads = slice(j * PAIRS + half * n, j * PAIRS + (half + 1) * n)
                            sp.dma_start(q_op[r][rows + c:rows + c + 1, heads, :].rearrange("o h (t q) -> o (h t) q", q=P),
                                         max_parts[half][j * n * QT:(j + 1) * n * QT, c, :]).then_inc(max_in[half], 16)

                load_masks(0, 0)
                load_keys(0, 0)
                store_queries(0)
                sp.wait_ge(stored[0], n_stores)
                load_queries(0, 0)
                for n in range(1, NCHUNK):
                    store_queries(n)
                load_masks(1, 1)
                load_keys(1, 1)
                load_queries(1, 1)
                sp.wait_ge(stored[1], n_stores * (NCHUNK - 1))
                maxima(0, 0, 0)
                maxima(0, 0, 1)
                with sp.Fori(0, (B - 2) // RING) as i:
                    for k in range(RING):
                        v, r = RING * i + 2 + k, (2 + k) % RING
                        sp.wait_ge(exped, (v - 2) * HEADS + 1)
                        load_masks(v, r)
                        load_keys(v, r)
                        load_queries(v, r)
                        maxima(v - 1, (r - 1) % RING, 0)
                        maxima(v - 1, (r - 1) % RING, 1)
                maxima(B - 1, (B - 1) % RING, 0)
                maxima(B - 1, (B - 1) % RING, 1)

            @block.gpsimd
            def _(pool):
                def masks(u, r, turn, first):
                    if cfg.slopes:
                        pool.wait_ge(mask_in[r], 32 * (turn + 1))
                    if not first:
                        pool.wait_ge(exped, (u - RING + 1) * HEADS)
                    if cfg.slopes:
                        pool.tensor_scalar(madd[r][:], mask_i[r][:], 0.0, -BIG, ALU.is_equal, ALU.mult).then_inc(masked, 1)
                        pool.tensor_scalar(maddT[r][:], maskT_i[r][:], 0.0, -BIG, ALU.is_equal, ALU.mult).then_inc(masked, 1)
                    else:
                        pool.tensor_copy(padT_now[r][:], padT[:, bass.ds(u, 1), :].rearrange("p o k -> p (o k)")).then_inc(pad_taken, 1)
                        pool.tensor_tensor(madd[r][:], tri[:], pad[:, bass.ds(u, 1), :].to_broadcast([P, QT, S2]), ALU.mult).then_inc(pad_mixed, 1)
                        pool.wait_ge(pad_mixed, u + 1)
                        pool.tensor_scalar(madd[r][:], madd[r][:], BIG, None, ALU.subtract).then_inc(masked, 1)
                        pool.wait_ge(pad_taken, u + 1)
                        for t in range(KT):
                            last = pool.tensor_scalar(maddT[r][:, t, :], triT[:, t, :], padT_now[r][:, t:t + 1], BIG, ALU.mult, ALU.subtract)
                        last.then_inc(masked, 1)

                for u in range(RING):
                    masks(u, u, 0, True)
                with pool.Fori(1, 2) as i:
                    for r in range(RING):
                        masks(RING * i + r, r, i, False)
                for u in range(2 * RING, B):
                    masks(u, u % RING, u // RING, False)

            @block.tensor
            def _(pe):
                for n in range(NCHUNK):
                    if n >= 2:
                        pe.wait_ge(biased, n - 1)
                    pe.matmul(psM[n % 2][:], wq[:], res.xnT[:, n * CHUNK:(n + 1) * CHUNK], start=True, stop=True).then_inc(query_made, 1)
                if cfg.q_bias:
                    pe.matmul(psX[0:1, 0:D], nb.bv[:], wo[:], start=True, stop=True).then_inc(bias_made, 1)
                pe.wait_ge(biased, NCHUNK)

                def turn_out(u):
                    pe.wait_ge(out_read, u + 1)
                    for t in range(QT):
                        for g in range(2):
                            n = t * 2 + g
                            last = pe.transpose(psX[:, n * P:(n + 1) * P], OT[:, g, t * P:(t + 1) * P], res.ident[:])
                    last.then_inc(out_turned, 1)

                def turn_back(u):
                    pe.wait_ge(normed, 2 * u + 2)
                    for t in range(QT):
                        last = pe.transpose(psX[:, t * P:(t + 1) * P], A[:, t, :], res.ident[:])
                    last.then_inc(back_turned, 1)

                def project(u):
                    pe.wait_ge(back_copied, u + 1)
                    for t in range(QT):
                        y = psX[:, t * P:(t + 1) * P]
                        if cfg.q_bias:
                            if t == 0:
                                pe.wait_ge(row_done, 1)
                            pe.matmul(y, res.ones[0:1, :], bias_row[:], start=True, stop=False)
                        last = pe.matmul(y, AT[:, t * P:(t + 1) * P], wo[:], start=not cfg.q_bias, stop=True)
                    last.then_inc(projected, 1)

                def maximum(v, r, h, t, first):
                    n = QT * h + t
                    if not (first and n < 2):
                        pe.wait_ge(max_read, v * HEADS * QT + n - 1)
                    pe.matmul(psM[t][:], q_op[r][0:rows, op_place(h), t * P:(t + 1) * P], k_op[r][0:rows, h // 2, :],
                              start=True, stop=True).then_inc(max_scored, 1)

                def turn_maxima(v, r, half):
                    pe.wait_ge(max_read, (v * HEADS + (half + 1) * HALF) * QT)
                    pe.transpose(psX[0:HALF * QT, 0:P], mx[r][:, half * HALF * QT:(half + 1) * HALF * QT], res.ident[:]).then_inc(max_turned, 1)

                def score(w, r, h, ts, first):
                    if ts[0] == 0:
                        if h % HALF == 0:
                            pe.wait_ge(max_in[h // HALF], 96 * (w + 1))
                        if not (first and h < 2):
                            pe.wait_ge(exped, w * HEADS + h - 1)
                    for t in ts:
                        out = psE[h % 2][:, t, :]
                        pe.matmul(out, k_op[r][0:rows + 3, h // 2, t * P:(t + 1) * P], q_op[r][0:rows + 3, op_place(h), :], start=True, stop=False)
                        last = pe.matmul(out, res.identb[:], maddT[r][:, t, :], start=False, stop=True)
                    if ts[-1] == KT - 1:
                        last.then_inc(scored, 1)

                def weigh(w, r, quad, t, first):
                    if t == 0:
                        pe.wait_ge(exped, w * HEADS + (quad + 1) * QUAD)
                        if quad == 0 and not first:
                            pe.wait_ge(out_read, w)
                    g, s = quad // 2, quad % 2
                    for j in range(QUAD):
                        h = quad * QUAD + j
                        last = pe.matmul(psO[32 * j:32 * j + 32, g, :], values[r][:, t, h, :], probs[h % (2 * QUAD)][:, t, :],
                                         start=(s == 0 and t == 0), stop=(s == 1 and t == KT - 1),
                                         tile_position=(0, 32 * j), skip_group_check=True)
                    if t == KT - 1:
                        last.then_inc(weighted, 1)

                def step(v, r, turn, inner=False):
                    take_max, take_exp, finish = inner or v < B, inner or v >= 1, inner or v >= 2
                    before, first = (r - 1) % RING, not inner and v <= 1
                    if take_max:
                        pe.wait_ge(loaded[r], 16 * n_loads * (turn + 1))
                    if take_exp:
                        pe.wait_ge(masked, v * 2)
                        pe.wait_ge(v_out, 2 * v)
                    for s in range(HEADS):
                        if take_max:
                            maximum(v, r, s, 0, first and v == 0)
                        if take_exp:
                            score(v - 1, before, s, (0, 1), first)
                        if take_max:
                            maximum(v, r, s, 1, first and v == 0)
                        if take_exp:
                            score(v - 1, before, s, (2, 3), first)
                        quad, t = s // QUAD - 1, s % QUAD
                        if quad >= 0 and take_exp:
                            weigh(v - 1, before, quad, t, first)
                        if quad < 0 and finish:
                            weigh(v - 2, (r - 2) % RING, QUADS - 1, t, False)
                        if take_exp and s == MAX_SLOTS[1]:
                            turn_maxima(v - 1, before, 1)
                        if finish:
                            if s == OUT_SLOT:
                                pe.wait_ge(max_split, 2 * n_split * v)
                                turn_out(v - 2)
                            if s == BACK_SLOT:
                                turn_back(v - 2)
                            if s == PROJECT_SLOT:
                                project(v - 2)
                        if take_max:
                            if s == MAX_SLOTS[0]:
                                if finish:
                                    pe.wait_ge(added, v - 1)
                                elif v >= 1:
                                    pe.wait_ge(max_split, 2 * n_split * v)
                                turn_maxima(v, r, 0)
                            if s == V_SLOT:
                                pe.wait_ge(max_split, 2 * n_split * v + n_split)
                                for t in range(KT):
                                    last = pe.matmul(psX[:, t * P:(t + 1) * P], cT[r][:, t * P:(t + 1) * P], wv[:], start=True, stop=True)
                                last.then_inc(v_made, 1)

                steps(pe, step)
                for t in range(KT):
                    weigh(B - 1, (B - 1) % RING, QUADS - 1, t, False)
                pe.wait_ge(added, B - 1)
                turn_out(B - 1)
                turn_back(B - 1)
                project(B - 1)

            @block.scalar
            def _(act):
                if cfg.q_bias:
                    act.wait_ge(bias_scaled, 1)
                for n in range(NCHUNK):
                    act.wait_ge(query_made, n + 1)
                    if n >= 2:
                        act.wait_ge(split, 4 * (n - 1))
                    act.activation(y[n % 2][:], psM[n % 2][:], ACT.Identity, bias=bqs[:] if cfg.q_bias else 0.0, scale=cfg.scale).then_inc(biased, 1)

                def read_out(u):
                    act.wait_ge(weighted, (u + 1) * QUADS)
                    act.copy(OT[:], psO[:]).then_inc(out_read, 1)

                def copy_back(u):
                    act.wait_ge(back_turned, u + 1)
                    act.copy(AT[:], psX[:, 0:S]).then_inc(back_copied, 1)

                def copy_values(v, r):
                    act.wait_ge(v_made, v + 1)
                    for s in range(2):
                        act.copy(values[r][:].rearrange("p k (g s j) m -> p (k g) s j m", g=2, s=2)[:, :, s, :, s * SLOT:s * SLOT + HEAD_E],
                                 psX[:].rearrange("p (n s j c) -> p n s j c", s=2, j=4, c=HEAD_E)[:, :, s]).then_inc(v_out, 1)

                def step(v, r, turn, inner=False):
                    take_max, take_exp, finish = inner or v < B, inner or v >= 1, inner or v >= 2
                    for s in range(HEADS):
                        if take_exp:
                            n = (v - 1) * HEADS + s
                            act.wait_ge(scored, n + 1)
                            if not (not inner and v == 1 and s < 2 * QUAD):
                                act.wait_ge(weighted, (v - 1) * QUADS + s // QUAD - 1)
                            act.activation(probs[s % (2 * QUAD)][:], psE[s % 2][:], ACT.Exp).then_inc(exped, 1)
                        if finish:
                            if s == READ_SLOT:
                                read_out(v - 2)
                            if s == BACK_SLOT:
                                copy_back(v - 2)
                        if take_max and s == V_SLOT:
                            copy_values(v, r)

                steps(act, step)
                read_out(B - 1)
                copy_back(B - 1)

            @block.vector
            def _(dve):
                if cfg.q_bias:
                    dve.tensor_scalar(bqs[:], nb.bq[:], cfg.scale, None, ALU.mult).then_inc(bias_scaled, 1)
                for n in range(NCHUNK):
                    dve.wait_ge(biased, n + 1)
                    p0, p1, p2 = (y_parts[n][:, k, :] for k in range(3))
                    dve.tensor_copy(p0, y[n % 2][:]).then_inc(split, 1)
                    dve.wait_ge(split, 4 * n + 1)
                    dve.tensor_tensor(y_rest[:], y[n % 2][:], p0, ALU.subtract).then_inc(split, 1)
                    dve.wait_ge(split, 4 * n + 2)
                    dve.tensor_copy(p1, y_rest[:]).then_inc(split, 1)
                    dve.wait_ge(split, 4 * n + 3)
                    dve.tensor_tensor(p2, y_rest[:], p1, ALU.subtract).then_inc(split, 1)
                if cfg.q_bias:
                    dve.wait_ge(bias_made, 1)
                    dve.tensor_tensor(bias_row[:], psX[0:1, 0:D], nb.bo[:], ALU.add).then_inc(row_done, 1)

                def normalise(u):
                    dve.wait_ge(out_turned, u + 1)
                    turned = psX[:].rearrange("p (n j m) -> p n j m", n=4, j=4)
                    dve.tensor_scalar(den[:], turned[:, :, :, HEAD_E:2 * SLOT:SLOT], cfg.sink, None, ALU.add).then_inc(den_done, 1)
                    dve.wait_ge(den_done, u + 1)
                    dve.reciprocal(rec[:], den[:]).then_inc(rec_done, 1)
                    dve.wait_ge(rec_done, u + 1)
                    for s in range(2):
                        dve.tensor_tensor(A[:].rearrange("p t (g s j c) -> p (t g) s j c", g=2, s=2, j=4)[:, :, s],
                                          turned[:, :, :, s * SLOT:s * SLOT + HEAD_E],
                                          rec[:, :, :, s:s + 1].to_broadcast([P, 4, 4, HEAD_E]), ALU.mult).then_inc(normed, 1)

                def add(u):
                    dve.wait_ge(projected, u + 1)
                    x = res.X[:, bass.ds(u * QT, QT), :].rearrange("p t d -> p (t d)")
                    dve.scalar_tensor_tensor(x, psX[:, 0:S], res.gates[:, cfg.gate:cfg.gate + 1], x, ALU.mult, ALU.add).then_inc(added, 1)

                def maximum(v, r, h):
                    for t in range(QT):
                        n = QT * h + t
                        dve.wait_ge(max_scored, v * HEADS * QT + n + 1)
                        dve.memset(carrier[t][:], 0.0)
                        dve.tensor_tensor_reduce(junk[t][:], psM[t][:], madd[r][:, t, :], 1.0, -3.0e38, ALU.add, ALU.max,
                                                 mx[r][:, max_place(h, t):max_place(h, t) + 1]).then_inc(max_read, 1)

                def split_max(v, half):
                    done = (2 * v + half) * n_split
                    dve.wait_ge(max_turned, 2 * v + half + 1)
                    m, parts = psX[0:HALF * QT, 0:P], max_parts[half]
                    dve.tensor_scalar(parts[:, 0, :], m, -1.0, None, ALU.mult).then_inc(max_split, 1)
                    dve.wait_ge(max_split, done + 1)
                    dve.scalar_tensor_tensor(max_rest[:], m, -1.0, parts[:, 0, :], ALU.mult, ALU.subtract).then_inc(max_split, 1)
                    dve.wait_ge(max_split, done + 2)
                    dve.tensor_copy(parts[:, 1, :], max_rest[:]).then_inc(max_split, 1)
                    dve.wait_ge(max_split, done + 3)
                    dve.tensor_tensor(parts[:, 2, :], max_rest[:], parts[:, 1, :], ALU.subtract).then_inc(max_split, 1)

                def step(v, r, turn, inner=False):
                    take_max, take_exp, finish = inner or v < B, inner or v >= 1, inner or v >= 2
                    if take_max:
                        dve.wait_ge(masked, 2 * v + 1)
                    for s in range(HEADS):
                        if not inner and v == B and STATS_SLOT <= s < STATS_SLOT + B - 1:
                            u = s - STATS_SLOT
                            dve.wait_ge(added, u + 1)
                            tile_stats(dve, res, u * QT, QT, u * QT, stats_done, aggr_done)
                        if take_max:
                            maximum(v, r, s)
                        if take_exp and s == MAX_SLOTS[1]:
                            if inner or v >= 2:
                                dve.wait_ge(max_in[1], 96 * (v - 1))
                            split_max(v - 1, 1)
                        if finish:
                            if s == OUT_SLOT:
                                normalise(v - 2)
                            if s == PROJECT_SLOT:
                                add(v - 2)
                        if take_max and s == MAX_SLOTS[0]:
                            if inner or v >= 1:
                                dve.wait_ge(max_in[0], 96 * v)
                            split_max(v, 0)

                steps(dve, step)
                normalise(B - 1)
                add(B - 1)
                dve.wait_ge(added, B)
                tile_stats(dve, res, (B - 1) * QT, QT, (B - 1) * QT, stats_done, aggr_done)
                dve.wait_ge(aggr_done, NTILE)



WIDE_E = 64
WIDE_V = HEADS * WIDE_E
W_PAIRS = HEADS // 2
VC = WIDE_V // CHUNK


def layer1_attention(nc, io, res):
    halves = 2
    with Phase(nc, "a1") as ph:
        G, q_bias, wv, wo, bias_row = res.G, res.q_bias, res.wv1, res.wo1, res.bias_row1

        cT = [ph.sb(f"cT{i}", [P, S2]) for i in range(RING)]
        cTb = [ph.sb(f"cTb{i}", [P, S2], BF16) for i in range(RING)]
        q_op = [ph.sb(f"q_op{i}", [P, HEADS, S]) for i in range(RING)]
        q_b = [ph.sb(f"q_b{i}", [P, S], BF16) for i in range(4)]
        values = [ph.sb(f"values{i}", [P, KT, WIDE_V]) for i in range(RING)]
        max_row = [ph.sb(f"max_row{i}", [P, HEADS * S], BF16) for i in range(RING)]
        mx = [ph.sb(f"mx{i}", [P, HEADS * QT]) for i in range(RING)]
        max_b = [ph.sb(f"max_b{i}", [HALF * QT, P], BF16) for i in range(2)]
        probs = [ph.sb(f"probs{i}", [P, KT, S]) for i in range(4)]
        half_sum = [ph.sb(f"half_sum{i}", [P, 2, S]) for i in range(2)]
        key_sum = [ph.sb(f"key_sum{i}", [P, S]) for i in range(4)]
        rec = ph.sb("rec", [P, S])
        OT = ph.sb("OT", [P, W_PAIRS, S])

        psM = [ph.ps(f"psM{i}", [P, S2]) for i in range(2)]
        psE = [ph.ps(f"psE{i}", [P, 2, S]) for i in range(halves)]
        psO = ph.ps("psO", [P, 2, S])
        psQ = [ph.ps(f"psQ{i}", [P, CHUNK]) for i in range(2)]
        psY = ph.ps("psY", [P, CHUNK])

        loaded = [ph.sem(f"loaded{i}") for i in range(RING)]
        cast, zeroed, q_cast = ph.sem("cast"), ph.sem("zeroed"), ph.sem("q_cast")
        q_made, q_out = ph.sem("q_made"), ph.sem("q_out")
        max_scored, max_read = ph.sem("max_scored"), ph.sem("max_read")
        max_turned, max_cast = ph.sem("max_turned"), ph.sem("max_cast")
        max_in = [ph.sem(f"max_in{i}") for i in range(2)]
        v_made, v_out = ph.sem("v_made"), ph.sem("v_out")
        scored, exped, weighted = ph.sem("scored"), ph.sem("exped"), ph.sem("weighted")
        halved, summed = ph.sem("halved"), ph.sem("summed")
        inverted, normed = ph.sem("inverted"), ph.sem("normed")
        projected, added = ph.sem("projected"), ph.sem("added")
        stats_done, aggr_done = ph.sem("stats_done"), ph.sem("aggr_done")
        n_v = KT * VC

        MAX_SLOTS, OUT_SLOT, V_SLOT = (12, 1), 2, 3
        STATS_SLOT = OUT_SLOT + 1

        def steps(eng, step):
            step(0, 0, 0)
            step(1, 1, 0)
            with eng.Fori(0, (B - 2) // RING) as i:
                for k in range(RING):
                    step(RING * i + 2 + k, (2 + k) % RING, i + (2 + k) // RING, inner=True)
            step(B, B % RING, B // RING)

        with ph.block() as block:
            @block.sync
            def _(sp):
                def load(u, r):
                    sp.dma_start(cT[r][:], io["ctxT"][:, bass.ds(u * S2, S2)]).then_inc(loaded[r], 16)

                def maxima(v, r, half):
                    sp.wait_ge(max_cast, 2 * v + half + 1)
                    sp.dma_start(max_row[r][0:1, half * HALF * S:(half + 1) * HALF * S].rearrange("o (n q) -> o n q", q=P), max_b[half][:]).then_inc(max_in[half], 16)

                load(0, 0)
                load(1, 1)
                sp.wait_ge(zeroed, RING)
                maxima(0, 0, 0)
                maxima(0, 0, 1)
                with sp.Fori(0, (B - 2) // RING) as i:
                    for k in range(RING):
                        v, r = RING * i + 2 + k, (2 + k) % RING
                        sp.wait_ge(weighted, (v - 2) * W_PAIRS + 1)
                        load(v, r)
                        maxima(v - 1, (r - 1) % RING, 0)
                        maxima(v - 1, (r - 1) % RING, 1)
                maxima(B - 1, (B - 1) % RING, 0)
                maxima(B - 1, (B - 1) % RING, 1)

            @block.gpsimd
            def _(pool):
                for r in range(RING):
                    pool.memset(max_row[r][:], 0.0).then_inc(zeroed, 1)

                def heads(w, first):
                    for h in range(HEADS):
                        n = w * HEADS + h
                        pool.wait_ge(exped, (n + 1) * halves)
                        pool.tensor_tensor(half_sum[h % 2][:], probs[h % 4][:, 0:2, :], probs[h % 4][:, 2:4, :], ALU.add).then_inc(halved, 1)
                        if not (first and h < 4):
                            pool.wait_ge(weighted, w * W_PAIRS + (h - 4) // 2 + 1)
                        pool.wait_ge(halved, n + 1)
                        pool.tensor_tensor(key_sum[h % 4][:], half_sum[h % 2][:, 0, :], half_sum[h % 2][:, 1, :], ALU.add).then_inc(summed, 1)

                heads(0, True)
                with pool.Fori(1, B) as w:
                    heads(w, False)

            @block.tensor
            def _(pe):
                def query(v, r, h, first):
                    if not (first and h < 2):
                        pe.wait_ge(q_cast, v * HEADS + h - 1)
                    pe.matmul(psQ[h % 2][:, 0:S], G[:, h, :], res.xnT[:, bass.ds(v * S, S)], start=True, stop=True).then_inc(q_made, 1)

                def maximum(v, r, h, t, first):
                    n = QT * h + t
                    pe.wait_ge(q_cast, v * HEADS + h + 1)
                    if not (first and n < 2):
                        pe.wait_ge(max_read, v * HEADS * QT + n - 1)
                    pe.matmul(psM[t][:], q_b[h % 4][:, t * P:(t + 1) * P], cTb[r][:], start=True, stop=True).then_inc(max_scored, 1)

                def turn_maxima(v, r, half):
                    pe.wait_ge(max_read, (v * HEADS + (half + 1) * HALF) * QT)
                    pe.transpose(psY[0:HALF * QT, 0:P], mx[r][:, half * HALF * QT:(half + 1) * HALF * QT], res.ident[:]).then_inc(max_turned, 1)

                def score(w, r, h, half, first):
                    if h % HALF == 0 and half == 0:
                        pe.wait_ge(max_in[h // HALF], 16 * (w + 1))
                    if not (first and h == 0):
                        pe.wait_ge(exped, (w * HEADS + h - 1) * halves + half + 1)
                    for t in range(2):
                        k = (2 * half + t) * P
                        pe.matmul(psE[half][:, t, :], cT[r][:, k:k + P], q_op[r][:, h, :], start=(t == 0), stop=False, skip_group_check=True)
                    pe.matmul(psE[half][:], res.onesb[:], max_row[r][:, h * S:(h + 1) * S].unsqueeze(1).to_broadcast([P, 2, S]),
                              start=False, stop=True, skip_group_check=True).then_inc(scored, 1)

                def weigh(w, r, pair, first):
                    pe.wait_ge(exped, (w * HEADS + 2 * pair + 2) * halves)
                    if not first:
                        pe.wait_ge(normed, w * W_PAIRS + pair)
                    for t in range(KT):
                        for i in range(2):
                            h = 2 * pair + i
                            pe.matmul(psO[i * WIDE_E:(i + 1) * WIDE_E, 0, :], values[r][:, t, h * WIDE_E:(h + 1) * WIDE_E], probs[h % 4][:, t, :],
                                      start=(t == 0), stop=False, tile_position=(0, i * WIDE_E), skip_group_check=True)

                def total(w, pair):
                    pe.wait_ge(summed, w * HEADS + 2 * pair + 2)
                    for i in range(2):
                        last = pe.matmul(psO[i * WIDE_E:(i + 1) * WIDE_E, 1, :], res.ones[:, 0:WIDE_E], key_sum[(2 * pair + i) % 4][:],
                                         start=False, stop=True, tile_position=(0, i * WIDE_E), skip_group_check=True)
                    last.then_inc(weighted, 1)

                def project(u):
                    pe.wait_ge(normed, (u + 1) * W_PAIRS)
                    for t in range(QT):
                        y = psY[:, t * P:(t + 1) * P]
                        pe.matmul(y, res.ones[0:1, :], bias_row[:], start=True, stop=False)
                        for p in range(W_PAIRS):
                            last = pe.matmul(y, OT[:, p, t * P:(t + 1) * P], wo[:, p, :], start=False, stop=(p == W_PAIRS - 1))
                    last.then_inc(projected, 1)

                def value(v, r, n, wait):
                    if n > 0:
                        pe.wait_ge(v_out, v * n_v + n)
                    t, c = n // VC, n % VC
                    pe.matmul(psY[:], cT[r][:, t * P:(t + 1) * P], wv[:, c * CHUNK:(c + 1) * CHUNK], start=True, stop=True).then_inc(v_made, 1)

                def step(v, r, turn, inner=False):
                    take_max, take_exp, finish = inner or v < B, inner or v >= 1, inner or v >= 2
                    first, before = not inner and v <= 1, (r - 1) % RING
                    if take_max:
                        pe.wait_ge(loaded[r], 16 * (turn + 1))
                        query(v, r, 0, first and v == 0)
                        query(v, r, 1, first and v == 0)
                    if take_exp:
                        pe.wait_ge(q_out, v * HEADS)
                        pe.wait_ge(v_out, v * n_v)
                    for s in range(HEADS):
                        if take_exp and s == MAX_SLOTS[1]:
                            pe.wait_ge(max_cast, 2 * v - 1)
                            turn_maxima(v - 1, before, 1)
                        if finish and s == OUT_SLOT:
                            pe.wait_ge(max_cast, 2 * v)
                            project(v - 2)
                        if take_max:
                            if V_SLOT <= s < V_SLOT + n_v:
                                if s == V_SLOT:
                                    if finish:
                                        pe.wait_ge(added, v - 1)
                                    elif v >= 1:
                                        pe.wait_ge(max_cast, 2 * v)
                                value(v, r, s - V_SLOT, first and v == 0)
                            if s == MAX_SLOTS[0]:
                                pe.wait_ge(v_out, (v + 1) * n_v)
                                turn_maxima(v, r, 0)
                            if s + 2 < HEADS:
                                query(v, r, s + 2, first and v == 0)
                        for half in range(halves):
                            if take_max and s > 0:
                                maximum(v, r, s, half, first and v == 0)
                            if take_exp:
                                score(v - 1, before, s, half, first)
                        if take_max and s == 0:
                            pe.wait_ge(cast, v + 1)
                            for t in range(QT):
                                maximum(v, r, 0, t, first and v == 0)
                        if take_exp:
                            if s >= 2 and s % 2 == 0:
                                weigh(v - 1, before, s // 2 - 1, first and s == 2)
                            if s >= 3 and s % 2 == 1:
                                total(v - 1, (s - 3) // 2)
                        if finish and s == 0:
                            weigh(v - 2, (r - 2) % RING, W_PAIRS - 1, False)
                        if finish and s == 1:
                            total(v - 2, W_PAIRS - 1)

                steps(pe, step)
                weigh(B - 1, (B - 1) % RING, W_PAIRS - 1, False)
                total(B - 1, W_PAIRS - 1)
                project(B - 1)

            @block.scalar
            def _(act):
                def query(v, r, h, first):
                    act.wait_ge(q_made, v * HEADS + h + 1)
                    act.activation(q_op[r][:, h, :], psQ[h % 2][:, 0:S], ACT.Identity, bias=q_bias[:, h:h + 1]).then_inc(q_out, 1)
                    if not (first and h < 4):
                        act.wait_ge(max_scored, (v * HEADS + h - 3) * QT)
                    act.activation(q_b[h % 4][:], psQ[h % 2][:, 0:S], ACT.Identity, bias=q_bias[:, h:h + 1]).then_inc(q_cast, 1)

                def step(v, r, turn, inner=False):
                    take_max, take_exp = inner or v < B, inner or v >= 1
                    first = not inner and v == 0
                    if take_max:
                        query(v, r, 0, first)
                        query(v, r, 1, first)
                    for s in range(HEADS):
                        if take_max:
                            if V_SLOT <= s < V_SLOT + n_v:
                                n = s - V_SLOT
                                act.wait_ge(v_made, v * n_v + n + 1)
                                act.copy(values[r][:, n // VC, n % VC * CHUNK:(n % VC + 1) * CHUNK], psY[:]).then_inc(v_out, 1)
                            if s + 2 < HEADS:
                                query(v, r, s + 2, first)
                        if take_exp:
                            w = v - 1
                            if not (not inner and v == 1 and s < 4):
                                act.wait_ge(weighted, w * W_PAIRS + (s - 4) // 2 + 1)
                            for half in range(halves):
                                act.wait_ge(scored, (w * HEADS + s) * halves + half + 1)
                                act.activation(probs[s % 4][:, 2 * half:2 * half + 2, :], psE[half][:], ACT.Exp).then_inc(exped, 1)

                steps(act, step)

            @block.vector
            def _(dve):
                def normalise(w, pair):
                    dve.wait_ge(weighted, w * W_PAIRS + pair + 1)
                    dve.reciprocal(rec[:], psO[:, 1, :]).then_inc(inverted, 1)
                    dve.wait_ge(inverted, w * W_PAIRS + pair + 1)
                    dve.tensor_tensor(OT[:, pair, :], psO[:, 0, :], rec[:], ALU.mult).then_inc(normed, 1)

                def cast_maxima(v, half, again):
                    dve.wait_ge(max_turned, 2 * v + half + 1)
                    if again:
                        dve.wait_ge(max_in[half], 16 * v)
                    dve.tensor_scalar(max_b[half][:], psY[0:HALF * QT, 0:P], -1.0, None, ALU.mult).then_inc(max_cast, 1)

                def add(u):
                    dve.wait_ge(projected, u + 1)
                    x = res.X[:, bass.ds(u * QT, QT), :].rearrange("p t d -> p (t d)")
                    dve.scalar_tensor_tensor(x, psY[:, 0:S], res.gates[:, 1:2], x, ALU.mult, ALU.add).then_inc(added, 1)

                def step(v, r, turn, inner=False):
                    take_max, take_exp, finish = inner or v < B, inner or v >= 1, inner or v >= 2
                    first = not inner and v == 0
                    if take_max:
                        dve.wait_ge(loaded[r], 16 * (turn + 1))
                        dve.tensor_copy(cTb[r][:], cT[r][:]).then_inc(cast, 1)
                    for s in range(HEADS):
                        if not inner and v == B and STATS_SLOT <= s < STATS_SLOT + B - 1:
                            u = s - STATS_SLOT
                            dve.wait_ge(added, u + 1)
                            tile_stats(dve, res, u * QT, QT, u * QT, stats_done, aggr_done)
                        if finish and s == OUT_SLOT:
                            add(v - 2)
                        if take_max:
                            for t in range(QT):
                                n = QT * s + t
                                dve.wait_ge(max_scored, v * HEADS * QT + n + 1)
                                dve.tensor_reduce(mx[r][:, n:n + 1], psM[t][:], AX.X, ALU.max).then_inc(max_read, 1)
                            if s == MAX_SLOTS[0]:
                                cast_maxima(v, 0, not first)
                        if take_exp and s == MAX_SLOTS[1]:
                            cast_maxima(v - 1, 1, inner or v >= 2)
                        if take_exp and s >= 3 and s % 2 == 1:
                            normalise(v - 1, (s - 3) // 2)
                        if finish and s == 1:
                            normalise(v - 2, W_PAIRS - 1)

                steps(dve, step)
                normalise(B - 1, W_PAIRS - 1)
                add(B - 1)
                dve.wait_ge(added, B)
                tile_stats(dve, res, (B - 1) * QT, QT, (B - 1) * QT, stats_done, aggr_done)
                dve.wait_ge(aggr_done, NTILE)



ROUND = 1.5 * 2.0 ** 23
INT8_MAX = 127.0


def layer1_int8(nc, io, res):
    with Phase(nc, "q1") as ph:
        ahead = NarrowConstants(ph, res.narrow)
        wT = ph.sb("wT", [P, D])
        w_max, w_scale, w_inv = (ph.sb(n, [P, 1]) for n in ("w_max", "w_scale", "w_inv"))
        wr = ph.sb("wr", [P, D])
        wq = ph.sb("wq", [P, D], BF16)
        diag = ph.sb("diag", [P, P])
        col_scale = ph.sb("col_scale", [P, D])
        x_max, x_scale, x_inv, x_gate = (ph.sb(n, [P, NTILE]) for n in ("x_max", "x_scale", "x_inv", "x_gate"))
        xr = ph.sb("xr", [P, NTILE, D])
        tmp = [ph.sb(f"tmp{i}", [P, D]) for i in range(4)]
        xq = ph.sb("xq", [P, NTILE * P], BF16)
        psW = ph.ps("psW", [P, CHUNK])
        psT = [ph.ps(f"psT{i}", [P, CHUNK]) for i in range(2)]
        psY = [ph.ps(f"psY{i}", [P, 4, D]) for i in range(2)]
        w_in, step, w_turned, w_copied = (ph.sem(n) for n in ("w_in", "step", "w_turned", "w_copied"))
        x_step, w_rounded, stats_done, aggr_done = (ph.sem(n) for n in ("x_step", "w_rounded", "stats_done", "aggr_done"))
        rounded, turned, copied, made, scaled, added = (ph.sem(n) for n in ("rounded", "turned", "copied", "made", "scaled", "added"))
        with ph.block() as block:
            @block.sync
            def _(sp):
                sp.dma_start(wT[:], io["L1_rhsT"]).then_inc(w_in, 16)
                ahead.sync(sp, io)

            @block.gpsimd
            def _(pool):
                ahead.gpsimd(pool)

            @block.vector
            def _(dve):
                dve.tensor_reduce(x_max[:], res.xn[:], AX.X, ALU.max, apply_absolute_value=True).then_inc(step, 1)
                dve.wait_ge(w_in, 16)
                dve.tensor_reduce(w_max[:], wT[:], AX.X, ALU.max, apply_absolute_value=True).then_inc(step, 1)
                dve.wait_ge(step, 2)
                dve.tensor_scalar(w_scale[:], w_max[:], 1e-12, 1.0 / INT8_MAX, ALU.max, ALU.mult).then_inc(step, 1)
                dve.tensor_scalar(x_scale[:], x_max[:], 1e-12, 1.0 / INT8_MAX, ALU.max, ALU.mult).then_inc(step, 1)
                dve.wait_ge(step, 4)
                dve.reciprocal(w_inv[:], w_scale[:]).then_inc(step, 1)
                dve.reciprocal(x_inv[:], x_scale[:]).then_inc(step, 1)
                dve.tensor_scalar(diag[:], res.ident[:], w_scale[:], None, ALU.mult).then_inc(step, 1)
                dve.tensor_scalar(x_gate[:], x_scale[:], res.gates[:, 5:6], None, ALU.mult).then_inc(step, 1)
                dve.wait_ge(step, 8)
                dve.tensor_scalar(wr[:], wT[:], w_inv[:], ROUND, ALU.mult, ALU.add).then_inc(step, 1)
                dve.wait_ge(step, 9)
                dve.tensor_scalar(wr[:], wr[:], ROUND, INT8_MAX, ALU.subtract, ALU.min).then_inc(step, 1)
                dve.wait_ge(step, 10)
                dve.tensor_scalar(wr[:], wr[:], -INT8_MAX, None, ALU.max).then_inc(w_rounded, 1)
                for c in range(NCHUNK):
                    four = xr[:, 4 * c:4 * c + 4, :]
                    for t in range(4 * c, 4 * c + 4):
                        dve.tensor_scalar(xr[:, t, :], res.xn[:, t, :], x_inv[:, t:t + 1], ROUND, ALU.mult, ALU.add).then_inc(x_step, 1)
                    dve.wait_ge(x_step, 5 * c + 4)
                    dve.tensor_scalar(four, four, ROUND, INT8_MAX, ALU.subtract, ALU.min).then_inc(x_step, 1)
                    dve.wait_ge(x_step, 5 * c + 5)
                    dve.tensor_scalar(four, four, -INT8_MAX, None, ALU.max).then_inc(rounded, 1)
                    if c == 0:
                        dve.wait_ge(w_turned, 1)
                        dve.tensor_copy(wq[:], psW[:, 0:D]).then_inc(w_copied, 1)
                        dve.tensor_copy(col_scale[:], psW[:, D:2 * D]).then_inc(w_copied, 1)
                ahead.vector(dve)
                dve.wait_ge(w_copied, 2)
                for c in range(NCHUNK):
                    dve.wait_ge(made, c + 1)
                    for k in range(4):
                        t = 4 * c + k
                        dve.scalar_tensor_tensor(tmp[t % 4][:], psY[c % 2][:, k, :], x_gate[:, t:t + 1], col_scale[:],
                                                 ALU.mult, ALU.mult).then_inc(scaled, 1)
                    for k in range(4):
                        t = 4 * c + k
                        dve.wait_ge(scaled, t + 1)
                        dve.tensor_tensor(res.X[:, t, :], res.X[:, t, :], tmp[t % 4][:], ALU.add).then_inc(added, 1)
                    dve.wait_ge(added, 4 * c + 4)
                    tile_stats(dve, res, 4 * c, 4, 4 * c, stats_done, aggr_done)
                dve.wait_ge(aggr_done, NTILE)

            @block.tensor
            def _(pe):
                pe.wait_ge(w_rounded, 1)
                pe.transpose(psW[:, 0:D], wr[:], res.ident[:])
                pe.matmul(psW[:, D:2 * D], res.ones[:], diag[:], start=True, stop=True).then_inc(w_turned, 1)

                def turn(c):
                    pe.wait_ge(rounded, c + 1)
                    if c >= 2:
                        pe.wait_ge(copied, c - 1)
                    for k in range(4):
                        last = pe.transpose(psT[c % 2][:, k * P:(k + 1) * P], xr[:, 4 * c + k, :], res.ident[:])
                    last.then_inc(turned, 1)

                turn(0)
                pe.wait_ge(w_copied, 2)
                for c in range(NCHUNK):
                    if c + 1 < NCHUNK:
                        turn(c + 1)
                    pe.wait_ge(copied, c + 1)
                    if c >= 2:
                        pe.wait_ge(scaled, 4 * (c - 1))
                    for k in range(4):
                        t = 4 * c + k
                        last = pe.matmul(psY[c % 2][:, k, :], xq[:, t * P:(t + 1) * P], wq[:], start=True, stop=True)
                    last.then_inc(made, 1)

            @block.scalar
            def _(act):
                ahead.scalar_zeros(act)
                for c in range(NCHUNK):
                    act.wait_ge(turned, c + 1)
                    act.copy(xq[:, c * CHUNK:(c + 1) * CHUNK], psT[c % 2][:]).then_inc(copied, 1)
                ahead.scalar(act)


def layer3_ternary(nc, io, res):
    with Phase(nc, "q3") as ph:
        w = ph.sb("w", [P, D])
        w_abs, w_mean, w_low, x_abs, x_scale, x_inv, out_scale = (
            ph.sb(n, [P, 1]) for n in ("w_abs", "w_mean", "w_low", "x_abs", "x_scale", "x_inv", "out_scale"))
        w_half = ph.sb("w_half", [P, 1])
        over, under = ph.sb("over", [P, D]), ph.sb("under", [P, D])
        wq = ph.sb("wq", [P, D], BF16)
        bias = ph.sb("bias", [P, D])
        x_top = ph.sb("x_top", [1, 1])
        xr = ph.sb("xr", [P, NTILE, D])
        tmp = [ph.sb(f"tmp{i}", [P, D]) for i in range(2)]
        xq = ph.sb("xq", [P, NTILE * P], BF16)
        psS = ph.ps("psS", [P, CHUNK])
        psT = [ph.ps(f"psT{i}", [P, CHUNK]) for i in range(2)]
        psY = [ph.ps(f"psY{i}", [P, 4, D]) for i in range(2)]
        w_in, step, x_reduced, x_turned, x_topped, w_reduced, w_summed = (
            ph.sem(n) for n in ("w_in", "step", "x_reduced", "x_turned", "x_topped", "w_reduced", "w_summed"))
        rounded, ternary, turned, copied, made, scaled, added = (
            ph.sem(n) for n in ("rounded", "ternary", "turned", "copied", "made", "scaled", "added"))
        with ph.block() as block:
            @block.sync
            def _(sp):
                sp.dma_start(w[:], io["L3_wT"]).then_inc(w_in, 16)
                sp.dma_start(bias[:], io["L3_bias"].partition_broadcast(P)).then_inc(w_in, 16)

            @block.vector
            def _(dve):
                dve.tensor_reduce(x_abs[:], res.xn[:], AX.XY, ALU.max, apply_absolute_value=True).then_inc(x_reduced, 1)
                dve.wait_ge(w_in, 32)
                dve.tensor_reduce(w_abs[:], w[:], AX.X, ALU.add, apply_absolute_value=True).then_inc(w_reduced, 1)
                dve.wait_ge(x_turned, 1)
                dve.tensor_reduce(x_top[:], psS[0:1, 0:P], AX.X, ALU.max).then_inc(x_topped, 1)
                dve.wait_ge(w_summed, 1)
                dve.tensor_scalar(w_mean[:], psS[:, P:P + 1], 1.0 / (D * D), None, ALU.mult).then_inc(step, 1)
                dve.tensor_scalar(w_half[:], psS[:, P:P + 1], 0.5 / (D * D), None, ALU.mult).then_inc(step, 1)
                dve.tensor_scalar(w_low[:], psS[:, P:P + 1], -0.5 / (D * D), None, ALU.mult).then_inc(step, 1)
                dve.tensor_scalar(x_scale[:], psS[:, P + 1:P + 2], 1.0 / INT8_MAX, None, ALU.mult).then_inc(step, 1)
                dve.wait_ge(step, 4)
                dve.reciprocal(x_inv[:], x_scale[:]).then_inc(step, 1)
                dve.tensor_scalar(over[:], w[:], w_half[:], None, ALU.is_gt).then_inc(step, 1)
                dve.tensor_scalar(under[:], w[:], w_low[:], None, ALU.is_lt).then_inc(step, 1)
                dve.scalar_tensor_tensor(out_scale[:], w_mean[:], res.gates[:, 7:8], x_scale[:], ALU.mult, ALU.mult).then_inc(step, 1)
                dve.wait_ge(step, 8)
                dve.tensor_tensor(wq[:], over[:], under[:], ALU.subtract).then_inc(ternary, 1)
                dve.tensor_scalar(bias[:], bias[:], res.gates[:, 7:8], None, ALU.mult).then_inc(step, 1)
                dve.tensor_scalar(xr[:], res.xn[:], x_inv[:], ROUND, ALU.mult, ALU.add).then_inc(step, 1)
                dve.wait_ge(step, 10)
                dve.tensor_scalar(xr[:], xr[:], ROUND, INT8_MAX, ALU.subtract, ALU.min).then_inc(step, 1)
                dve.wait_ge(step, 11)
                dve.tensor_scalar(xr[:], xr[:], -INT8_MAX - 1.0, None, ALU.max).then_inc(rounded, 1)
                for c in range(NCHUNK):
                    dve.wait_ge(made, c + 1)
                    for k in range(4):
                        t = 4 * c + k
                        dve.scalar_tensor_tensor(tmp[k % 2][:], psY[c % 2][:, k, :], out_scale[:], bias[:],
                                                 ALU.mult, ALU.add).then_inc(scaled, 1)
                        dve.wait_ge(scaled, t + 1)
                        dve.tensor_tensor(res.X[:, t, :], res.X[:, t, :], tmp[k % 2][:], ALU.add).then_inc(added, 1)
                dve.wait_ge(added, NTILE)

            @block.tensor
            def _(pe):
                pe.wait_ge(x_reduced, 1)
                pe.transpose(psS[0:1, 0:P], x_abs[:], res.ident[:]).then_inc(x_turned, 1)
                pe.wait_ge(w_reduced, 1)
                pe.wait_ge(x_topped, 1)
                pe.matmul(psS[:, P:P + 1], res.ones[:], w_abs[:], start=True, stop=True)
                pe.matmul(psS[:, P + 1:P + 2], res.ones[0:1, :], x_top[:], start=True, stop=True).then_inc(w_summed, 1)
                pe.wait_ge(rounded, 1)
                for c in range(NCHUNK):
                    if c >= 2:
                        pe.wait_ge(copied, c - 1)
                    for k in range(4):
                        last = pe.transpose(psT[c % 2][:, k * P:(k + 1) * P], xr[:, 4 * c + k, :], res.ident[:])
                    last.then_inc(turned, 1)
                pe.wait_ge(ternary, 1)
                for c in range(NCHUNK):
                    pe.wait_ge(copied, c + 1)
                    if c >= 2:
                        pe.wait_ge(scaled, 4 * (c - 1))
                    for k in range(4):
                        t = 4 * c + k
                        last = pe.matmul(psY[c % 2][:, k, :], xq[:, t * P:(t + 1) * P], wq[:], start=True, stop=True)
                    last.then_inc(made, 1)

            @block.scalar
            def _(act):
                for c in range(NCHUNK):
                    act.wait_ge(turned, c + 1)
                    act.copy(xq[:, c * CHUNK:(c + 1) * CHUNK], psT[c % 2][:]).then_inc(copied, 1)


def more_layouts(a, io):
    io["c_iota"] = np.arange(16, dtype=np.float32)
    io["c_tri"] = np.triu(np.ones((P, P), np.float32))
    io["c_lane"] = np.arange(P, dtype=np.float32)
    io["c_place"] = np.arange(L0_CAPACITY, dtype=np.float32)
    io["L0_Wg"] = a["L0_ffn_Wg"]
    io["L0_W1"], io["L0_W2"], io["L0_b2"] = a["L0_ffn_W1"], a["L0_ffn_W2"], a["L0_ffn_b2"]
    io["L0_b1"] = a["L0_ffn_b1"].reshape(8, 4, P).transpose(0, 2, 1)
    shared = lambda s, e: np.concatenate([a["L2_ffn_" + s][None], a["L2_ffn_" + e]])
    io["L2_router_W"], io["L2_router_b"] = a["L2_ffn_router_W"], a["L2_ffn_router_b"]
    io["L2_W1"], io["L2_W2"], io["L2_b2"] = shared("sW1", "eW1"), shared("sW2", "eW2"), shared("sb2", "eb2")
    io["L2_b1"] = shared("sb1", "eb1").reshape(16, 1, P).transpose(0, 2, 1)
    io["L1_rhsT"] = a["L1_ffn_rhs"].T
    io["L3_wT"], io["L3_bias"] = a["L3_ffn_weight"].T, a["L3_ffn_bias"]

    io["key_pos"] = a["itok_BxS2_1_8191"]
    io["mask"] = a["mask_BxSxS2_if1"]
    io["maskT"] = a["mask_BxSxS2_if1"].transpose(0, 2, 1)
    io["tri"] = a["mask_SxS2_bk0"]
    io["triT"] = np.ascontiguousarray(a["mask_SxS2_bk0"].T)
    io["pad"] = a["mask_BxS2_bk1"].reshape(B * S2)
    io["padT"] = np.ascontiguousarray(a["mask_BxS2_bk1"].reshape(B, KT, P).transpose(2, 0, 1))
    ratio = 2.0 ** (-8.0 / HEADS)
    rest = np.array([ratio ** i for i in range(1, HEADS + 1)], np.float32)
    io["c_slopes"] = np.zeros((9, HEADS, S), np.float32)
    for part in range(3):
        top = (rest.view(np.uint32) & np.uint32(0xFFFF0000)).view(np.float32)
        io["c_slopes"][3 * part:3 * part + 3] = top[None, :, None]
        rest = rest - top
    io["c_slopes"] = io["c_slopes"].reshape(9, PAIRS, 2, S).transpose(0, 2, 1, 3).reshape(9, HEADS, S)

    io["L1_wq"] = a["L1_xattn_w_query"].transpose(1, 2, 0)
    io["L1_wk"] = a["L1_xattn_w_key"].transpose(1, 2, 0)
    io["L1_wv"] = a["L1_xattn_w_value"].reshape(D, WIDE_V)
    io["L1_wo"] = a["L1_xattn_w_projection"].transpose(0, 2, 1).reshape(WIDE_V, D)
    io["L1_bq"] = a["L1_xattn_b_query"].reshape(HEADS, WIDE_E).T
    io["L1_bv"] = a["L1_xattn_b_value"].reshape(W_PAIRS, P).T
    io["L1_bp"] = a["L1_xattn_b_projection"]



def build(nc, io):
    res = Resident()
    with Phase(nc, "res") as ph:
        res.X = ph.sb("X", [P, NTILE, D])
        res.xn = ph.sb("xn", [P, NTILE, D])
        res.xnT = ph.sb("xnT", [P, NTILE * P])
        res.stats, res.mv = ph.sb("stats", [P, NTILE, 6]), ph.sb("mv", [P, NTILE, 2])
        res.gates = ph.sb("gates", [P, 8])
        res.ident = ph.sb("ident", [P, P])
        res.identb = ph.sb("identb", [P, P], BF16)
        res.ones = ph.sb("ones", [P, P])
        res.onesb = ph.sb("onesb", [P, P], BF16)
        with Phase(nc, "ahead") as pa:
            res.G = pa.sb("G", [P, HEADS, D])
            res.q_bias = pa.sb("q_bias", [P, HEADS])
            res.wv1 = pa.sb("wv1", [P, WIDE_V])
            res.wo1 = pa.sb("wo1", [P, W_PAIRS, D])
            res.bias_row1 = pa.sb("bias_row1", [1, D])
            res.keys = [nc.dram_tensor(f"keys{i}", [B, 2, 3, HEAD_E, PAIRS, S2], BF16).ap() for i in (2, 3)]
            with Phase(nc, "l0") as pl:
                res.ctxT = pl.sb("ctxT", [P, NTILE, P, 2])
                res.w_qkv, res.b_qkv = pl.sb("w_qkv", [P, 3 * D]), pl.sb("b_qkv", [P, 3 * D])
                load_phase(nc, io, res)
                norm_phase(nc, io, res, "n0")
                layer0_attention(nc, io, res)
            norm_phase(nc, io, res, "n1")
            layer0_experts(nc, io, res)
            norm_phase(nc, io, res, "n2")
            layer1_attention(nc, io, res)
        Phase.clear_used(nc)
        with Phase(nc, "narrow") as pn:
            res.narrow = NarrowBuffers(nc, pn)
            norm_phase(nc, io, res, "n3", transposed=False)
            layer1_int8(nc, io, res)
            norm_phase(nc, io, res, "n4")
            narrow_attention(nc, io, res, LayerTwo)
            Phase.clear_used(nc)
            with Phase(nc, "masks") as pm:
                res.narrow.add_masks(pm)
                norm_phase(nc, io, res, "n5")
                layer2_experts(nc, io, res)
                norm_phase(nc, io, res, "n6")
                narrow_attention(nc, io, res, LayerThree)
        Phase.clear_used(nc)
        norm_phase(nc, io, res, "n7", transposed=False)
        layer3_ternary(nc, io, res)
        store_phase(nc, io, res)



def layouts(inputs):
    a = {k: np.asarray(v) for k, v in inputs.items()}
    tr = lambda w: np.ascontiguousarray(w.T)
    io = {
        "x": a["x"].reshape(B * S, D),
        "ctxT": np.ascontiguousarray(a["ctx_1024"].reshape(B * S2, D).T),
        "g_xattn": a["g_xattn"], "g_ffn": a["g_ffn"],
        "c_ident": np.eye(P, dtype=np.float32),
    }
    for w in ("Wq", "Wk", "Wv", "Wo"):
        io[f"L0_{w}T"] = tr(a[f"L0_xattn_{w}"])
        io[f"L3_{w}T"] = tr(a[f"L3_xattn_{w}"])
    for b in ("bq", "bk", "bv", "bo"):
        io[f"L0_{b}"] = a[f"L0_xattn_{b}"]
        io[f"L3_{b}"] = a[f"L3_xattn_{b}"]
    for w in ("q", "k", "v", "o"):
        io[f"L2_W{w}T"] = tr(a[f"L2_xattn_W_{w}"])
    for name in ("L2_WqT", "L2_WkT", "L3_WqT", "L3_WkT"):
        io[name] = io[name].reshape(D, PAIRS, 2, HEAD_E).transpose(0, 2, 3, 1).reshape(D, D)
    for name in ("L3_bq", "L3_bk"):
        io[name] = io[name].reshape(PAIRS, 2, HEAD_E).transpose(1, 2, 0).reshape(D)
    more_layouts(a, io)
    return {k: np.ascontiguousarray(v) for k, v in io.items()}


def kernel(**inputs):
    import concourse.bacc as bacc
    from concourse.bass_utils import run_bass_kernel_spmd

    nc = bacc.Bacc("TRN2", target_bir_lowering=False, num_devices=1)
    arrays = layouts(inputs)
    io = {n: nc.dram_tensor(f"in_{n}", v.shape, mybir.dt.from_np(v.dtype), kind="ExternalInput").ap() for n, v in arrays.items()}
    io["out"] = nc.dram_tensor("out_0", (B * S, D), F32, kind="ExternalOutput").ap()
    build(nc, io)
    got = run_bass_kernel_spmd(nc, [{f"in_{n}": v for n, v in arrays.items()}], core_ids=[0])
    return got.results[0]["out_0"].reshape(B, S, D)
```
